# Optimizing a Trainium2 kernel written in Bass

```python
import numpy as np
import jax
import jax.numpy as jnp

def _softmax(x, axis=-1):
    return jax.nn.softmax(x, axis=axis)

def _gelu(x):
    return jax.nn.gelu(x, approximate=True)

def _silu(x):
    return jax.nn.silu(x)

def _sigmoid(x):
    return jax.nn.sigmoid(x)

def _layernorm(x, axis=-1, eps=1e-05):
    m = jnp.mean(x, axis=axis, keepdims=True)
    v = jnp.var(x, axis=axis, keepdims=True)
    return (x - m) / jnp.sqrt(v + eps)

def _scatter_add(tgt, idx, src, axis=0):
    return tgt.at[idx].add(src)

def _segment_sum(src, seg, n):
    return jax.ops.segment_sum(src, seg, n)
kernel_name = 'mk_vit_tower_d1_tok_img256_r4_4801e3'

def setup_inputs(seed: int=0):
    np.random.seed(seed)
    _w = jnp.asarray

    def _rec_inputs():
        import jax
        import jax.numpy as jnp
        _rk = jax.random.key(seed)
        x = 9.04603e-05 + 1.00016 * jax.random.normal(jax.random.fold_in(_rk, 1), (4, 1, 224, 224), jnp.float32)
        return x
    x = _rec_inputs()

    def _L0_tok_setup():
        import jax, jax.numpy as jnp
        import numpy as np
        WS = 7
        H = W = 56
        C = 64
        NH = 8
        HD = C // NH
        SCALE = HD ** (-0.5)
        SHIFT = WS // 2
        N = WS * WS

        def _rel_pos_index():
            coords = np.stack(np.meshgrid(np.arange(WS), np.arange(WS), indexing='ij'))
            cf = coords.reshape(2, -1)
            rel = (cf[:, :, None] - cf[:, None, :]).transpose(1, 2, 0).copy()
            rel[..., 0] += WS - 1
            rel[..., 1] += WS - 1
            rel[..., 0] *= 2 * WS - 1
            return jnp.array(rel.sum(-1))

        def _attn_mask():
            img = np.zeros((H, W), np.int32)
            cnt = 0
            for h in (slice(0, -WS), slice(-WS, -SHIFT), slice(-SHIFT, None)):
                for w in (slice(0, -WS), slice(-WS, -SHIFT), slice(-SHIFT, None)):
                    cnt += 1
                    img[h, w] = cnt
            mw = img.reshape(H // WS, WS, W // WS, WS).transpose(0, 2, 1, 3).reshape(-1, N)
            diff = mw[:, None, :] - mw[:, :, None]
            return jnp.array(np.where(diff != 0, -100.0, 0.0).astype(np.float32))

        def _layernorm(x, g, b):
            m = x.mean(-1, keepdims=True)
            v = ((x - m) ** 2).mean(-1, keepdims=True)
            return (x - m) * jax.lax.rsqrt(v + 1e-05) * g + b

        def _window_partition(x):
            B = x.shape[0]
            x = x.reshape(B, H // WS, WS, W // WS, WS, C).transpose(0, 1, 3, 2, 4, 5)
            return x.reshape(-1, N, C)

        def _window_reverse(xw, B):
            x = xw.reshape(B, H // WS, W // WS, WS, WS, C).transpose(0, 1, 3, 2, 4, 5)
            return x.reshape(B, H, W, C)

        def _swin_block(x, p, shift, rpi, amask):
            B = x.shape[0]
            shortcut = x
            h = _layernorm(x, p['n1g'], p['n1b']).reshape(B, H, W, C)
            if shift > 0:
                h = jnp.roll(h, (-shift, -shift), axis=(1, 2))
            xw = _window_partition(h)
            B_ = xw.shape[0]
            qkv = (xw @ p['qkv_w'].T + p['qkv_b']).reshape(B_, N, 3, NH, HD).transpose(2, 0, 3, 1, 4)
            q, k, v = (qkv[0], qkv[1], qkv[2])
            attn = jnp.einsum('bhnd,bhmd->bhnm', q * SCALE, k)
            attn = attn + p['rpb'][rpi].transpose(2, 0, 1)[None]
            if shift > 0:
                nW = amask.shape[0]
                attn = attn.reshape(B_ // nW, nW, NH, N, N) + amask[None, :, None]
                attn = attn.reshape(B_, NH, N, N)
            attn = jax.nn.softmax(attn, axis=-1)
            o = jnp.einsum('bhnm,bhmd->bhnd', attn, v).transpose(0, 2, 1, 3).reshape(B_, N, C)
            o = o @ p['proj_w'].T + p['proj_b']
            h = _window_reverse(o, B)
            if shift > 0:
                h = jnp.roll(h, (shift, shift), axis=(1, 2))
            x = shortcut + h.reshape(B, H * W, C)
            y = _layernorm(x, p['n2g'], p['n2b'])
            y = jax.nn.gelu(y @ p['w1'].T + p['b1'], approximate=False)
            return x + y @ p['w2'].T + p['b2']
        key = jax.random.key(seed)
        ks = jax.random.split(key, 8)
        s = 0.02
        return {'x': jax.random.normal(ks[0], (16, 1, 224, 224), jnp.float32), 'pe_w': jax.random.normal(ks[1], (C, 1, 4, 4), jnp.float32) * s, 'pe_b': jnp.zeros((C,), jnp.float32), 'pe_ng': jnp.ones((C,), jnp.float32), 'pe_nb': jnp.zeros((C,), jnp.float32), 'n1g': jnp.ones((2, C), jnp.float32), 'n1b': jnp.zeros((2, C), jnp.float32), 'qkv_w': jax.random.normal(ks[2], (2, 3 * C, C), jnp.float32) * s, 'qkv_b': jnp.zeros((2, 3 * C), jnp.float32), 'rpb': jax.random.normal(ks[3], (2, (2 * WS - 1) ** 2, NH), jnp.float32) * s, 'proj_w': jax.random.normal(ks[4], (2, C, C), jnp.float32) * s, 'proj_b': jnp.zeros((2, C), jnp.float32), 'n2g': jnp.ones((2, C), jnp.float32), 'n2b': jnp.zeros((2, C), jnp.float32), 'w1': jax.random.normal(ks[5], (2, 4 * C, C), jnp.float32) * s, 'b1': jnp.zeros((2, 4 * C), jnp.float32), 'w2': jax.random.normal(ks[6], (2, C, 4 * C), jnp.float32) * s, 'b2': jnp.zeros((2, C), jnp.float32)}
    _L0_tok_all = _L0_tok_setup()
    _L0_tok_in = {k: v for k, v in _L0_tok_all.items() if k in ('pe_w', 'pe_b', 'pe_ng', 'pe_nb', 'n1g', 'n1b', 'qkv_w', 'qkv_b', 'rpb', 'proj_w', 'proj_b', 'n2g', 'n2b', 'w1', 'b1', 'w2', 'b2')}
    del _L0_tok_all

    def _L0_attn_setup():
        import jax, jax.numpy as jnp
        import numpy as np
        SEQ_LEN = 512
        EMBED_DIM = 64
        BATCH = 8
        LN_EPS = 1e-05

        def _layernorm(x, g, b):
            mu = jnp.mean(x, axis=-1, keepdims=True)
            var = jnp.mean(jnp.square(x - mu), axis=-1, keepdims=True)
            return (x - mu) * jax.lax.rsqrt(var + LN_EPS) * g + b
        key = jax.random.key(seed)
        ks = jax.random.split(key, 8)
        C = EMBED_DIM
        x = jax.random.normal(ks[0], (BATCH, SEQ_LEN, C), dtype=jnp.float32)
        qkv_w = jax.random.normal(ks[1], (C, 3 * C), dtype=jnp.float32) * 0.02
        qkv_b = jnp.zeros((3 * C,), dtype=jnp.float32)
        proj_w = jax.random.normal(ks[2], (C, C), dtype=jnp.float32) * 0.02
        proj_b = jnp.zeros((C,), dtype=jnp.float32)
        ln1_g = jnp.ones((C,), dtype=jnp.float32)
        ln1_b = jnp.zeros((C,), dtype=jnp.float32)
        ln2_g = jnp.ones((C,), dtype=jnp.float32)
        ln2_b = jnp.zeros((C,), dtype=jnp.float32)
        bias_table = jax.random.truncated_normal(ks[3], -2.0, 2.0, (2 * SEQ_LEN - 1,), dtype=jnp.float32) * 0.02
        scale = jnp.asarray(1.0 / np.sqrt(C), dtype=jnp.float32)
        return {'x': x, 'ln1_g': ln1_g, 'ln1_b': ln1_b, 'qkv_w': qkv_w, 'qkv_b': qkv_b, 'bias_table': bias_table, 'scale': scale, 'proj_w': proj_w, 'proj_b': proj_b, 'ln2_g': ln2_g, 'ln2_b': ln2_b}
    _L0_attn_all = _L0_attn_setup()
    _L0_attn_in = {k: v for k, v in _L0_attn_all.items() if k in ('ln1_g', 'ln1_b', 'qkv_w', 'qkv_b', 'bias_table', 'scale', 'proj_w', 'proj_b', 'ln2_g', 'ln2_b')}
    del _L0_attn_all

    def _L0_ffn_setup():
        import jax, jax.numpy as jnp
        import numpy as np
        E = 8
        K = 2
        D = 64
        H = 128
        DOUT = 64
        EPS = 1e-05
        key = jax.random.key(seed)
        ks = jax.random.split(key, 9)
        s = 0.02
        return {'x': jax.random.normal(ks[0], (4, 2048, D), jnp.float32), 'gamma': 1.0 + 0.05 * jax.random.normal(ks[1], (D,), jnp.float32), 'beta': 0.05 * jax.random.normal(ks[2], (D,), jnp.float32), 'Wr': 0.01 * jax.random.normal(ks[3], (D, E), jnp.float32), 'br': jnp.zeros((E,), jnp.float32), 'W1': s * jax.random.normal(ks[4], (E, D, H), jnp.float32), 'b1': s * jax.random.normal(ks[5], (E, H), jnp.float32), 'W2': s * jax.random.normal(ks[6], (E, H, DOUT), jnp.float32), 'b2': s * jax.random.normal(ks[7], (E, DOUT), jnp.float32)}
    _L0_ffn_all = _L0_ffn_setup()
    _L0_ffn_in = {k: v for k, v in _L0_ffn_all.items() if k in ('gamma', 'beta', 'Wr', 'br', 'W1', 'b1', 'W2', 'b2')}
    del _L0_ffn_all
    return {'x': x, 'L0_tok_pe_w': _L0_tok_in['pe_w'], 'L0_tok_pe_b': _L0_tok_in['pe_b'], 'L0_tok_pe_ng': _L0_tok_in['pe_ng'], 'L0_tok_pe_nb': _L0_tok_in['pe_nb'], 'L0_tok_n1g': _L0_tok_in['n1g'], 'L0_tok_n1b': _L0_tok_in['n1b'], 'L0_tok_qkv_w': _L0_tok_in['qkv_w'], 'L0_tok_qkv_b': _L0_tok_in['qkv_b'], 'L0_tok_rpb': _L0_tok_in['rpb'], 'L0_tok_proj_w': _L0_tok_in['proj_w'], 'L0_tok_proj_b': _L0_tok_in['proj_b'], 'L0_tok_n2g': _L0_tok_in['n2g'], 'L0_tok_n2b': _L0_tok_in['n2b'], 'L0_tok_w1': _L0_tok_in['w1'], 'L0_tok_b1': _L0_tok_in['b1'], 'L0_tok_w2': _L0_tok_in['w2'], 'L0_tok_b2': _L0_tok_in['b2'], 'L0_attn_ln1_g': _L0_attn_in['ln1_g'], 'L0_attn_ln1_b': _L0_attn_in['ln1_b'], 'L0_attn_qkv_w': _L0_attn_in['qkv_w'], 'L0_attn_qkv_b': _L0_attn_in['qkv_b'], 'L0_attn_bias_table': _L0_attn_in['bias_table'], 'L0_attn_scale': _L0_attn_in['scale'], 'L0_attn_proj_w': _L0_attn_in['proj_w'], 'L0_attn_proj_b': _L0_attn_in['proj_b'], 'L0_attn_ln2_g': _L0_attn_in['ln2_g'], 'L0_attn_ln2_b': _L0_attn_in['ln2_b'], 'L0_ffn_gamma': _L0_ffn_in['gamma'], 'L0_ffn_beta': _L0_ffn_in['beta'], 'L0_ffn_Wr': _L0_ffn_in['Wr'], 'L0_ffn_br': _L0_ffn_in['br'], 'L0_ffn_W1': _L0_ffn_in['W1'], 'L0_ffn_b1': _L0_ffn_in['b1'], 'L0_ffn_W2': _L0_ffn_in['W2'], 'L0_ffn_b2': _L0_ffn_in['b2']}

def reference(x, L0_tok_pe_w, L0_tok_pe_b, L0_tok_pe_ng, L0_tok_pe_nb, L0_tok_n1g, L0_tok_n1b, L0_tok_qkv_w, L0_tok_qkv_b, L0_tok_rpb, L0_tok_proj_w, L0_tok_proj_b, L0_tok_n2g, L0_tok_n2b, L0_tok_w1, L0_tok_b1, L0_tok_w2, L0_tok_b2, L0_attn_ln1_g, L0_attn_ln1_b, L0_attn_qkv_w, L0_attn_qkv_b, L0_attn_bias_table, L0_attn_scale, L0_attn_proj_w, L0_attn_proj_b, L0_attn_ln2_g, L0_attn_ln2_b, L0_ffn_gamma, L0_ffn_beta, L0_ffn_Wr, L0_ffn_br, L0_ffn_W1, L0_ffn_b1, L0_ffn_W2, L0_ffn_b2):
    import jax
    import jax.numpy as jnp

    def _L0_tok_ref(x, pe_w, pe_b, pe_ng, pe_nb, n1g, n1b, qkv_w, qkv_b, rpb, proj_w, proj_b, n2g, n2b, w1, b1, w2, b2):
        import jax, jax.numpy as jnp
        import numpy as np
        WS = 7
        H = W = 56
        C = 64
        NH = 8
        HD = C // NH
        SCALE = HD ** (-0.5)
        SHIFT = WS // 2
        N = WS * WS

        def _rel_pos_index():
            coords = np.stack(np.meshgrid(np.arange(WS), np.arange(WS), indexing='ij'))
            cf = coords.reshape(2, -1)
            rel = (cf[:, :, None] - cf[:, None, :]).transpose(1, 2, 0).copy()
            rel[..., 0] += WS - 1
            rel[..., 1] += WS - 1
            rel[..., 0] *= 2 * WS - 1
            return jnp.array(rel.sum(-1))

        def _attn_mask():
            img = np.zeros((H, W), np.int32)
            cnt = 0
            for h in (slice(0, -WS), slice(-WS, -SHIFT), slice(-SHIFT, None)):
                for w in (slice(0, -WS), slice(-WS, -SHIFT), slice(-SHIFT, None)):
                    cnt += 1
                    img[h, w] = cnt
            mw = img.reshape(H // WS, WS, W // WS, WS).transpose(0, 2, 1, 3).reshape(-1, N)
            diff = mw[:, None, :] - mw[:, :, None]
            return jnp.array(np.where(diff != 0, -100.0, 0.0).astype(np.float32))

        def _layernorm(x, g, b):
            m = x.mean(-1, keepdims=True)
            v = ((x - m) ** 2).mean(-1, keepdims=True)
            return (x - m) * jax.lax.rsqrt(v + 1e-05) * g + b

        def _window_partition(x):
            B = x.shape[0]
            x = x.reshape(B, H // WS, WS, W // WS, WS, C).transpose(0, 1, 3, 2, 4, 5)
            return x.reshape(-1, N, C)

        def _window_reverse(xw, B):
            x = xw.reshape(B, H // WS, W // WS, WS, WS, C).transpose(0, 1, 3, 2, 4, 5)
            return x.reshape(B, H, W, C)

        def _swin_block(x, p, shift, rpi, amask):
            B = x.shape[0]
            shortcut = x
            h = _layernorm(x, p['n1g'], p['n1b']).reshape(B, H, W, C)
            if shift > 0:
                h = jnp.roll(h, (-shift, -shift), axis=(1, 2))
            xw = _window_partition(h)
            B_ = xw.shape[0]
            qkv = (xw @ p['qkv_w'].T + p['qkv_b']).reshape(B_, N, 3, NH, HD).transpose(2, 0, 3, 1, 4)
            q, k, v = (qkv[0], qkv[1], qkv[2])
            attn = jnp.einsum('bhnd,bhmd->bhnm', q * SCALE, k)
            attn = attn + p['rpb'][rpi].transpose(2, 0, 1)[None]
            if shift > 0:
                nW = amask.shape[0]
                attn = attn.reshape(B_ // nW, nW, NH, N, N) + amask[None, :, None]
                attn = attn.reshape(B_, NH, N, N)
            attn = jax.nn.softmax(attn, axis=-1)
            o = jnp.einsum('bhnm,bhmd->bhnd', attn, v).transpose(0, 2, 1, 3).reshape(B_, N, C)
            o = o @ p['proj_w'].T + p['proj_b']
            h = _window_reverse(o, B)
            if shift > 0:
                h = jnp.roll(h, (shift, shift), axis=(1, 2))
            x = shortcut + h.reshape(B, H * W, C)
            y = _layernorm(x, p['n2g'], p['n2b'])
            y = jax.nn.gelu(y @ p['w1'].T + p['b1'], approximate=False)
            return x + y @ p['w2'].T + p['b2']
        B = x.shape[0]
        h = jax.lax.conv_general_dilated(x, pe_w, (4, 4), 'VALID', dimension_numbers=('NCHW', 'OIHW', 'NCHW'))
        h = h + pe_b[None, :, None, None]
        t = h.reshape(B, C, H * W).transpose(0, 2, 1)
        t = _layernorm(t, pe_ng, pe_nb)
        rpi = _rel_pos_index()
        amask = _attn_mask()
        for i, shift in enumerate((0, SHIFT)):
            p = {'n1g': n1g[i], 'n1b': n1b[i], 'qkv_w': qkv_w[i], 'qkv_b': qkv_b[i], 'rpb': rpb[i], 'proj_w': proj_w[i], 'proj_b': proj_b[i], 'n2g': n2g[i], 'n2b': n2b[i], 'w1': w1[i], 'b1': b1[i], 'w2': w2[i], 'b2': b2[i]}
            t = _swin_block(t, p, shift, rpi, amask)
        return t

    def _L0_attn_ref(x, ln1_g, ln1_b, qkv_w, qkv_b, bias_table, scale, proj_w, proj_b, ln2_g, ln2_b):
        import jax, jax.numpy as jnp
        import numpy as np
        SEQ_LEN = 512
        EMBED_DIM = 64
        BATCH = 8
        LN_EPS = 1e-05

        def _layernorm(x, g, b):
            mu = jnp.mean(x, axis=-1, keepdims=True)
            var = jnp.mean(jnp.square(x - mu), axis=-1, keepdims=True)
            return (x - mu) * jax.lax.rsqrt(var + LN_EPS) * g + b
        B, N, C = x.shape
        h = _layernorm(x, ln1_g, ln1_b)
        qkv = h @ qkv_w + qkv_b
        q, k, v = jnp.split(qkv, 3, axis=-1)
        coords = jnp.arange(N)
        rel_idx = coords[None, :] - coords[:, None] + (N - 1)
        rel_bias = bias_table[rel_idx]
        attn = jnp.einsum('bnc,bmc->bnm', q, k) + rel_bias
        attn = jax.nn.softmax(attn, axis=-1) * scale
        out = jnp.einsum('bnm,bmc->bnc', attn, v)
        out = out @ proj_w + proj_b
        out = _layernorm(out, ln2_g, ln2_b)
        return out

    def _L0_ffn_ref(x, gamma, beta, Wr, br, W1, b1, W2, b2):
        import jax, jax.numpy as jnp
        import numpy as np
        E = 8
        K = 2
        D = 64
        H = 128
        DOUT = 64
        EPS = 1e-05
        mu = jnp.mean(x, axis=-1, keepdims=True)
        var = jnp.mean(jnp.square(x - mu), axis=-1, keepdims=True)
        xn = (x - mu) * jax.lax.rsqrt(var + EPS) * gamma + beta
        logits = jnp.einsum('bsd,de->bse', xn, Wr) + br
        top_vals, top_idx = jax.lax.top_k(logits, K)
        w = jax.nn.softmax(top_vals, axis=-1)
        w_full = jnp.einsum('bsk,bske->bse', w, jax.nn.one_hot(top_idx, E, dtype=w.dtype))
        y = jnp.zeros(x.shape[:-1] + (DOUT,), x.dtype)
        for e in range(E):
            h = jax.nn.gelu(jnp.einsum('bsd,dh->bsh', xn, W1[e]) + b1[e], approximate=False)
            y_e = jnp.einsum('bsh,hd->bsd', h, W2[e]) + b2[e]
            y = y + y_e * w_full[..., e, None]
        return y
    h = _L0_tok_ref(x, L0_tok_pe_w, L0_tok_pe_b, L0_tok_pe_ng, L0_tok_pe_nb, L0_tok_n1g, L0_tok_n1b, L0_tok_qkv_w, L0_tok_qkv_b, L0_tok_rpb, L0_tok_proj_w, L0_tok_proj_b, L0_tok_n2g, L0_tok_n2b, L0_tok_w1, L0_tok_b1, L0_tok_w2, L0_tok_b2)
    h = h + _L0_attn_ref(_layernorm(h, axis=-1), L0_attn_ln1_g, L0_attn_ln1_b, L0_attn_qkv_w, L0_attn_qkv_b, L0_attn_bias_table, L0_attn_scale, L0_attn_proj_w, L0_attn_proj_b, L0_attn_ln2_g, L0_attn_ln2_b)
    h = h + _L0_ffn_ref(_layernorm(h, axis=-1), L0_ffn_gamma, L0_ffn_beta, L0_ffn_Wr, L0_ffn_br, L0_ffn_W1, L0_ffn_b1, L0_ffn_W2, L0_ffn_b2)
    return h

_drawn_inputs = setup_inputs


def setup_inputs(seed=0):
    import zlib

    import numpy as np

    out = dict(_drawn_inputs(seed))
    spreads = {'L0_tok_pe_b': (0.0, 0.1),
     'L0_tok_pe_ng': (1.0, 0.2),
     'L0_tok_pe_nb': (0.0, 0.1),
     'L0_tok_n1g': (1.0, 0.6),
     'L0_tok_n1b': (0.0, 0.8),
     'L0_tok_qkv_b': (0.0, 0.594),
     'L0_tok_proj_b': (0.0, 0.1),
     'L0_tok_n2g': (1.0, 0.6),
     'L0_tok_n2b': (0.0, 0.8),
     'L0_tok_b1': (0.0, 0.53),
     'L0_tok_b2': (0.0, 0.1),
     'L0_attn_ln1_g': (1.0, 0.6),
     'L0_attn_ln1_b': (0.0, 0.8),
     'L0_attn_qkv_b': (0.0, 0.535),
     'L0_attn_proj_b': (0.0, 0.1),
     'L0_attn_ln2_g': (1.0, 0.2),
     'L0_attn_ln2_b': (0.0, 0.1),
     'L0_ffn_br': (0.0, 0.534)}
    factors = {'L0_tok_rpb': 57.47,
     'L0_attn_bias_table': 64.0,
     'L0_ffn_gamma': 8.0,
     'L0_ffn_beta': 8.0,
     'L0_ffn_Wr': 8.0,
     'L0_ffn_W1': 6.032,
     'L0_ffn_b1': 8.0,
     'L0_ffn_W2': 6.301,
     'L0_ffn_b2': 20.156}
    for name, (base, spread) in spreads.items():
        noise = np.random.default_rng([zlib.crc32(name.encode()), seed]).standard_normal(out[name].shape)
        drawn = base * np.exp(spread * noise) if base else spread * noise
        out[name] = jnp.asarray(drawn.astype(out[name].dtype))
    for name, factor in factors.items():
        out[name] = (out[name] * factor).astype(out[name].dtype)
    return out
```

```python
import concourse.bass as bass
from concourse import mybir
from contextlib import ExitStack

F32 = mybir.dt.float32
BF16 = mybir.dt.bfloat16
U32 = mybir.dt.uint32
ALU = mybir.AluOpType
ACT = mybir.ActivationFunctionType
AX = mybir.AxisListType.X

B, HW, C = 4, 56, 64
PAIRS = B // 2
TP = 2 * HW
GW = 8
GROUPS = HW // GW
HALF = GW // 2 * TP
WS, NH, HD = 7, 8, 8
WN = WS * WS
NW = HW // WS
SHIFT = WS // 2
SCALE = HD ** -0.5
SLOT = 64
YW, YH = 66, 59
HP = NH // 2
N = HW * HW
KT = N // TP
QT = N // HALF
QFLAT = 4
KBIAS = 10
TAB = 1023
AK = 96
E, HID = 8, 128
EPS = 1e-5
BLOCKS = 2

COLS = (["n1g0", "n1b0", "n1g1", "n1b1", "n2g0", "n2b0", "n2g1", "n2b1", "qb0", "kb0", "qb1", "kb1",
         "ag", "ab", "fg", "fb", "scale", "last"]
        + [f"mb{l}{f}" for l in range(2) for f in range(2)] + [f"eb{e}" for e in range(E)])
ROWS = ["peb", "peg", "pen", "b20", "b21", "apb", "a2g", "a2b"]

LOADS = {
    "image_loaded": "pixels and the embedding's weights",
    "constants_loaded": "constants",
    "tables_loaded": "a stage's tables",
    "mlp_weights_loaded": "the MLP's weights",
    "stored": "the result is in DRAM",
}
SIGNALS = {
    "attn_evacuated": "ScalarE: a query tile's outputs and denominators are in SBUF",
    "attn_exponentials": "ScalarE: a key tile's exponentials are in SBUF",
    "attn_scored": "TensorE: a key tile's scores less the maxima",
    "attn_weighted": "TensorE: a key tile's values are added to the outputs",
    "bias_flipped": "TensorE: a piece of the Toeplitz bias is turned round",
    "bias_set": "VectorE: bias rows or pieces are in place",
    "centred": "VectorE: a group less its means",
    "cleared": "GpSimd: padding and fixed rows are set",
    "conv_biased": "VectorE: a group's patch embedding is in the residual stream, before its norm",
    "convolved": "TensorE: a group's patch embedding",
    "denominators_read": "VectorE: reciprocals of the denominators",
    "denominators_ready": "TensorE: the denominators on their heads' partitions",
    "embedded": "GpSimd: a group's normalised embedding is in the residual stream",
    "evacuated": "ScalarE: a channel-major half group with its gain and bias",
    "expert_biased": "VectorE: a column's expert outputs with their biases",
    "expert_gelu": "ScalarE: an expert's hidden activations",
    "expert_hidden": "TensorE: an expert's hidden layer",
    "expert_weighted": "GpSimd: a column's expert outputs times their gates",
    "experts_done": "TensorE: a column's expert outputs",
    "exponentials_ready": "ScalarE: a pair of windows' exponentials",
    "gain_applied": "GpSimd: a group times its gain",
    "gate_scored": "TensorE: a group's router logits",
    "gate_step": "VectorE: a step of the gating",
    "gelu_done": "ScalarE: half of the hidden activations of a half group",
    "hidden_ready": "TensorE: half of the hidden layer of a half group",
    "keys_by_head": "GpSimd: a chunk's keys, block-diagonal by head",
    "keys_evacuated": "the keys have left PSUM",
    "keys_ready": "TensorE: a tile of keys",
    "keys_rounded": "ScalarE: a key tile's high part, and the tile itself",
    "lead_ready": "VectorE: the first logit less the second",
    "maxima_ready": "VectorE: maxima of rows of scores",
    "maximum_moved": "TensorE: the maxima as a row",
    "maximum_set": "ScalarE: that row is below the queries",
    "mean_ready": "VectorE: a group's means",
    "mixed": "VectorE: a column's sum over experts",
    "mlp_biased": "GpSimd: the second layer's bias is added to the residual stream",
    "mlp_ready": "TensorE: a group's MLP output",
    "normalised": "VectorE: a group's normalised tokens",
    "ones_set": "GpSimd: rows and columns of ones",
    "output_ready": "GpSimd: a group of the attention's output with gain and bias",
    "outputs_evacuated": "ScalarE: a chunk's outputs are in SBUF",
    "outputs_normalised": "VectorE: outputs over their denominators",
    "outputs_ready": "TensorE: a chunk's outputs",
    "outputs_staged": "GpSimd: a group's outputs are in the projection's buffer",
    "patchT_ready": "VectorE: transposed patches are in SBUF",
    "patches_ready": "VectorE: a group's pixels by patch",
    "patches_transposed": "TensorE: a group's patches, transposed",
    "probs_evacuated": "ScalarE: transposed exponentials are in SBUF",
    "probs_transposed": "TensorE: exponentials, transposed",
    "projected": "TensorE: a group's projection",
    "projection_biased": "VectorE: a group's projection with its bias",
    "qbias_ready": "VectorE: the scaled query biases",
    "qk_ready": "TensorE: a chunk's queries and keys",
    "queries_evacuated": "ScalarE: a chunk's queries are in SBUF",
    "queries_split": "VectorE: a query tile's low part",
    "query_ready": "TensorE: a query tile",
    "query_rounded": "ScalarE: a query tile's high part, and the tile itself",
    "residual_added": "a group of the residual stream is up to date",
    "row_maximum": "VectorE: minus the maxima of a query tile",
    "rstd_ready": "GpSimd: a group's reciprocal standard deviations",
    "scores_biased": "VectorE: a key tile's scores with varying bias",
    "scores_ready": "TensorE: a pair of windows' scores",
    "shifted": "VectorE: a pair of windows' scores less their maxima",
    "squared": "ScalarE: squares of a centred group",
    "squares_summed": "VectorE: their sums",
    "summed": "VectorE: a group's sums",
    "tanh_ready": "ScalarE: tanh of half the lead",
    "tile_biased": "VectorE: a score tile with varying bias, for the maximum",
    "tile_maximum": "VectorE: a score tile's row maxima",
    "tile_scored": "TensorE: a score tile for the maximum",
    "tokens_staged": "GpSimd: an image's tokens are in the fixed buffer",
    "transposed": "TensorE: a half group, transposed",
    "values_by_head": "VectorE: a chunk's values, block-diagonal by head",
    "values_evacuated": "ScalarE: seven tiles of values are in SBUF",
    "values_ready": "TensorE: values",
    "variance_ready": "VectorE: a group's variances with epsilon",
    "weights_scaled": "VectorE: reciprocals times the attention's scale",
    "windows_staged": "GpSimd: a chunk's windows are in the fixed buffer",
    "wrapped": "GpSimd: copies at the image's seam",
}



def build(nc, img, out, d):
    ctx = ExitStack()
    with ctx:
        def sb(name, shape, dt=F32):
            return ctx.enter_context(nc.sbuf_tensor(name, shape, dt))

        class Signal:
            def __init__(self, name):
                self.sem, self.past = ctx.enter_context(nc.semaphore(name)), int(name in SIGNALS)

            def at(self, n):
                return n + self.past

        on = {name: Signal(name) for name in (*LOADS, *SIGNALS)}

        def ended(**counts):
            for name, n in counts.items():
                on[name].past += n

        with nc.Block() as block:
            @block.sync
            def _(e):
                for name in SIGNALS:
                    e.nop(nofuse=True).then_inc(on[name].sem, 1)

        xr = sb("xr", [TP, PAIRS * HW + GW, C])
        ident = sb("ident", [128, 128])
        cols = sb("cols_sb", [128, len(COLS)])
        rows = sb("rows_sb", [TP, len(ROWS), C])
        neghalf = sb("neghalf", [TP, GW])
        cent = sb("cent", [TP, 2, GW, C])
        sq = sb("sq", [TP, GW, C])
        stat = sb("stat", [TP, 5, GW])
        bank = [ctx.enter_context(nc.psum_tensor(f"bank{i}", [128, 512], F32)) for i in range(8)]

        def col(name, p0=0, p1=C):
            return cols[p0:p1, COLS.index(name):COLS.index(name) + 1]

        def row(name, n=GW):
            return rows[:, ROWS.index(name), :].unsqueeze(1).broadcast_to([TP, n, C])

        def group(p, w):
            return xr[:, bass.ds(p * HW + w, GW), :]

        def per_token(ap):
            return ap.unsqueeze(2).broadcast_to([TP, GW, C])

        def norm_vector(e, x, k, n, freed=None, weight=1.0, extra=EPS, copy_out=None):
            e.tensor_reduce(out=stat[:, 0, :], in_=x, axis=AX, op=ALU.add).then_inc(on["summed"].sem, 1)
            e.wait_ge(on["summed"].sem, on["summed"].at(n + 1))
            e.tensor_scalar(stat[:, 1, :], stat[:, 0, :], 1.0 / C, None, ALU.mult).then_inc(on["mean_ready"].sem, 1)
            e.wait_ge(on["mean_ready"].sem, on["mean_ready"].at(n + 1))
            if freed:
                e.wait_ge(freed[0].sem, freed[0].at(freed[1]))
            e.tensor_tensor(cent[:, k], x, per_token(stat[:, 1, :]), ALU.subtract).then_inc(on["centred"].sem, 1)
            e.wait_ge(on["squared"].sem, on["squared"].at(n + 1))
            e.tensor_reduce(out=stat[:, 2, :], in_=sq[:], axis=AX, op=ALU.add).then_inc(on["squares_summed"].sem, 1)
            e.wait_ge(on["squares_summed"].sem, on["squares_summed"].at(n + 1))
            e.tensor_scalar(stat[:, 3, :], stat[:, 2, :], weight / C, extra, ALU.mult, ALU.add).then_inc(on["variance_ready"].sem, 1)
            e.wait_ge(on["rstd_ready"].sem, on["rstd_ready"].at(n + 1))
            e.tensor_tensor(cent[:, k], cent[:, k], per_token(stat[:, 4, :]), ALU.mult).then_inc(on["normalised"].sem, 1)

        def norm_scalar(e, k, n):
            e.wait_ge(on["centred"].sem, on["centred"].at(n + 1))
            e.activation(sq[:], cent[:, k], ACT.Square).then_inc(on["squared"].sem, 1)

        def norm_gpsimd(e, n):
            e.wait_ge(on["variance_ready"].sem, on["variance_ready"].at(n + 1))
            e.tensor_tensor(stat[:, 4, :], stat[:, 3, :], neghalf[:], ALU.pow).then_inc(on["rstd_ready"].sem, 1)

        def norm_ended(n):
            ended(summed=n, mean_ready=n, centred=n, squared=n, squares_summed=n, variance_ready=n,
                  rstd_ready=n, normalised=n)

        def transpose_group(e, k, n):
            e.wait_ge(on["normalised"].sem, on["normalised"].at(n + 1))
            e.wait_ge(on["evacuated"].sem, on["evacuated"].at(2 * n))
            e.nop(nofuse=True)
            for half in range(2):
                for w in range(4):
                    last = e.transpose(bank[half][0:C, w * TP:(w + 1) * TP], cent[:, k, half * 4 + w, :],
                                       ident[0:TP, 0:TP])
                last.then_inc(on["transposed"].sem, 1)

        def loop_groups(e, body):
            with e.Fori(0, GROUPS) as j:
                body(2 * j, 0, GW * j, 1, GW * j)
                body(2 * j + 1, 1, GW * j, 0, GW * j + GW)

        wqk, wv, pw = sb("wqk", [C, BLOCKS, 128]), sb("wv", [C + 1, BLOCKS, C]), sb("pw", [128, BLOCKS, C])
        awq, awk, awv, awp = sb("awq", [C, C]), sb("awk", [C, C]), sb("awv", [C + 1, C]), sb("awp", [C + 1, C + 1])
        qbias = sb("qbias", [C, BLOCKS])
        loads = [(ident[:], d["ident"]), (cols[:], d["cols"]),
                 (rows[:], d["rows"].unsqueeze(0).broadcast_to([TP, len(ROWS), C])),
                 (wqk[:], d["wqk"]), (wv[:], d["wv"]), (pw[:], d["pw"]),
                 (awq[:], d["awq"]), (awk[:], d["awk"]), (awv[:], d["awv"]), (awp[:], d["awp"])]
        with ExitStack() as part:
            px = part.enter_context(nc.sbuf_tensor("px", [TP, PAIRS, 4, 4 * (HW + GW)], F32))
            patches = part.enter_context(nc.sbuf_tensor("patches", [TP, GW, 16], F32))
            patchT = part.enter_context(nc.sbuf_tensor("patchT", [128, 2, TP], F32))
            gained = part.enter_context(nc.sbuf_tensor("gained", [TP, GW, C], F32))
            pew = part.enter_context(nc.sbuf_tensor("pew", [128, GW * C], F32))
            with nc.Block() as block:
                @block.sync
                def _(e):
                    for p in range(PAIRS):
                        for b in range(2):
                            e.dma_start(px[HW * b:HW * (b + 1), p, :, 0:4 * HW],
                                             img[2 * p + b, 0].rearrange("(h i) w -> h i w", i=4)).then_inc(on["image_loaded"].sem, 16)
                    e.dma_start(pew[:], d["pew"]).then_inc(on["image_loaded"].sem, 16)
                    for to, src in loads:
                        e.dma_start(to, src).then_inc(on["constants_loaded"].sem, 16)

                @block.gpsimd
                def _(e):
                    e.memset(neghalf[:], -0.5).then_inc(on["cleared"].sem, 1)
                    e.memset(px[:, :, :, 4 * HW:], 0.0).then_inc(on["cleared"].sem, 1)
                    e.memset(xr[:, PAIRS * HW:, :], 0.0).then_inc(on["cleared"].sem, 1)
                    e.wait_ge(on["cleared"].sem, on["cleared"].at(3))

                    def body(n, p, w, p1, w1):
                        norm_gpsimd(e, n)
                        e.wait_ge(on["normalised"].sem, on["normalised"].at(n + 1))
                        e.tensor_tensor(gained[:], cent[:, p], row("peg"), ALU.mult).then_inc(on["gain_applied"].sem, 1)
                        e.wait_ge(on["gain_applied"].sem, on["gain_applied"].at(n + 1))
                        e.tensor_tensor(group(p, w), gained[:], row("pen"), ALU.add).then_inc(on["embedded"].sem, 1)
                        e.wait_ge(on["embedded"].sem, on["embedded"].at(n + 1))
                    loop_groups(e, body)

                @block.vector
                def _(e):
                    e.wait_ge(on["image_loaded"].sem, on["image_loaded"].at(16 * 5))
                    e.wait_ge(on["constants_loaded"].sem, on["constants_loaded"].at(16 * len(loads)))
                    e.wait_ge(on["cleared"].sem, on["cleared"].at(3))
                    for l in range(BLOCKS):
                        e.tensor_scalar(qbias[:, l:l + 1], col(f"qb{l}"), SCALE, None, ALU.mult).then_inc(on["qbias_ready"].sem, 1)

                    def take_patches(n, p, w):
                        e.wait_ge(on["patches_transposed"].sem, on["patches_transposed"].at(n))
                        e.tensor_copy(patches[:].rearrange("q w (i j) -> q w i j", i=4),
                                           px[:, p, :, bass.ds(4 * w, 4 * GW)].rearrange("q i (w j) -> q w i j", j=4)).then_inc(on["patches_ready"].sem, 1)
                        e.wait_ge(on["patches_transposed"].sem, on["patches_transposed"].at(n + 1))
                        e.tensor_copy(patchT[:, p], bank[2 + p][:, 0:TP]).then_inc(on["patchT_ready"].sem, 1)

                    take_patches(0, 0, 0)

                    def body(n, p, w, p1, w1):
                        take_patches(n + 1, p1, w1)
                        e.wait_ge(on["convolved"].sem, on["convolved"].at(n + 1))
                        e.tensor_tensor(group(p, w), bank[4 + p][0:TP, :].rearrange("q (w c) -> q w c", c=C),
                                             row("peb"), ALU.add).then_inc(on["conv_biased"].sem, 1)
                        e.wait_ge(on["conv_biased"].sem, on["conv_biased"].at(n + 1))
                        e.nop(nofuse=True)
                        norm_vector(e, group(p, w), p, n, freed=(on["embedded"], n))
                    loop_groups(e, body)

                @block.scalar
                def _(e):
                    loop_groups(e, lambda n, p, w, p1, w1: norm_scalar(e, p, n))

                @block.tensor
                def _(e):
                    def convolve(n, p):
                        e.wait_ge(on["patches_ready"].sem, on["patches_ready"].at(n + 1))
                        e.wait_ge(on["patchT_ready"].sem, on["patchT_ready"].at(n))
                        e.transpose(bank[2 + p][:, 0:TP], patches[:].rearrange("q w i -> q (w i)"),
                                         ident[0:TP, 0:TP]).then_inc(on["patches_transposed"].sem, 1)
                        e.wait_ge(on["patchT_ready"].sem, on["patchT_ready"].at(n + 1))
                        e.matmul(bank[4 + p][0:TP, :], patchT[:, p], pew[:], start=True, stop=True).then_inc(on["convolved"].sem, 1)

                    convolve(0, 0)

                    def body(n, p, w, p1, w1):
                        e.wait_ge(on["conv_biased"].sem, on["conv_biased"].at(n))
                        convolve(n + 1, p1)
                    loop_groups(e, body)
            G = PAIRS * GROUPS
            norm_ended(G)
            ended(image_loaded=16 * 5, constants_loaded=16 * len(loads), cleared=3, qbias_ready=2, gain_applied=G,
                  embedded=G, patches_transposed=G + 1, patches_ready=G + 1, patchT_ready=G + 1, conv_biased=G,
                  convolved=G + 1)

        def swin_block(l):
            shift = SHIFT * l
            with ExitStack() as part:
                def psb(name, shape, dt=F32):
                    return part.enter_context(nc.sbuf_tensor(f"{name}_{l}", shape, dt))

                yo = psb("yo", [128, B, YW, YH])
                ywin = psb("ywin", [C + 1, 2, NW, SLOT])
                qwin = psb("qwin", [C + WN, 2, NW, SLOT])
                ksb = psb("ksb", [C, NW, SLOT])
                kbd = psb("kbd", [C + WN, 2, NW, NH, WN])
                vbd = psb("vbd", [128, 2, NW, HP, 32])
                P = psb("P", [128, 2, NH, SLOT])
                pT = psb("pT", [128, 2, 512])
                mx = psb("mx", [128, 2, NH])
                osb = psb("osb", [128, 512])
                rden = psb("rden", [128, 512])
                sel, heads, vmask = psb("sel", [128, 128]), psb("heads", [C, NH]), psb("vmask", [128, 16])
                rpb = psb("rpb", [C + WN, NH, WN])
                masks = psb("masks", [C + WN, 3, WN])

                with nc.Block() as block:
                    @block.sync
                    def _(e):
                        for to, src in ((sel[:], d["sel"]), (heads[:], d["heads"]), (vmask[:], d["vmask"]),
                                        (rpb[C:C + WN], d["rpb"][:, l]), (masks[C:C + WN], d["masks"])):
                            e.dma_start(to, src).then_inc(on["tables_loaded"].sem, 16)
                        for k in range(2):
                            for s in range(NW):
                                e.dma_start(qwin[C:C + WN, k, s, 0:WN], d["ident"][0:WN, 0:WN]).then_inc(on["tables_loaded"].sem, 16)
                        e.wait_ge(on["tables_loaded"].sem, on["tables_loaded"].at(16 * (5 + 2 * NW)))

                    @block.gpsimd
                    def _(e):
                        for i, a in enumerate((ywin[0:C], qwin[:, :, :, WN:], P[:], vbd[:], yo[0:C, :, HW:, :],
                                               yo[0:C, :, 0:HW, HW:])):
                            e.memset(a, 0.0).then_inc(on["cleared"].sem, 1)
                            e.wait_ge(on["cleared"].sem, on["cleared"].at(i + 1))
                        for i, a in enumerate((ywin[C:C + 1], vbd[0:C, :, :, :, 16:17], vbd[C:128, :, :, :, 17:18])):
                            e.memset(a, 1.0).then_inc(on["ones_set"].sem, 1)
                            e.wait_ge(on["ones_set"].sem, on["ones_set"].at(i + 1))
                        norm_gpsimd(e, 0)
                        loop_groups(e, lambda n, p, w, p1, w1: norm_gpsimd(e, n + 1))

                    @block.vector
                    def _(e):
                        norm_vector(e, group(0, 0), 0, 0)

                        def body(n, p, w, p1, w1):
                            e.nop(nofuse=True)
                            norm_vector(e, group(p1, w1), p1, n + 1, freed=(on["transposed"], 2 * n))
                        loop_groups(e, body)

                    @block.tensor
                    def _(e):
                        loop_groups(e, lambda n, p, w, p1, w1: transpose_group(e, p, n))

                    @block.scalar
                    def _(e):
                        e.wait_ge(on["cleared"].sem, on["cleared"].at(6))
                        norm_scalar(e, 0, 0)

                        def body(n, p, w, p1, w1):
                            norm_scalar(e, p1, n + 1)
                            for half in range(2):
                                e.wait_ge(on["transposed"].sem, on["transposed"].at(2 * n + half + 1))
                                e.nop(nofuse=True)
                                e.activation(yo[0:C, 2 * p:2 * p + 2, bass.ds(w + 4 * half, 4), 0:HW]
                                                  .rearrange("c b w h -> c w b h"),
                                                  bank[half][0:C, 0:HALF].rearrange("c (w b h) -> c w b h", w=4, b=2),
                                                  ACT.Identity, scale=col(f"n1g{l}"), bias=col(f"n1b{l}")).then_inc(on["evacuated"].sem, 1)
                        loop_groups(e, body)
                norm_ended(2 * GROUPS + 1)
                ended(transposed=4 * GROUPS, evacuated=4 * GROUPS, tables_loaded=16 * (5 + 2 * NW), cleared=6, ones_set=3)

                def bias_rows(e, w_edge):
                    for k in range(2):
                        for s in range(NW):
                            to = kbd[C:C + WN, k, s]
                            m = (2 if w_edge else 0) if s == NW - 1 else 1 if w_edge else None
                            if shift and m is not None:
                                ins = e.tensor_tensor(to, rpb[C:C + WN],
                                                      masks[C:C + WN, m].unsqueeze(1).broadcast_to([WN, NH, WN]), ALU.add)
                            else:
                                ins = e.tensor_copy(to, rpb[C:C + WN])
                            ins.then_inc(on["bias_set"].sem, 1)

                with nc.Block() as block:
                    @block.vector
                    def _(e):
                        bias_rows(e, False)
                        e.wait_ge(on["bias_set"].sem, on["bias_set"].at(2 * NW))
                    if shift:
                        @block.gpsimd
                        def _(e):
                            e.tensor_copy(yo[0:C, :, 0:HW, HW:HW + shift], yo[0:C, :, 0:HW, 0:shift]).then_inc(on["wrapped"].sem, 1)
                            e.wait_ge(on["wrapped"].sem, on["wrapped"].at(1))
                            e.tensor_copy(yo[0:C, :, HW:HW + shift, 0:HW + shift], yo[0:C, :, 0:shift, 0:HW + shift]).then_inc(on["wrapped"].sem, 1)
                            e.wait_ge(on["wrapped"].sem, on["wrapped"].at(2))
                ended(bias_set=2 * NW, wrapped=2 if shift else 0)

                def windows(w_from, w_to):
                    chunks, pairs = (w_to - w_from) * B, (w_to - w_from) * B * 4

                    def tokens(b, w):
                        return yo[:, b, bass.ds(WS * w + shift, WS), shift:shift + HW].rearrange("c w (s r) -> c s w r", r=WS)

                    def slots(ap):
                        return ap[:, :, 0:WN].rearrange("c s (w r) -> c s w r", w=WS)

                    def loop_chunks(e, head, main):
                        head(0, 0, w_from, 0)
                        with e.Fori(w_from, w_to) as i:
                            for b in range(B):
                                n = (i - w_from) * B + b
                                main(n, b, i, b % 2, lambda: head(n + 1, (b + 1) % B, i + (b + 1) // B, (b + 1) % 2))

                    QK, V, S, T, O, D = bank[0], bank[1], (bank[2], bank[3]), (bank[4], bank[5]), bank[6], bank[7]

                    with nc.Block() as block:
                        @block.gpsimd
                        def _(e):
                            def head(n, b, w, k):
                                e.wait_ge(on["keys_evacuated"].sem, on["keys_evacuated"].at(n))
                                e.nop(nofuse=True)
                                e.tensor_copy(slots(ywin[0:C, k]), tokens(b, w)[0:C]).then_inc(on["windows_staged"].sem, 1)
                                e.wait_ge(on["keys_evacuated"].sem, on["keys_evacuated"].at(n + 1))
                                e.tensor_tensor(kbd[0:C, k], ksb[:, :, 0:WN].unsqueeze(2).broadcast_to([C, NW, NH, WN]),
                                                     heads[:].unsqueeze(1).unsqueeze(3).broadcast_to([C, NW, NH, WN]),
                                                     ALU.mult).then_inc(on["keys_by_head"].sem, 1)
                            loop_chunks(e, head, lambda n, b, w, k, ahead: ahead())

                        @block.tensor
                        def _(e):
                            e.nop(nofuse=True).then_inc(on["probs_transposed"].sem, 1)

                            def head(n, b, w, k):
                                e.wait_ge(on["windows_staged"].sem, on["windows_staged"].at(n + 1))
                                e.wait_ge(on["keys_evacuated"].sem, on["keys_evacuated"].at(n))
                                e.matmul(QK[:, :], wqk[:, l], ywin[0:C, k].rearrange("c s t -> c (s t)"),
                                              start=True, stop=True).then_inc(on["qk_ready"].sem, 1)
                                e.wait_ge(on["values_by_head"].sem, on["values_by_head"].at(n))
                                for s in range(NW):
                                    for half in range(2):
                                        last = e.matmul(V[64 * half:64 * half + 64, s * C:(s + 1) * C], ywin[:, k, s],
                                                        wv[:, l], start=True, stop=True)
                                last.then_inc(on["values_ready"].sem, 1)

                            def scores(n, g, k):
                                e.wait_ge(on["shifted"].sem, on["shifted"].at(4 * n + g + 1))
                                for a in range(2):
                                    s = 2 * g + a
                                    last = e.matmul(S[g % 2][64 * a:64 * a + 64, 0:NH * WN], qwin[:, k, s],
                                                    kbd[:, k, s].rearrange("c h t -> c (h t)"), start=True, stop=True)
                                last.then_inc(on["scores_ready"].sem, 1)

                            def transposes(n, g):
                                e.wait_ge(on["exponentials_ready"].sem, on["exponentials_ready"].at(4 * n + g + 1))
                                e.wait_ge(on["probs_evacuated"].sem, on["probs_evacuated"].at(4 * n + g + 1))
                                for hp in range(HP):
                                    last = e.transpose(T[g % 2][:, 128 * hp:128 * hp + 128],
                                                       P[:, g % 2, 2 * hp:2 * hp + 2].rearrange("q h t -> q (h t)"), ident[:])
                                last.then_inc(on["probs_transposed"].sem, 1)

                            def weighted(n, g, k):
                                e.wait_ge(on["probs_evacuated"].sem, on["probs_evacuated"].at(4 * n + g + 3))
                                if g == 0:
                                    e.wait_ge(on["outputs_evacuated"].sem, on["outputs_evacuated"].at(n))
                                for a in range(2):
                                    for hp in range(HP):
                                        s = 2 * g + a
                                        last = e.matmul(O[32 * hp:32 * hp + 32, s * SLOT:(s + 1) * SLOT], vbd[:, k, s, hp],
                                                        pT[:, g % 2, 128 * hp + 64 * a:128 * hp + 64 * a + 64],
                                                        start=True, stop=True)
                                if g == 3:
                                    last.then_inc(on["outputs_ready"].sem, 1)

                            def main(n, b, w, k, ahead):
                                e.wait_ge(on["keys_by_head"].sem, on["keys_by_head"].at(n + 1))
                                scores(n, 0, k)
                                ahead()
                                scores(n, 1, k)
                                transposes(n, 0)
                                scores(n, 2, k)
                                e.wait_ge(on["values_by_head"].sem, on["values_by_head"].at(n + 1))
                                weighted(n, 0, k)
                                transposes(n, 1)
                                scores(n, 3, k)
                                weighted(n, 1, k)
                                transposes(n, 2)
                                weighted(n, 2, k)
                                transposes(n, 3)
                                weighted(n, 3, k)
                                e.wait_ge(on["outputs_evacuated"].sem, on["outputs_evacuated"].at(n + 1))
                                e.wait_ge(on["denominators_read"].sem, on["denominators_read"].at(n))
                                e.matmul(D[:, :], sel[:], osb[:], start=True, stop=True).then_inc(on["denominators_ready"].sem, 1)
                            loop_chunks(e, head, main)

                        @block.scalar
                        def _(e):
                            e.nop(nofuse=True).then_inc(on["probs_evacuated"].sem, 2)

                            def head(n, b, w, k):
                                e.wait_ge(on["qk_ready"].sem, on["qk_ready"].at(n + 1))
                                e.activation(qwin[0:C, k].rearrange("c s t -> c (s t)"), QK[0:C, :], ACT.Identity,
                                                  scale=SCALE, bias=qbias[:, l:l + 1]).then_inc(on["queries_evacuated"].sem, 1)
                                e.wait_ge(on["keys_by_head"].sem, on["keys_by_head"].at(n))
                                e.activation(ksb[:].rearrange("c s t -> c (s t)"), QK[C:128, :], ACT.Identity,
                                                  bias=col(f"kb{l}")).then_inc(on["keys_evacuated"].sem, 1)

                            def exponentials(n, g):
                                e.wait_ge(on["shifted"].sem, on["shifted"].at(4 * n + g + 3))
                                e.activation(P[:, g % 2, :, 0:WN], P[:, g % 2, :, 0:WN], ACT.Exp).then_inc(on["exponentials_ready"].sem, 1)

                            def evacuate(n, g):
                                e.wait_ge(on["probs_transposed"].sem, on["probs_transposed"].at(4 * n + g + 2))
                                e.copy(pT[:, g % 2], T[g % 2][:, :]).then_inc(on["probs_evacuated"].sem, 1)

                            def main(n, b, w, k, ahead):
                                exponentials(n, 0)
                                ahead()
                                exponentials(n, 1)
                                evacuate(n, 0)
                                exponentials(n, 2)
                                evacuate(n, 1)
                                exponentials(n, 3)
                                evacuate(n, 2)
                                evacuate(n, 3)
                                e.wait_ge(on["outputs_ready"].sem, on["outputs_ready"].at(n + 1))
                                e.wait_ge(on["outputs_normalised"].sem, on["outputs_normalised"].at(n))
                                e.copy(osb[:], O[:, :]).then_inc(on["outputs_evacuated"].sem, 1)
                            loop_chunks(e, head, main)

                        @block.vector
                        def _(e):
                            e.nop(nofuse=True).then_inc(on["shifted"].sem, 2)

                            def head(n, b, w, k):
                                e.wait_ge(on["values_ready"].sem, on["values_ready"].at(n + 1))
                                e.tensor_tensor(vbd[:, k, :, :, 0:16].rearrange("t s h c -> t (s h) c"),
                                                     V[:, :].rearrange("t (x c) -> t x c", c=16),
                                                     vmask[:].unsqueeze(1).broadcast_to([128, NW * HP, 16]), ALU.mult).then_inc(on["values_by_head"].sem, 1)

                            def shift_scores(n, g):
                                e.wait_ge(on["scores_ready"].sem, on["scores_ready"].at(4 * n + g + 1))
                                sc = S[g % 2][:, 0:NH * WN].rearrange("q (h t) -> q h t", h=NH)
                                e.tensor_reduce(out=mx[:, g % 2], in_=sc, axis=AX, op=ALU.max).then_inc(on["maxima_ready"].sem, 1)
                                e.wait_ge(on["maxima_ready"].sem, on["maxima_ready"].at(4 * n + g + 1))
                                e.wait_ge(on["probs_transposed"].sem, on["probs_transposed"].at(4 * n + g))
                                e.tensor_tensor(P[:, g % 2, :, 0:WN], sc,
                                                     mx[:, g % 2].unsqueeze(2).broadcast_to([128, NH, WN]), ALU.subtract).then_inc(on["shifted"].sem, 1)

                            def main(n, b, w, k, ahead):
                                shift_scores(n, 0)
                                ahead()
                                for g in range(1, 4):
                                    shift_scores(n, g)
                                e.wait_ge(on["denominators_ready"].sem, on["denominators_ready"].at(n + 1))
                                e.reciprocal(rden[:], D[:, :]).then_inc(on["denominators_read"].sem, 1)
                                e.wait_ge(on["denominators_read"].sem, on["denominators_read"].at(n + 1))
                                e.tensor_tensor(tokens(b, w), slots(osb[:].rearrange("c (s t) -> c s t", s=NW)),
                                                     slots(rden[:].rearrange("c (s t) -> c s t", s=NW)), ALU.mult).then_inc(on["outputs_normalised"].sem, 1)
                            loop_chunks(e, head, main)
                    h, g = chunks + 1, pairs
                    ended(windows_staged=h, keys_evacuated=h, keys_by_head=h, qk_ready=h, values_ready=h, values_by_head=h,
                          queries_evacuated=h, shifted=g + 2, scores_ready=g, exponentials_ready=g, probs_evacuated=g + 2,
                          probs_transposed=g + 1, maxima_ready=g, outputs_evacuated=chunks, outputs_ready=chunks,
                          denominators_ready=chunks, denominators_read=chunks, outputs_normalised=chunks)

                windows(0, NW - 1 if shift else NW)
                if shift:
                    with nc.Block() as block:
                        @block.vector
                        def _(e):
                            bias_rows(e, True)
                            e.wait_ge(on["bias_set"].sem, on["bias_set"].at(2 * NW))
                    ended(bias_set=2 * NW)
                    windows(NW - 1, NW)
                    with nc.Block() as block:
                        @block.gpsimd
                        def _(e):
                            e.tensor_copy(yo[:, :, 0:shift, shift:HW + shift], yo[:, :, HW:HW + shift, shift:HW + shift]).then_inc(on["wrapped"].sem, 1)
                            e.wait_ge(on["wrapped"].sem, on["wrapped"].at(1))
                            e.tensor_copy(yo[:, :, 0:HW, 0:shift], yo[:, :, 0:HW, HW:HW + shift]).then_inc(on["wrapped"].sem, 1)
                            e.wait_ge(on["wrapped"].sem, on["wrapped"].at(2))
                    ended(wrapped=2)

                ost = osb2 = psb("ost", [128, 2, GW, TP])
                with nc.Block() as block:
                    @block.gpsimd
                    def _(e):
                        def body(n, p, w, p1, w1):
                            e.wait_ge(on["projected"].sem, on["projected"].at(n))
                            e.nop(nofuse=True)
                            e.tensor_copy(ost[:, p].rearrange("c w (b h) -> c w b h", b=2),
                                               yo[:, 2 * p:2 * p + 2, bass.ds(w, GW), 0:HW].rearrange("c b w h -> c w b h")).then_inc(on["outputs_staged"].sem, 1)
                        loop_groups(e, body)

                    @block.tensor
                    def _(e):
                        def body(n, p, w, p1, w1):
                            e.wait_ge(on["outputs_staged"].sem, on["outputs_staged"].at(n + 1))
                            e.wait_ge(on["residual_added"].sem, on["residual_added"].at(n))
                            for x in range(GW):
                                last = e.matmul(bank[p][0:TP, C * x:C * (x + 1)], ost[:, p, x], pw[:, l], start=True, stop=True)
                            last.then_inc(on["projected"].sem, 1)
                        loop_groups(e, body)

                    @block.vector
                    def _(e):
                        def body(n, p, w, p1, w1):
                            e.wait_ge(on["projected"].sem, on["projected"].at(n + 1))
                            e.tensor_tensor(group(p, w), group(p, w), bank[p][0:TP, :].rearrange("t (w c) -> t w c", c=C),
                                                 ALU.add).then_inc(on["residual_added"].sem, 1)
                        loop_groups(e, body)
                G = 2 * GROUPS
                ended(outputs_staged=G, projected=G, residual_added=G)

            with ExitStack() as part:
                def psb(name, shape, dt=F32):
                    return part.enter_context(nc.sbuf_tensor(f"{name}_{l}", shape, dt))
                y = psb("mlp_in", [C, GW, TP])
                hid = psb("mlp_hid", [128, 2, GW, TP])
                w1, w2 = psb("w1", [C, 2 * HID]), psb("w2", [128, 2, C])
                with nc.Block() as block:
                    @block.sync
                    def _(e):
                        e.dma_start(w1[:], d["w1"][:, l]).then_inc(on["mlp_weights_loaded"].sem, 16)
                        e.dma_start(w2[:], d["w2"][:, l]).then_inc(on["mlp_weights_loaded"].sem, 16)
                        e.wait_ge(on["mlp_weights_loaded"].sem, on["mlp_weights_loaded"].at(32))

                    @block.gpsimd
                    def _(e):
                        norm_gpsimd(e, 0)

                        def body(n, p, w, p1, w1_):
                            norm_gpsimd(e, n + 1)
                            e.wait_ge(on["centred"].sem, on["centred"].at(n + 1))
                            e.nop(nofuse=True)
                            e.tensor_tensor(group(p, w), group(p, w), row(f"b2{l}"), ALU.add).then_inc(on["mlp_biased"].sem, 1)
                        loop_groups(e, body)

                    @block.vector
                    def _(e):
                        norm_vector(e, group(0, 0), 0, 0)

                        def body(n, p, w, p1, w1_):
                            e.nop(nofuse=True)
                            norm_vector(e, group(p1, w1_), p1, n + 1, freed=(on["transposed"], 2 * n))
                            e.wait_ge(on["mlp_biased"].sem, on["mlp_biased"].at(n + 1))
                            e.wait_ge(on["mlp_ready"].sem, on["mlp_ready"].at(n + 1))
                            e.tensor_tensor(group(p, w), group(p, w), bank[6][0:TP, :].rearrange("t (w c) -> t w c", c=C),
                                                 ALU.add).then_inc(on["residual_added"].sem, 1)
                        loop_groups(e, body)

                    @block.scalar
                    def _(e):
                        norm_scalar(e, 0, 0)

                        def body(n, p, w, p1, w1_):
                            norm_scalar(e, p1, n + 1)
                            for half in range(2):
                                e.wait_ge(on["transposed"].sem, on["transposed"].at(2 * n + half + 1))
                                e.activation(y[:, 4 * half:4 * half + 4].rearrange("c w t -> c (w t)"), bank[half][0:C, 0:HALF],
                                                  ACT.Identity, scale=col(f"n2g{l}"), bias=col(f"n2b{l}")).then_inc(on["evacuated"].sem, 1)
                            for half in range(2):
                                for f in range(2):
                                    e.wait_ge(on["hidden_ready"].sem, on["hidden_ready"].at(4 * n + 2 * half + f + 1))
                                    e.activation(hid[:, f, 4 * half:4 * half + 4].rearrange("c w t -> c (w t)"),
                                                      bank[2 + 2 * half + f][:, 0:HALF], ACT.Gelu, bias=col(f"mb{l}{f}", 0, 128)).then_inc(on["gelu_done"].sem, 1)
                        loop_groups(e, body)

                    @block.tensor
                    def _(e):
                        e.wait_ge(on["mlp_weights_loaded"].sem, on["mlp_weights_loaded"].at(32))

                        def body(n, p, w, p1, w1_):
                            transpose_group(e, p, n)
                            e.wait_ge(on["gelu_done"].sem, on["gelu_done"].at(4 * n))
                            for half in range(2):
                                e.wait_ge(on["evacuated"].sem, on["evacuated"].at(2 * n + half + 1))
                                for f in range(2):
                                    e.matmul(bank[2 + 2 * half + f][:, 0:HALF], w1[:, HID * f:HID * (f + 1)],
                                                  y[:, 4 * half:4 * half + 4].rearrange("c w t -> c (w t)"),
                                                  start=True, stop=True).then_inc(on["hidden_ready"].sem, 1)
                            e.wait_ge(on["residual_added"].sem, on["residual_added"].at(n))
                            for x in range(GW):
                                if x % 4 == 0:
                                    e.wait_ge(on["gelu_done"].sem, on["gelu_done"].at(4 * n + (2 if x == 0 else 4)))
                                for f in range(2):
                                    last = e.matmul(bank[6][0:TP, C * x:C * (x + 1)], hid[:, f, x], w2[:, f],
                                                    start=f == 0, stop=f == 1)
                            last.then_inc(on["mlp_ready"].sem, 1)
                        loop_groups(e, body)
                G = 2 * GROUPS
                norm_ended(G + 1)
                ended(mlp_weights_loaded=32, mlp_biased=G, mlp_ready=G, residual_added=G, transposed=2 * G, evacuated=2 * G,
                      hidden_ready=4 * G, gelu_done=4 * G)

        swin_block(0)
        swin_block(1)
        with ExitStack() as part:
            def psb(name, shape, dt=F32):
                return part.enter_context(nc.sbuf_tensor(name, shape, dt))

            hT = psb("hT", [C + 1, B, N])
            kst = psb("kst", [AK, N])
            khi, klo = psb("khi", [128, N], BF16), psb("klo", [128, N], BF16)
            vst = psb("vst", [TP, KT, C + 1])
            qst = psb("qst", [AK, HALF])
            qsplit = psb("qsplit", [128, HALF], BF16)
            biasT = psb("biasT", [TP, 2352])
            biasQ = psb("biasQ", [TP, 2576])
            biased = psb("biased", [TP, 2, HALF])
            pexp = psb("pexp", [TP, 3, HALF])
            tmx, rmx, nmx = psb("tmx", [TP, 4, QT]), psb("rmx", [TP, 4]), psb("nmx", [TP, 4])
            awk2, awq2 = psb("awk2", [C, 2, C]), psb("awq2", [C, 2, C])
            bias2 = psb("bias2", [128, 2])

            flip = psb("flip", [TP, TP])
            pieces = [(t, slice(i, i + n)) for t, n in ((biasT, 392), (biasQ, 368)) for i in range(0, t.shape[1], n)]

            with nc.Block() as block:
                @block.sync
                def _(e):
                    for w in range(2):
                        e.dma_start(awk2[:, w], d["awk"]).then_inc(on["tables_loaded"].sem, 16)
                        e.dma_start(awq2[:, w], d["awq"]).then_inc(on["tables_loaded"].sem, 16)
                        e.dma_start(bias2[C * w:C * (w + 1)], d["bias2"]).then_inc(on["tables_loaded"].sem, 16)
                    for to, src in ((biasT, d["ext"]), (biasQ, d["extq"])):
                        e.dma_start(to[:], bass.AP(src.tensor, 0, [[1, TP], [1, to.shape[1]]])).then_inc(on["tables_loaded"].sem, 16)
                    e.dma_start(flip[:], d["flip"]).then_inc(on["tables_loaded"].sem, 16)
                    e.wait_ge(on["tables_loaded"].sem, on["tables_loaded"].at(16 * 9))

                @block.gpsimd
                def _(e):
                    for i, (a, v) in enumerate(((kst[C:AK], 0.0), (kst[C:C + 1], 1.0), (qst[C:AK], 0.0),
                                                (vst[:, :, C:], 1.0))):
                        e.memset(a, v).then_inc(on["cleared"].sem, 1)
                        e.wait_ge(on["cleared"].sem, on["cleared"].at(i + 1))
                    norm_gpsimd(e, 0)
                    loop_groups(e, lambda n, p, w, p1, w1: norm_gpsimd(e, n + 1))

                @block.vector
                def _(e):
                    for i, (t, at) in enumerate(pieces):
                        e.wait_ge(on["bias_flipped"].sem, on["bias_flipped"].at(i + 1))
                        e.tensor_scalar(t[:, at], bank[2 + i % 2][0:TP, 0:at.stop - at.start], col("last", 0, TP), None,
                                             ALU.subtract).then_inc(on["bias_set"].sem, 1)
                    norm_vector(e, group(0, 0), 0, 0, weight=1 + EPS, extra=EPS ** 2)

                    def body(n, p, w, p1, w1):
                        e.nop(nofuse=True)
                        norm_vector(e, group(p1, w1), p1, n + 1, freed=(on["transposed"], 2 * n), weight=1 + EPS, extra=EPS ** 2)
                    loop_groups(e, body)
                    e.wait_ge(on["bias_set"].sem, on["bias_set"].at(len(pieces)))

                @block.tensor
                def _(e):
                    e.wait_ge(on["tables_loaded"].sem, on["tables_loaded"].at(16 * 9))
                    for i, (t, at) in enumerate(pieces):
                        e.wait_ge(on["bias_set"].sem, on["bias_set"].at(max(i - 1, 0)))
                        e.matmul(bank[2 + i % 2][0:TP, 0:at.stop - at.start], flip[:], t[:, at], start=True, stop=True).then_inc(on["bias_flipped"].sem, 1)
                    loop_groups(e, lambda n, p, w, p1, w1: transpose_group(e, p, n))

                @block.scalar
                def _(e):
                    norm_scalar(e, 0, 0)

                    def body(n, p, w, p1, w1):
                        norm_scalar(e, p1, n + 1)
                        for half in range(2):
                            e.wait_ge(on["transposed"].sem, on["transposed"].at(2 * n + half + 1))
                            e.nop(nofuse=True)
                            e.activation(hT[0:C, 2 * p:2 * p + 2, :].rearrange("c b (h w) -> c w b h", w=HW)
                                              [:, bass.ds(w + 4 * half, 4)],
                                              bank[half][0:C, 0:HALF].rearrange("c (w b h) -> c w b h", w=4, b=2),
                                              ACT.Identity, scale=col("ag"), bias=col("ab")).then_inc(on["evacuated"].sem, 1)
                    loop_groups(e, body)
            norm_ended(2 * GROUPS + 1)
            ended(transposed=4 * GROUPS, evacuated=4 * GROUPS, tables_loaded=16 * 9, cleared=4, bias_set=len(pieces), bias_flipped=len(pieces))

            S, M, X, O, V = (bank[0], bank[1], bank[2]), (bank[3], bank[4]), bank[5], bank[6], bank[7]

            def loop_tiles(e, image, tile):
                with e.Fori(0, B) as b:
                    image(b)
                    with e.Fori(0, QFLAT) as q:
                        tile(b, q, b * QT + q, (b * QT + q) * KT, False)
                    with e.Fori(QFLAT, QT) as q:
                        tile(b, q, b * QT + q, (b * QT + q) * KT, True)

            with nc.Block() as block:
                @block.gpsimd
                def _(e):
                    with e.Fori(0, B) as b:
                        e.wait_ge(on["attn_weighted"].sem, on["attn_weighted"].at(b * QT * KT))
                        e.nop(nofuse=True)
                        e.tensor_copy(kst[0:C, :], hT[0:C, b, :]).then_inc(on["tokens_staged"].sem, 1)

                @block.tensor
                def _(e):
                    def image(b):
                        e.wait_ge(on["tokens_staged"].sem, on["tokens_staged"].at(b + 1))
                        for g in range(4):
                            e.wait_ge(on["values_evacuated"].sem, on["values_evacuated"].at(4 * b + g))
                            for t in range(7):
                                last = e.matmul(V[0:TP, C * t:C * (t + 1)], kst[0:C + 1, (7 * g + t) * TP:(7 * g + t + 1) * TP],
                                                awv[:], start=True, stop=True)
                            last.then_inc(on["values_ready"].sem, 1)
                        for t in range(QT):
                            e.wait_ge(on["keys_evacuated"].sem, on["keys_evacuated"].at(QT * b + t))
                            e.nop(nofuse=True)
                            e.matmul(X[:, 0:HALF], awk2[:].rearrange("c x k -> c (x k)"),
                                          hT[0:C, b, t * HALF:(t + 1) * HALF], start=True, stop=True).then_inc(on["keys_ready"].sem, 1)

                    def tile(b, q, Q, U, late):
                        e.wait_ge(on["keys_evacuated"].sem, on["keys_evacuated"].at(QT * b + QT))
                        e.wait_ge(on["maximum_set"].sem, on["maximum_set"].at(Q))
                        e.nop(nofuse=True)
                        e.matmul(X[:, 0:HALF], awq2[:].rearrange("c x k -> c (x k)"), hT[0:C, b, bass.ds(q * HALF, HALF)],
                                      start=True, stop=True).then_inc(on["query_ready"].sem, 1)
                        e.wait_ge(on["queries_split"].sem, on["queries_split"].at(Q + 1))
                        for s in range(4):
                            for t in range(QT):
                                e.wait_ge(on["tile_maximum"].sem, on["tile_maximum"].at(U + 7 * s + t + 1))
                                for i, k in enumerate((khi, klo)):
                                    last = e.matmul(M[(7 * s + t) % 2][0:TP, 0:HALF], qsplit[:, TP * s:TP * (s + 1)],
                                                    k[:, t * HALF:(t + 1) * HALF], start=i == 0, stop=i == 1)
                                last.then_inc(on["tile_scored"].sem, 1)
                        e.wait_ge(on["row_maximum"].sem, on["row_maximum"].at(Q + 1))
                        for s in range(4):
                            last = e.matmul(X[C:C + 1, TP * s:TP * (s + 1)], nmx[:, s:s + 1], ident[0:TP, 0:TP],
                                            start=True, stop=True)
                        last.then_inc(on["maximum_moved"].sem, 1)
                        e.wait_ge(on["maximum_set"].sem, on["maximum_set"].at(Q + 1))

                        def scores(t):
                            e.wait_ge(on["attn_exponentials"].sem, on["attn_exponentials"].at(U + t + 1))
                            e.matmul(S[t % 3][0:TP, 0:HALF], kst[:, TP * t:TP * (t + 1)], qst[:], start=True, stop=True).then_inc(on["attn_scored"].sem, 1)
                        scores(0)
                        scores(1)
                        for t in range(KT):
                            if t + 2 < KT:
                                scores(t + 2)
                            e.wait_ge(on["attn_exponentials"].sem, on["attn_exponentials"].at(U + t + 4))
                            if t == 0:
                                e.wait_ge(on["attn_evacuated"].sem, on["attn_evacuated"].at(Q))
                            e.matmul(O[0:C + 1, 0:HALF], vst[:, t], pexp[:, t % 3], start=t == 0, stop=t == KT - 1).then_inc(on["attn_weighted"].sem, 1)
                    loop_tiles(e, image, tile)

                @block.scalar
                def _(e):
                    e.nop(nofuse=True).then_inc(on["attn_exponentials"].sem, 3)

                    def image(b):
                        for g in range(4):
                            e.wait_ge(on["values_ready"].sem, on["values_ready"].at(4 * b + g + 1))
                            e.copy(vst[:, 7 * g:7 * g + 7, 0:C], V[0:TP, 0:7 * C].rearrange("t (x c) -> t x c", c=C)).then_inc(on["values_evacuated"].sem, 1)
                        for t in range(QT):
                            at = slice(t * HALF, (t + 1) * HALF)
                            e.wait_ge(on["keys_ready"].sem, on["keys_ready"].at(QT * b + t + 1))
                            e.activation(khi[:, at], X[:, 0:HALF], ACT.Identity, bias=bias2[:, 0:1])
                            e.activation(kst[0:C, at], X[0:C, 0:HALF], ACT.Identity, bias=bias2[0:C, 0:1]).then_inc(on["keys_rounded"].sem, 1)

                    def tile(b, q, Q, U, late):
                        e.wait_ge(on["query_ready"].sem, on["query_ready"].at(Q + 1))
                        e.activation(qsplit[:], X[:, 0:HALF], ACT.Identity, bias=bias2[:, 1:2])
                        e.activation(qst[0:C, :], X[0:C, 0:HALF], ACT.Identity, bias=bias2[0:C, 1:2]).then_inc(on["query_rounded"].sem, 1)
                        e.wait_ge(on["maximum_moved"].sem, on["maximum_moved"].at(Q + 1))
                        e.copy(qst[C:C + 1, :], X[C:C + 1, 0:HALF]).then_inc(on["maximum_set"].sem, 1)
                        for t in range(KT):
                            if late and t < KBIAS:
                                e.wait_ge(on["scores_biased"].sem, on["scores_biased"].at((b * (QT - QFLAT) + q - QFLAT) * KBIAS + t + 1))
                                x = biased[:, t % 2]
                            else:
                                e.wait_ge(on["attn_scored"].sem, on["attn_scored"].at(U + t + 1))
                                x = S[t % 3][0:TP, 0:HALF]
                            e.activation(pexp[:, t % 3], x, ACT.Exp).then_inc(on["attn_exponentials"].sem, 1)
                        e.wait_ge(on["attn_weighted"].sem, on["attn_weighted"].at(U + KT))
                        e.nop(nofuse=True)
                        e.copy(hT[:, b, bass.ds(q * HALF, HALF)], O[0:C + 1, 0:HALF]).then_inc(on["attn_evacuated"].sem, 1)
                    loop_tiles(e, image, tile)

                @block.vector
                def _(e):
                    e.nop(nofuse=True).then_inc(on["tile_maximum"].sem, 2)

                    def image(b):
                        for t in range(QT):
                            at = slice(t * HALF, (t + 1) * HALF)
                            e.wait_ge(on["keys_rounded"].sem, on["keys_rounded"].at(QT * b + t + 1))
                            e.scalar_tensor_tensor(klo[:, at], X[:, 0:HALF], bias2[:, 0:1], khi[:, at], ALU.add, ALU.subtract).then_inc(on["keys_evacuated"].sem, 1)

                    def tile(b, q, Q, U, late):
                        e.wait_ge(on["query_rounded"].sem, on["query_rounded"].at(Q + 1))
                        e.scalar_tensor_tensor(qsplit[C:, :], X[C:, 0:HALF], bias2[C:, 1:2], qsplit[C:, :],
                                                    ALU.add, ALU.subtract).then_inc(on["queries_split"].sem, 1)
                        late_tile = (b * (QT - QFLAT) + q - QFLAT) if late else None
                        for s in range(4):
                            for t in range(QT):
                                e.wait_ge(on["tile_scored"].sem, on["tile_scored"].at(U + 7 * s + t + 1))
                                x = M[(7 * s + t) % 2][0:TP, 0:HALF]
                                if late and t < 3:
                                    e.nop(nofuse=True)
                                    e.tensor_tensor(biased[:, t % 2], x,
                                                         biasQ[:, bass.ds(TP * (KT - 1) - HALF * q - TP * s + HALF * t, HALF)],
                                                         ALU.add).then_inc(on["tile_biased"].sem, 1)
                                    e.wait_ge(on["tile_biased"].sem, on["tile_biased"].at(late_tile * 12 + 3 * s + t + 1))
                                    x = biased[:, t % 2]
                                e.tensor_reduce(out=tmx[:, s, t:t + 1], in_=x, axis=AX, op=ALU.max).then_inc(on["tile_maximum"].sem, 1)
                        e.wait_ge(on["tile_maximum"].sem, on["tile_maximum"].at(U + KT + 2))
                        e.tensor_reduce(out=rmx[:], in_=tmx[:], axis=AX, op=ALU.max).then_inc(on["maxima_ready"].sem, 1)
                        e.wait_ge(on["maxima_ready"].sem, on["maxima_ready"].at(Q + 1))
                        e.tensor_scalar(nmx[:], rmx[:], -1.0, None, ALU.mult).then_inc(on["row_maximum"].sem, 1)
                        if late:
                            for t in range(KBIAS):
                                e.wait_ge(on["attn_scored"].sem, on["attn_scored"].at(U + t + 1))
                                e.wait_ge(on["attn_exponentials"].sem, on["attn_exponentials"].at(U + t + 1 + 1))
                                e.nop(nofuse=True)
                                e.tensor_tensor(biased[:, t % 2], S[t % 3][0:TP, 0:HALF],
                                                     biasT[:, bass.ds(HALF * q - TP * t - 784, HALF)], ALU.add).then_inc(on["scores_biased"].sem, 1)
                    loop_tiles(e, image, tile)
            u = B * QT * KT
            late = B * (QT - QFLAT)
            ended(tokens_staged=B, values_ready=4 * B, values_evacuated=4 * B, keys_ready=QT * B, keys_evacuated=QT * B,
                  keys_rounded=QT * B, query_ready=QT * B, query_rounded=QT * B, queries_split=QT * B, tile_scored=u,
                  tile_maximum=u + 2, tile_biased=12 * late, maxima_ready=QT * B, row_maximum=QT * B, maximum_moved=QT * B,
                  maximum_set=QT * B, attn_scored=u, attn_exponentials=u + 3, attn_weighted=u, attn_evacuated=QT * B,
                  scores_biased=KBIAS * late)

            ost = psb("attn_ost", [C + 1, 2, GW, TP])
            raw = psb("attn_raw", [TP, 2, GW, C])
            rd = psb("attn_rd", [TP, 2, GW])
            gained = psb("attn_gained", [TP, GW, C])
            with nc.Block() as block:
                @block.gpsimd
                def _(e):
                    def stage(n, p, w):
                        e.wait_ge(on["projected"].sem, on["projected"].at(n))
                        e.nop(nofuse=True)
                        e.tensor_copy(ost[:, p].rearrange("c w (b h) -> c w b h", b=2),
                                           hT[:, 2 * p:2 * p + 2, :].rearrange("c b (h w) -> c w b h", w=HW)[:, bass.ds(w, GW)]).then_inc(on["outputs_staged"].sem, 1)

                    def body(n, p, w, p1, w1):
                        stage(n, p, w)
                        norm_gpsimd(e, n)
                        e.wait_ge(on["normalised"].sem, on["normalised"].at(n + 1))
                        e.tensor_tensor(gained[:], cent[:, p], row("a2g"), ALU.mult).then_inc(on["gain_applied"].sem, 1)
                        e.wait_ge(on["gain_applied"].sem, on["gain_applied"].at(n + 1))
                        e.tensor_tensor(raw[:, p], gained[:], row("a2b"), ALU.add).then_inc(on["output_ready"].sem, 1)
                        e.wait_ge(on["output_ready"].sem, on["output_ready"].at(n + 1))
                        e.nop(nofuse=True)
                        e.tensor_tensor(group(p, w), group(p, w), raw[:, p], ALU.add).then_inc(on["residual_added"].sem, 1)
                    loop_groups(e, body)

                @block.tensor
                def _(e):
                    def body(n, p, w, p1, w1):
                        e.wait_ge(on["outputs_staged"].sem, on["outputs_staged"].at(n + 1))
                        e.wait_ge(on["outputs_normalised"].sem, on["outputs_normalised"].at(2 * n))
                        for x in range(GW):
                            last = e.matmul(bank[x // 4][0:TP, (C + 1) * (x % 4):(C + 1) * (x % 4 + 1)], ost[:, p, x], awp[:],
                                            start=True, stop=True)
                        last.then_inc(on["projected"].sem, 1)
                    loop_groups(e, body)

                @block.scalar
                def _(e):
                    loop_groups(e, lambda n, p, w, p1, w1: norm_scalar(e, p, n))

                @block.vector
                def _(e):
                    def body(n, p, w, p1, w1):
                        e.wait_ge(on["projected"].sem, on["projected"].at(n + 1))
                        for h in range(2):
                            x = bank[h][0:TP, 0:4 * (C + 1)].rearrange("t (w c) -> t w c", c=C + 1)
                            e.reciprocal(rd[:, 0, 4 * h:4 * h + 4], x[:, :, C]).then_inc(on["denominators_read"].sem, 1)
                            e.wait_ge(on["denominators_read"].sem, on["denominators_read"].at(2 * n + h + 1))
                            e.tensor_scalar(rd[:, 1, 4 * h:4 * h + 4], rd[:, 0, 4 * h:4 * h + 4], col("scale", 0, TP), None,
                                                 ALU.mult).then_inc(on["weights_scaled"].sem, 1)
                            e.wait_ge(on["weights_scaled"].sem, on["weights_scaled"].at(2 * n + h + 1))
                            e.tensor_tensor(raw[:, p, 4 * h:4 * h + 4], x[:, :, 0:C],
                                                 rd[:, 1, 4 * h:4 * h + 4].unsqueeze(2).broadcast_to([TP, 4, C]), ALU.mult).then_inc(on["outputs_normalised"].sem, 1)
                        e.wait_ge(on["outputs_normalised"].sem, on["outputs_normalised"].at(2 * n + 2))
                        e.tensor_tensor(raw[:, p], raw[:, p], row("apb"), ALU.add).then_inc(on["projection_biased"].sem, 1)
                        e.wait_ge(on["projection_biased"].sem, on["projection_biased"].at(n + 1))
                        norm_vector(e, raw[:, p], p, n, freed=(on["residual_added"], n))
                    loop_groups(e, body)
            G = 2 * GROUPS
            norm_ended(G)
            ended(outputs_staged=G, gain_applied=G, output_ready=G, residual_added=G, projected=G, denominators_read=2 * G,
                  weights_scaled=2 * G, outputs_normalised=2 * G, projection_biased=G)

        with ExitStack() as part:
            def psb(name, shape, dt=F32):
                return part.enter_context(nc.sbuf_tensor(name, shape, dt))

            wr, ew1, ew2 = psb("wr", [C + 1, E]), psb("ew1", [C, E, HID]), psb("ew2", [HID, E, C])
            eb2, number = psb("eb2", [TP, E * C]), psb("number", [TP, E])
            xn = psb("xn", [C + 1, GW, TP])
            hid = psb("ehid", [HID, 2, E, HALF])
            lg, top = psb("lg", [TP, GW, E]), psb("top", [TP, GW, E])
            at = psb("at", [TP, GW, E], U32)
            atf = psb("atf", [TP, GW, 2])
            lead, tanh = psb("lead", [TP, GW]), psb("tanh", [TP, GW])
            share = psb("share", [TP, 2, GW])
            one = psb("one", [TP, 2, GW, E])
            gate = psb("gate", [TP, 2, GW, E])
            yb, yw = psb("yb", [TP, 2, E * C]), psb("yw", [TP, 2, E * C])
            mix = psb("mix", [TP, GW, C])
            STEPS = 8

            with nc.Block() as block:
                @block.sync
                def _(e):
                    for to, src in ((wr, d["wr"]), (ew1, d["ew1"]), (ew2, d["ew2"]),
                                    (eb2, d["eb2"].rearrange("e c -> (e c)").unsqueeze(0).broadcast_to([TP, E * C])),
                                    (number, d["number"].unsqueeze(0).broadcast_to([TP, E]))):
                        e.dma_start(to[:], src).then_inc(on["tables_loaded"].sem, 16)
                    e.wait_ge(on["tables_loaded"].sem, on["tables_loaded"].at(16 * 5))

                @block.gpsimd
                def _(e):
                    e.memset(xn[C:C + 1], 1.0).then_inc(on["ones_set"].sem, 1)
                    e.wait_ge(on["ones_set"].sem, on["ones_set"].at(1))
                    norm_gpsimd(e, 0)

                    def body(n, p, w, p1, w1):
                        norm_gpsimd(e, n + 1)
                        for x in range(GW):
                            e.wait_ge(on["expert_biased"].sem, on["expert_biased"].at(GW * n + x + 1))
                            e.wait_ge(on["mixed"].sem, on["mixed"].at(GW * n + x))
                            e.tensor_tensor(yw[:, x % 2].rearrange("t (e c) -> t e c", e=E),
                                                 yb[:, x % 2].rearrange("t (e c) -> t e c", e=E),
                                                 gate[:, p, x].unsqueeze(2).broadcast_to([TP, E, C]), ALU.mult).then_inc(on["expert_weighted"].sem, 1)
                    loop_groups(e, body)

                @block.vector
                def _(e):
                    norm_vector(e, group(0, 0), 0, 0, weight=1 + EPS, extra=EPS ** 2)
                    e.wait_ge(on["tables_loaded"].sem, on["tables_loaded"].at(16 * 5))

                    def body(n, p, w, p1, w1):
                        e.nop(nofuse=True)
                        norm_vector(e, group(p1, w1), p1, n + 1, freed=(on["transposed"], 2 * n), weight=1 + EPS, extra=EPS ** 2)
                        step = STEPS * n
                        e.wait_ge(on["gate_scored"].sem, on["gate_scored"].at(n + 1))
                        e.tensor_copy(lg[:].rearrange("t w e -> t (w e)"), bank[2][0:TP, 0:GW * E]).then_inc(on["gate_step"].sem, 1)
                        e.wait_ge(on["gate_step"].sem, on["gate_step"].at(step + 1))
                        e.nop(nofuse=True)
                        for x in range(GW):
                            last = e.max(top[:, x], lg[:, x])
                        last.then_inc(on["gate_step"].sem, 1)
                        e.wait_ge(on["gate_step"].sem, on["gate_step"].at(step + 2))
                        e.tensor_tensor(lead[:], top[:, :, 0], top[:, :, 1], ALU.subtract).then_inc(on["lead_ready"].sem, 1)
                        for x in range(GW):
                            last = e.max_index(at[:, x], top[:, x], lg[:, x])
                        last.then_inc(on["gate_step"].sem, 1)
                        e.wait_ge(on["gate_step"].sem, on["gate_step"].at(step + 3))
                        e.tensor_copy(atf[:], at[:, :, 0:2]).then_inc(on["gate_step"].sem, 1)
                        e.wait_ge(on["gate_step"].sem, on["gate_step"].at(step + 4))
                        e.wait_ge(on["tanh_ready"].sem, on["tanh_ready"].at(n + 1))
                        for i in range(2):
                            last = e.tensor_scalar(share[:, i], tanh[:], 0.5 - i, 0.5, ALU.mult, ALU.add)
                        last.then_inc(on["gate_step"].sem, 1)
                        for i in range(2):
                            last = e.tensor_tensor(one[:, i], number[:].unsqueeze(1).broadcast_to([TP, GW, E]),
                                                   atf[:, :, i].unsqueeze(2).broadcast_to([TP, GW, E]), ALU.is_equal)
                        last.then_inc(on["gate_step"].sem, 1)
                        e.wait_ge(on["gate_step"].sem, on["gate_step"].at(step + 6))
                        for i in range(2):
                            last = e.tensor_tensor(one[:, i], one[:, i], share[:, i].unsqueeze(2).broadcast_to([TP, GW, E]), ALU.mult)
                        last.then_inc(on["gate_step"].sem, 1)
                        e.wait_ge(on["gate_step"].sem, on["gate_step"].at(step + 7))
                        e.tensor_tensor(gate[:, p], one[:, 0], one[:, 1], ALU.add).then_inc(on["gate_step"].sem, 1)
                        e.wait_ge(on["gate_step"].sem, on["gate_step"].at(step + 8))

                        def bias(x):
                            e.wait_ge(on["experts_done"].sem, on["experts_done"].at(GW * n + x + 1))
                            e.tensor_tensor(yb[:, x % 2], bank[6 + x % 2][0:TP, :], eb2[:], ALU.add).then_inc(on["expert_biased"].sem, 1)
                        bias(0)
                        for x in range(GW):
                            if x + 1 < GW:
                                bias(x + 1)
                            e.wait_ge(on["expert_weighted"].sem, on["expert_weighted"].at(GW * n + x + 1))
                            e.tensor_reduce(out=mix[:, x], in_=yw[:, x % 2].rearrange("t (e c) -> t c e", e=E), axis=AX,
                                                 op=ALU.add).then_inc(on["mixed"].sem, 1)
                        e.wait_ge(on["mixed"].sem, on["mixed"].at(GW * n + GW))
                        e.nop(nofuse=True)
                        e.tensor_tensor(group(p, w), group(p, w), mix[:], ALU.add).then_inc(on["residual_added"].sem, 1)
                    loop_groups(e, body)

                @block.scalar
                def _(e):
                    e.nop(nofuse=True).then_inc(on["expert_gelu"].sem, 3)
                    norm_scalar(e, 0, 0)

                    def body(n, p, w, p1, w1):
                        norm_scalar(e, p1, n + 1)
                        for half in range(2):
                            e.wait_ge(on["transposed"].sem, on["transposed"].at(2 * n + half + 1))
                            e.activation(xn[0:C, 4 * half:4 * half + 4].rearrange("c w t -> c (w t)"), bank[half][0:C, 0:HALF],
                                              ACT.Identity, scale=col("fg"), bias=col("fb")).then_inc(on["evacuated"].sem, 1)
                        e.wait_ge(on["lead_ready"].sem, on["lead_ready"].at(n + 1))
                        e.activation(tanh[:], lead[:], ACT.Tanh, scale=0.5).then_inc(on["tanh_ready"].sem, 1)
                        for half in range(2):
                            for x in range(E):
                                i = E * half + x
                                e.wait_ge(on["expert_hidden"].sem, on["expert_hidden"].at(2 * E * n + i + 1))
                                e.activation(hid[:, half, x], bank[3 + x % 3][:, 0:HALF], ACT.Gelu,
                                                  bias=col(f"eb{x}", 0, 128)).then_inc(on["expert_gelu"].sem, 1)
                    loop_groups(e, body)

                @block.tensor
                def _(e):
                    e.wait_ge(on["tables_loaded"].sem, on["tables_loaded"].at(16 * 5))
                    e.wait_ge(on["ones_set"].sem, on["ones_set"].at(1))

                    def body(n, p, w, p1, w1):
                        transpose_group(e, p, n)
                        e.wait_ge(on["evacuated"].sem, on["evacuated"].at(2 * n + 2))
                        e.wait_ge(on["lead_ready"].sem, on["lead_ready"].at(n))
                        for x in range(GW):
                            last = e.matmul(bank[2][0:TP, E * x:E * (x + 1)], xn[:, x], wr[:], start=True, stop=True)
                        last.then_inc(on["gate_scored"].sem, 1)
                        for half in range(2):
                            for x in range(E):
                                i = 2 * E * n + E * half + x
                                e.wait_ge(on["expert_gelu"].sem, on["expert_gelu"].at(i + (1 if x > 2 else 3)))
                                e.matmul(bank[3 + x % 3][:, 0:HALF], ew1[:, x],
                                              xn[0:C, 4 * half:4 * half + 4].rearrange("c w t -> c (w t)"),
                                              start=True, stop=True).then_inc(on["expert_hidden"].sem, 1)
                        for x in range(GW):
                            if x % 4 == 0:
                                e.wait_ge(on["expert_gelu"].sem, on["expert_gelu"].at(2 * E * n + E * (x // 4 + 1) + 3))
                            e.wait_ge(on["expert_biased"].sem, on["expert_biased"].at(GW * n + x))
                            for f in range(E):
                                last = e.matmul(bank[6 + x % 2][0:TP, C * f:C * (f + 1)], hid[:, x // 4, f, TP * (x % 4):TP * (x % 4 + 1)],
                                                ew2[:, f], start=True, stop=True)
                            last.then_inc(on["experts_done"].sem, 1)
                    loop_groups(e, body)
            G = 2 * GROUPS
            norm_ended(G + 1)
            ended(tables_loaded=16 * 5, ones_set=1, transposed=2 * G, evacuated=2 * G)

        with nc.Block() as block:
            @block.sync
            def _(e):
                for p in range(PAIRS):
                    for b in range(2):
                        e.dma_start(out[2 * p + b].rearrange("(h w) c -> h w c", w=HW),
                                         xr[HW * b:HW * (b + 1), p * HW:(p + 1) * HW, :]).then_inc(on["stored"].sem, 16)
                e.wait_ge(on["stored"].sem, on["stored"].at(16 * B))


def layouts(i):
    import numpy as np
    t = {k: np.asarray(v) for k, v in i.items()}
    T = lambda k: t["L0_tok_" + k]
    A = lambda k: t["L0_attn_" + k]
    FF = lambda k: t["L0_ffn_" + k]
    f = np.float32
    vec = {"ag": A("ln1_g"), "ab": A("ln1_b"),
           "fg": FF("gamma"), "fb": FF("beta"),
           "scale": np.broadcast_to(A("scale").reshape(1), (128,)),
           "last": np.broadcast_to(A("bias_table")[-1:], (128,))}
    for l in range(BLOCKS):
        vec |= {f"n1g{l}": T("n1g")[l], f"n1b{l}": T("n1b")[l], f"n2g{l}": T("n2g")[l], f"n2b{l}": T("n2b")[l],
                f"qb{l}": T("qkv_b")[l, 0:C], f"kb{l}": T("qkv_b")[l, C:2 * C]}
        for q in range(2):
            vec[f"mb{l}{q}"] = T("b1")[l, 128 * q:128 * (q + 1)]
    for q in range(E):
        vec[f"eb{q}"] = FF("b1")[q]
    cols = np.zeros((128, len(COLS)), f)
    for n, k in enumerate(COLS):
        cols[:len(vec[k]), n] = vec[k]
    rows = np.stack([T("pe_b"), T("pe_ng"), T("pe_nb"), T("b2")[0], T("b2")[1], A("proj_b"), A("ln2_g"), A("ln2_b")])
    pew = np.zeros((GW, 16, GW, C), f)
    for w in range(GW):
        pew[w, :, w, :] = T("pe_w").reshape(C, 16).T
    wv = np.concatenate([T("qkv_w")[:, 2 * C:].transpose(2, 0, 1), T("qkv_b")[:, 2 * C:][None]], 0)
    pw = np.zeros((HP, 32, BLOCKS, C), f)
    pw[:, 0:16] = T("proj_w").transpose(2, 0, 1).reshape(HP, 16, BLOCKS, C)
    pw[0, 16] = T("proj_b")
    c, r = np.divmod(np.arange(WN), WS)
    rel = (r[:, None] - r[None, :] + WS - 1) * (2 * WS - 1) + c[:, None] - c[None, :] + WS - 1
    edge = lambda x: (x >= WS - SHIFT).astype(int)
    masks = np.stack([np.where(g[:, None] != g[None, :], f(-100), f(0))
                      for g in (edge(r), edge(c), 2 * edge(r) + edge(c))], 1)
    sel = np.zeros((128, 128), f)
    for q in range(128):
        hp, j = divmod(q, 32)
        sel[32 * hp + (17 if 8 <= j < 16 or j == 17 else 16), q] = 1
    heads = np.zeros((C, NH), f)
    vmask = np.zeros((128, 16), f)
    for h in range(NH):
        heads[HD * h:HD * (h + 1), h] = 1
    vmask[0:64, 0:8] = 1
    vmask[64:128, 8:16] = 1
    awp = np.zeros((C + 1, C + 1), f)
    awp[0:C, 0:C], awp[C, C] = A("proj_w"), 1
    table = A("bias_table")
    ext = table[TAB - 1 - np.clip(np.arange(2352 + TP) - 1440, 0, TAB - 1)]
    extq = table[np.clip(np.arange(2576 + TP), 0, TAB - 1)]
    x = {"cols": cols, "rows": rows, "ident": np.eye(128, dtype=f), "pew": pew.reshape(128, GW * C),
         "wqk": T("qkv_w")[:, 0:2 * C].transpose(2, 0, 1), "wv": wv, "pw": pw.reshape(128, BLOCKS, C),
         "w1": T("w1").transpose(2, 0, 1), "w2": T("w2").transpose(2, 0, 1).reshape(2, 128, BLOCKS, C).transpose(1, 2, 0, 3),
         "awq": A("qkv_w")[:, 0:C], "awk": A("qkv_w")[:, C:2 * C],
         "awv": np.concatenate([A("qkv_w")[:, 2 * C:], A("qkv_b")[2 * C:][None]], 0), "awp": awp,
         "rpb": T("rpb")[:, rel].transpose(1, 0, 3, 2), "masks": masks, "sel": sel, "heads": heads, "vmask": vmask,
         "wr": np.concatenate([FF("Wr"), FF("br")[None]], 0), "ew1": FF("W1").transpose(1, 0, 2),
         "ew2": FF("W2").transpose(1, 0, 2), "eb2": FF("b2"),
         "ext": ext, "flip": np.eye(TP, dtype=f)[::-1], "bias2": np.stack([A("qkv_b")[C:2 * C], A("qkv_b")[0:C]], 1), "extq": extq, "number": np.arange(E, dtype=f)}
    return x


def kernel(**inputs):
    import numpy as np
    import concourse.bacc as bacc
    from concourse.bass_utils import run_bass_kernel_spmd as run

    nc = bacc.Bacc("TRN2", target_bir_lowering=False, num_devices=1)
    arrays = {f"in_{k}": np.ascontiguousarray(v) for k, v in layouts(inputs).items()}
    arrays["in_x"] = np.ascontiguousarray(inputs["x"])
    dram = {k: nc.dram_tensor(k, v.shape, mybir.dt.from_np(v.dtype), kind="ExternalInput").ap() for k, v in arrays.items()}
    out = nc.dram_tensor("out", (B, N, C), F32, kind="ExternalOutput").ap()
    build(nc, dram["in_x"], out, {k[3:]: v for k, v in dram.items()})
    return run(nc, [arrays], core_ids=[0]).results[0]["out"]
```

```python
import concourse.bass as bass
from concourse import mybir
from contextlib import ExitStack

F32 = mybir.dt.float32
BF16 = mybir.dt.bfloat16
U32 = mybir.dt.uint32
ALU = mybir.AluOpType
ACT = mybir.ActivationFunctionType
AX = mybir.AxisListType.X

B, HW, C = 4, 56, 64
PAIRS = B // 2
TP = 2 * HW
GW = 8
GROUPS = HW // GW
HALF = GW // 2 * TP
WS, NH, HD = 7, 8, 8
WN = WS * WS
NW = HW // WS
SHIFT = WS // 2
SCALE = HD ** -0.5
SLOT = 64
YW, YH = 66, 59
HP = NH // 2
N = HW * HW
KT = N // TP
QT = N // HALF
QFLAT = 4
KBIAS = 10
TAB = 1023
AK = 96
E, HID = 8, 128
EPS = 1e-5
BLOCKS = 2

COLS = (["n1g0", "n1b0", "n1g1", "n1b1", "n2g0", "n2b0", "n2g1", "n2b1", "qb0", "kb0", "qb1", "kb1",
         "ag", "ab", "fg", "fb", "scale", "last", "b20", "b21"]
        + [f"mb{l}{f}" for l in range(2) for f in range(2)] + [f"eb{e}" for e in range(E)])
ROWS = ["peb", "peg", "pen", "apb", "a2g", "a2b"]

LOADS = {
    "denominators_stored": "a query tile's denominators are in DRAM",
    "image_loaded": "pixels and the embedding's weights",
    "constants_loaded": "constants",
    "tables_loaded": "a stage's tables",
    "mlp_weights_loaded": "the MLP's weights",
    "stored": "the result is in DRAM",
}
SIGNALS = {
    "summed_vector": "VectorE: an even key tile's exponentials are added up",
    "summed_gpsimd": "GpSimd: an odd key tile's exponentials are added up",
    "row_free": "SyncE: the row of denominators is in DRAM",
    "query_set": "VectorE: the next query tile is in the products' buffer",
    "attn_evacuated": "ScalarE: a query tile's outputs and denominators are in SBUF",
    "attn_exponentials": "ScalarE: a key tile's exponentials are in SBUF",
    "attn_scored": "TensorE: a key tile's scores less the maxima",
    "attn_weighted": "TensorE: a key tile's values are added to the outputs",
    "bias_flipped": "TensorE: a piece of the Toeplitz bias is turned round",
    "bias_set": "VectorE: bias rows or pieces are in place",
    "centred": "VectorE: a group less its means",
    "cleared": "GpSimd: padding and fixed rows are set",
    "conv_biased": "VectorE: a group's patch embedding is in the residual stream, before its norm",
    "convolved": "TensorE: a group's patch embedding",
    "denominators_read": "VectorE: reciprocals of the denominators",
    "denominators_ready": "TensorE: the denominators on their heads' partitions",
    "embedded": "GpSimd: a group's normalised embedding is in the residual stream",
    "evacuated": "ScalarE: a channel-major half group with its gain and bias",
    "expert_gelu": "ScalarE: an expert's hidden activations",
    "expert_hidden": "TensorE: an expert's hidden layer",
    "expert_weighted": "VectorE: a column's expert outputs times their gates",
    "experts_done": "TensorE: a column's expert outputs",
    "exponentials_ready": "ScalarE: a pair of windows' exponentials",
    "gain_applied": "GpSimd: a group times its gain",
    "gate_scored": "TensorE: a group's router logits",
    "gate_step": "VectorE: a step of the gating",
    "gelu_done": "ScalarE: half of the hidden activations of a half group",
    "hidden_ready": "TensorE: half of the hidden layer of a half group",
    "keys_by_head": "GpSimd: a chunk's keys, block-diagonal by head",
    "keys_evacuated": "the keys have left PSUM",
    "keys_ready": "TensorE: a tile of keys",
    "keys_rounded": "ScalarE: a key tile's high part, and the tile itself",
    "lead_ready": "VectorE: the first logit less the second",
    "maxima_ready": "VectorE: maxima of rows of scores",
    "maximum_moved": "TensorE: the maxima as a row",
    "maximum_set": "ScalarE: that row is below the queries",
    "mean_ready": "VectorE: a group's means",
    "mixed": "VectorE: a column's sum over experts",
    "mlp_ready": "TensorE: a group's MLP output",
    "normalised": "VectorE: a group's normalised tokens",
    "ones_set": "GpSimd: rows and columns of ones",
    "output_ready": "GpSimd: a group of the attention's output with gain and bias",
    "outputs_evacuated": "ScalarE: a chunk's outputs are in SBUF",
    "outputs_normalised": "VectorE: outputs over their denominators",
    "outputs_ready": "TensorE: a chunk's outputs",
    "outputs_staged": "GpSimd: a group's outputs are in the projection's buffer",
    "patchT_ready": "VectorE: transposed patches are in SBUF",
    "patches_ready": "VectorE: a group's pixels by patch",
    "patches_transposed": "TensorE: a group's patches, transposed",
    "probs_evacuated": "ScalarE: transposed exponentials are in SBUF",
    "probs_transposed": "TensorE: exponentials, transposed",
    "projected": "TensorE: a group's projection",
    "projection_biased": "VectorE: a group's projection with its bias",
    "qbias_ready": "VectorE: the scaled query biases",
    "qk_ready": "TensorE: a chunk's queries and keys",
    "queries_evacuated": "ScalarE: a chunk's queries are in SBUF",
    "queries_split": "VectorE: a query tile's low part",
    "query_ready": "TensorE: a query tile",
    "query_rounded": "ScalarE: a query tile's high part, and the tile itself",
    "residual_added": "a group of the residual stream is up to date",
    "row_maximum": "VectorE: minus the maxima of a query tile",
    "rstd_ready": "GpSimd: a group's reciprocal standard deviations",
    "scores_biased": "VectorE: a key tile's scores with varying bias",
    "scores_ready": "TensorE: a pair of windows' scores",
    "shifted": "VectorE: a pair of windows' scores less their maxima",
    "squared": "ScalarE or GpSimd: squares of a centred group",
    "squares_summed": "VectorE: their sums",
    "summed": "VectorE: a group's sums",
    "tanh_ready": "ScalarE: tanh of half the lead",
    "tile_biased": "VectorE: a score tile with varying bias, for the maximum",
    "tile_maximum": "VectorE: a score tile's row maxima",
    "tile_scored": "TensorE: a score tile for the maximum",
    "tokens_staged": "VectorE: an image's tokens are in the fixed buffer",
    "transposed": "TensorE: a half group, transposed",
    "values_by_head": "VectorE: a chunk's values, block-diagonal by head",
    "values_evacuated": "ScalarE: seven tiles of values are in SBUF",
    "values_ready": "TensorE: values",
    "variance_ready": "VectorE: a group's variances with epsilon",
    "weights_scaled": "VectorE: reciprocals times the attention's scale",
    "windows_staged": "GpSimd: a chunk's windows are in the fixed buffer",
    "wrapped": "GpSimd: copies at the image's seam",
}



def build(nc, img, out, d):
    d["dens"] = nc.dram_tensor("dens", (B * N,), F32).ap()
    ctx = ExitStack()
    with ctx:
        def sb(name, shape, dt=F32):
            return ctx.enter_context(nc.sbuf_tensor(name, shape, dt))

        class Signal:
            def __init__(self, name):
                self.sem, self.past = ctx.enter_context(nc.semaphore(name)), int(name in SIGNALS)

            def at(self, n):
                return n + self.past

        on = {name: Signal(name) for name in (*LOADS, *SIGNALS)}

        def ended(**counts):
            for name, n in counts.items():
                on[name].past += n

        with nc.Block() as block:
            @block.sync
            def _(e):
                for name in SIGNALS:
                    e.nop(nofuse=True).then_inc(on[name].sem, 1)

        xr = sb("xr", [TP, PAIRS * HW + GW, C])
        ident = sb("ident", [128, 128])
        cols = sb("cols_sb", [128, len(COLS)])
        rows = sb("rows_sb", [TP, len(ROWS), C])
        neghalf = sb("neghalf", [TP, GW])
        cent = sb("cent", [TP, 2, GW, C])
        normed = sb("normed", [TP, 2, GW, C])
        sq = sb("sq", [TP, GW, C])
        stat = sb("stat", [TP, 5, GW])
        bank = [ctx.enter_context(nc.psum_tensor(f"bank{i}", [128, 512], F32)) for i in range(8)]

        def col(name, p0=0, p1=C):
            return cols[p0:p1, COLS.index(name):COLS.index(name) + 1]

        def row(name, n=GW):
            return rows[:, ROWS.index(name), :].unsqueeze(1).broadcast_to([TP, n, C])

        def group(p, w):
            return xr[:, bass.ds(p * HW + w, GW), :]

        def per_token(ap):
            return ap.unsqueeze(2).broadcast_to([TP, GW, C])

        def norm_centre(e, x, k, n):
            e.tensor_reduce(out=stat[:, 0, :], in_=x, axis=AX, op=ALU.add).then_inc(on["summed"].sem, 1)
            e.wait_ge(on["summed"].sem, on["summed"].at(n + 1))
            e.tensor_scalar(stat[:, 1, :], stat[:, 0, :], 1.0 / C, None, ALU.mult).then_inc(on["mean_ready"].sem, 1)
            e.wait_ge(on["mean_ready"].sem, on["mean_ready"].at(n + 1))
            e.tensor_tensor(cent[:, k], x, per_token(stat[:, 1, :]), ALU.subtract).then_inc(on["centred"].sem, 1)

        def norm_variance(e, n, weight=1.0, extra=EPS):
            e.wait_ge(on["squared"].sem, on["squared"].at(n + 1))
            e.tensor_reduce(out=stat[:, 2, :], in_=sq[:], axis=AX, op=ALU.add).then_inc(on["squares_summed"].sem, 1)
            e.wait_ge(on["squares_summed"].sem, on["squares_summed"].at(n + 1))
            e.tensor_scalar(stat[:, 3, :], stat[:, 2, :], weight / C, extra, ALU.mult, ALU.add).then_inc(on["variance_ready"].sem, 1)

        def norm_scale(e, k, n, freed=None):
            e.wait_ge(on["rstd_ready"].sem, on["rstd_ready"].at(n + 1))
            if freed:
                e.wait_ge(freed[0].sem, freed[0].at(freed[1]))
            e.tensor_tensor(normed[:, k], cent[:, k], per_token(stat[:, 4, :]), ALU.mult).then_inc(on["normalised"].sem, 1)

        def norm_vector(e, x, k, n, freed=None, weight=1.0, extra=EPS):
            norm_centre(e, x, k, n)
            norm_variance(e, n, weight, extra)
            norm_scale(e, k, n, freed)

        def norm_scalar(e, k, n):
            e.wait_ge(on["centred"].sem, on["centred"].at(n + 1))
            e.activation(sq[:], cent[:, k], ACT.Square).then_inc(on["squared"].sem, 1)

        def norm_squares(e, k, n):
            e.wait_ge(on["centred"].sem, on["centred"].at(n + 1))
            e.tensor_tensor(sq[:], cent[:, k], cent[:, k], ALU.mult).then_inc(on["squared"].sem, 1)

        def norm_gpsimd(e, n):
            e.wait_ge(on["variance_ready"].sem, on["variance_ready"].at(n + 1))
            e.tensor_tensor(stat[:, 4, :], stat[:, 3, :], neghalf[:], ALU.pow).then_inc(on["rstd_ready"].sem, 1)

        def norm_ended(n, centred):
            ended(summed=centred, mean_ready=centred, centred=centred, squared=centred, squares_summed=n, variance_ready=n,
                  rstd_ready=n, normalised=n)

        def transpose_group(e, k, n):
            e.wait_ge(on["normalised"].sem, on["normalised"].at(n + 1))
            e.wait_ge(on["evacuated"].sem, on["evacuated"].at(2 * n))
            e.nop(nofuse=True)
            for half in range(2):
                for w in range(4):
                    last = e.transpose(bank[half][0:C, w * TP:(w + 1) * TP], normed[:, k, half * 4 + w, :],
                                       ident[0:TP, 0:TP])
                last.then_inc(on["transposed"].sem, 1)

        def loop_groups(e, body):
            with e.Fori(0, GROUPS) as j:
                body(2 * j, 0, GW * j, 1, GW * j)
                body(2 * j + 1, 1, GW * j, 0, GW * j + GW)

        def loop_but_last(e, body):
            with e.Fori(0, GROUPS - 1) as j:
                body(2 * j, 0, GW * j, 1, GW * j)
                body(2 * j + 1, 1, GW * j, 0, GW * j + GW)
            j = GROUPS - 1
            body(2 * j, 0, GW * j, 1, GW * j)
            body(2 * j + 1, 1, GW * j, None, None)

        wqk, wv, pw = sb("wqk", [C, BLOCKS, 128]), sb("wv", [C + 1, BLOCKS, C]), sb("pw", [128, BLOCKS, C])
        awq, awk, awv, awp = sb("awq", [C, C]), sb("awk", [C, C]), sb("awv", [C + 1, C]), sb("awp", [128, C])
        qbias = sb("qbias", [C, BLOCKS])
        loads = [(ident[:], d["ident"]), (cols[:], d["cols"]),
                 (rows[:], d["rows"].unsqueeze(0).broadcast_to([TP, len(ROWS), C])),
                 (wqk[:], d["wqk"]), (wv[:], d["wv"]), (pw[:], d["pw"]),
                 (awq[:], d["awq"]), (awk[:], d["awk"]), (awv[:], d["awv"]), (awp[:], d["awp"])]
        with ExitStack() as part:
            px = part.enter_context(nc.sbuf_tensor("px", [TP, PAIRS, 4, 4 * (HW + GW)], F32))
            patches = part.enter_context(nc.sbuf_tensor("patches", [TP, GW, 16], F32))
            patchT = part.enter_context(nc.sbuf_tensor("patchT", [128, 2, TP], F32))
            gained = part.enter_context(nc.sbuf_tensor("gained", [TP, GW, C], F32))
            pew = part.enter_context(nc.sbuf_tensor("pew", [128, GW * C], F32))
            with nc.Block() as block:
                @block.sync
                def _(e):
                    for p in range(PAIRS):
                        for b in range(2):
                            e.dma_start(px[HW * b:HW * (b + 1), p, :, 0:4 * HW],
                                             img[2 * p + b, 0].rearrange("(h i) w -> h i w", i=4)).then_inc(on["image_loaded"].sem, 16)
                    e.dma_start(pew[:], d["pew"]).then_inc(on["image_loaded"].sem, 16)
                    for to, src in loads:
                        e.dma_start(to, src).then_inc(on["constants_loaded"].sem, 16)

                @block.gpsimd
                def _(e):
                    e.memset(neghalf[:], -0.5).then_inc(on["cleared"].sem, 1)
                    e.memset(px[:, :, :, 4 * HW:], 0.0).then_inc(on["cleared"].sem, 1)
                    e.memset(xr[:, PAIRS * HW:, :], 0.0).then_inc(on["cleared"].sem, 1)
                    e.wait_ge(on["cleared"].sem, on["cleared"].at(3))

                    def body(n, p, w, p1, w1):
                        norm_gpsimd(e, n)
                        e.wait_ge(on["normalised"].sem, on["normalised"].at(n + 1))
                        e.tensor_tensor(gained[:], normed[:, p], row("peg"), ALU.mult).then_inc(on["gain_applied"].sem, 1)
                        e.wait_ge(on["gain_applied"].sem, on["gain_applied"].at(n + 1))
                        e.tensor_tensor(group(p, w), gained[:], row("pen"), ALU.add).then_inc(on["embedded"].sem, 1)
                        e.wait_ge(on["embedded"].sem, on["embedded"].at(n + 1))
                    loop_groups(e, body)

                @block.vector
                def _(e):
                    e.wait_ge(on["image_loaded"].sem, on["image_loaded"].at(16 * 5))
                    e.wait_ge(on["constants_loaded"].sem, on["constants_loaded"].at(16 * len(loads)))
                    e.wait_ge(on["cleared"].sem, on["cleared"].at(3))
                    for l in range(BLOCKS):
                        e.tensor_scalar(qbias[:, l:l + 1], col(f"qb{l}"), SCALE, None, ALU.mult).then_inc(on["qbias_ready"].sem, 1)

                    def take_patches(n, p, w):
                        e.wait_ge(on["patches_transposed"].sem, on["patches_transposed"].at(n))
                        e.tensor_copy(patches[:].rearrange("q w (i j) -> q w i j", i=4),
                                           px[:, p, :, bass.ds(4 * w, 4 * GW)].rearrange("q i (w j) -> q w i j", j=4)).then_inc(on["patches_ready"].sem, 1)
                        e.wait_ge(on["patches_transposed"].sem, on["patches_transposed"].at(n + 1))
                        e.tensor_copy(patchT[:, p], bank[2 + p][:, 0:TP]).then_inc(on["patchT_ready"].sem, 1)

                    take_patches(0, 0, 0)

                    def body(n, p, w, p1, w1):
                        take_patches(n + 1, p1, w1)
                        e.wait_ge(on["convolved"].sem, on["convolved"].at(n + 1))
                        e.tensor_tensor(group(p, w), bank[4 + p][0:TP, :].rearrange("q (w c) -> q w c", c=C),
                                             row("peb"), ALU.add).then_inc(on["conv_biased"].sem, 1)
                        e.wait_ge(on["conv_biased"].sem, on["conv_biased"].at(n + 1))
                        e.nop(nofuse=True)
                        norm_vector(e, group(p, w), p, n, freed=(on["embedded"], n))
                    loop_groups(e, body)

                @block.scalar
                def _(e):
                    loop_groups(e, lambda n, p, w, p1, w1: norm_scalar(e, p, n))

                @block.tensor
                def _(e):
                    def convolve(n, p):
                        e.wait_ge(on["patches_ready"].sem, on["patches_ready"].at(n + 1))
                        e.wait_ge(on["patchT_ready"].sem, on["patchT_ready"].at(n))
                        e.transpose(bank[2 + p][:, 0:TP], patches[:].rearrange("q w i -> q (w i)"),
                                         ident[0:TP, 0:TP]).then_inc(on["patches_transposed"].sem, 1)
                        e.wait_ge(on["patchT_ready"].sem, on["patchT_ready"].at(n + 1))
                        e.matmul(bank[4 + p][0:TP, :], patchT[:, p], pew[:], start=True, stop=True).then_inc(on["convolved"].sem, 1)

                    convolve(0, 0)

                    def body(n, p, w, p1, w1):
                        e.wait_ge(on["conv_biased"].sem, on["conv_biased"].at(n))
                        convolve(n + 1, p1)
                    loop_groups(e, body)
            G = PAIRS * GROUPS
            norm_ended(G, G)
            ended(image_loaded=16 * 5, constants_loaded=16 * len(loads), cleared=3, qbias_ready=2, gain_applied=G,
                  embedded=G, patches_transposed=G + 1, patches_ready=G + 1, patchT_ready=G + 1, conv_biased=G,
                  convolved=G + 1)

        def swin_block(l):
            shift = SHIFT * l
            with ExitStack() as part:
                def psb(name, shape, dt=F32):
                    return part.enter_context(nc.sbuf_tensor(f"{name}_{l}", shape, dt))

                yo = psb("yo", [128, B, YW, YH])
                ywin = psb("ywin", [C + 1, 2, NW, SLOT])
                qwin = psb("qwin", [C + WN, 2, NW, SLOT])
                ksb = psb("ksb", [C, NW, SLOT])
                kbd = psb("kbd", [C + WN, 2, NW, NH, WN])
                vbd = psb("vbd", [128, 2, NW, HP, 32])
                P = psb("P", [128, 2, NH, SLOT])
                pT = psb("pT", [128, 2, 512])
                mx = psb("mx", [128, 2, NH])
                osb = psb("osb", [128, 512])
                rden = psb("rden", [128, 512])
                sel, heads, vmask = psb("sel", [128, 128]), psb("heads", [C, NH]), psb("vmask", [128, 16])
                rpb = psb("rpb", [C + WN, NH, WN])
                masks = psb("masks", [C + WN, 3, WN])

                with nc.Block() as block:
                    @block.sync
                    def _(e):
                        for to, src in ((sel[:], d["sel"]), (heads[:], d["heads"]), (vmask[:], d["vmask"]),
                                        (rpb[C:C + WN], d["rpb"][:, l]), (masks[C:C + WN], d["masks"])):
                            e.dma_start(to, src).then_inc(on["tables_loaded"].sem, 16)
                        for k in range(2):
                            for s in range(NW):
                                e.dma_start(qwin[C:C + WN, k, s, 0:WN], d["ident"][0:WN, 0:WN]).then_inc(on["tables_loaded"].sem, 16)
                        e.wait_ge(on["tables_loaded"].sem, on["tables_loaded"].at(16 * (5 + 2 * NW)))

                    @block.gpsimd
                    def _(e):
                        for i, a in enumerate((ywin[0:C], qwin[:, :, :, WN:], P[:], vbd[:], yo[0:C, :, HW:, :],
                                               yo[0:C, :, 0:HW, HW:])):
                            e.memset(a, 0.0).then_inc(on["cleared"].sem, 1)
                            e.wait_ge(on["cleared"].sem, on["cleared"].at(i + 1))
                        for i, a in enumerate((ywin[C:C + 1], vbd[0:C, :, :, :, 16:17], vbd[C:128, :, :, :, 17:18])):
                            e.memset(a, 1.0).then_inc(on["ones_set"].sem, 1)
                            e.wait_ge(on["ones_set"].sem, on["ones_set"].at(i + 1))
                        loop_groups(e, lambda n, p, w, p1, w1: norm_gpsimd(e, n))

                    @block.vector
                    def _(e):
                        norm_centre(e, group(0, 0), 0, 0)

                        def body(n, p, w, p1, w1):
                            norm_variance(e, n)
                            e.nop(nofuse=True)
                            norm_centre(e, group(p1, w1), p1, n + 1)
                            norm_scale(e, p, n, freed=(on["transposed"], 2 * n))
                        loop_groups(e, body)

                    @block.tensor
                    def _(e):
                        loop_groups(e, lambda n, p, w, p1, w1: transpose_group(e, p, n))

                    @block.scalar
                    def _(e):
                        e.wait_ge(on["cleared"].sem, on["cleared"].at(6))
                        norm_scalar(e, 0, 0)

                        def body(n, p, w, p1, w1):
                            norm_scalar(e, p1, n + 1)
                            for half in range(2):
                                e.wait_ge(on["transposed"].sem, on["transposed"].at(2 * n + half + 1))
                                e.nop(nofuse=True)
                                e.activation(yo[0:C, 2 * p:2 * p + 2, bass.ds(w + 4 * half, 4), 0:HW]
                                                  .rearrange("c b w h -> c w b h"),
                                                  bank[half][0:C, 0:HALF].rearrange("c (w b h) -> c w b h", w=4, b=2),
                                                  ACT.Identity, scale=col(f"n1g{l}"), bias=col(f"n1b{l}")).then_inc(on["evacuated"].sem, 1)
                        loop_groups(e, body)
                norm_ended(2 * GROUPS, 2 * GROUPS + 1)
                ended(transposed=4 * GROUPS, evacuated=4 * GROUPS, tables_loaded=16 * (5 + 2 * NW), cleared=6, ones_set=3)

                def bias_rows(e, w_edge):
                    for k in range(2):
                        for s in range(NW):
                            to = kbd[C:C + WN, k, s]
                            m = (2 if w_edge else 0) if s == NW - 1 else 1 if w_edge else None
                            if shift and m is not None:
                                ins = e.tensor_tensor(to, rpb[C:C + WN],
                                                      masks[C:C + WN, m].unsqueeze(1).broadcast_to([WN, NH, WN]), ALU.add)
                            else:
                                ins = e.tensor_copy(to, rpb[C:C + WN])
                            ins.then_inc(on["bias_set"].sem, 1)

                with nc.Block() as block:
                    @block.vector
                    def _(e):
                        bias_rows(e, False)
                        e.wait_ge(on["bias_set"].sem, on["bias_set"].at(2 * NW))
                    if shift:
                        @block.gpsimd
                        def _(e):
                            e.tensor_copy(yo[0:C, :, 0:HW, HW:HW + shift], yo[0:C, :, 0:HW, 0:shift]).then_inc(on["wrapped"].sem, 1)
                            e.wait_ge(on["wrapped"].sem, on["wrapped"].at(1))
                            e.tensor_copy(yo[0:C, :, HW:HW + shift, 0:HW + shift], yo[0:C, :, 0:shift, 0:HW + shift]).then_inc(on["wrapped"].sem, 1)
                            e.wait_ge(on["wrapped"].sem, on["wrapped"].at(2))
                ended(bias_set=2 * NW, wrapped=2 if shift else 0)

                def windows(w_from, w_to):
                    chunks, pairs = (w_to - w_from) * B, (w_to - w_from) * B * 4

                    def tokens(b, w):
                        return yo[:, b, bass.ds(WS * w + shift, WS), shift:shift + HW].rearrange("c w (s r) -> c s w r", r=WS)

                    def slots(ap):
                        return ap[:, :, 0:WN].rearrange("c s (w r) -> c s w r", w=WS)

                    def loop_chunks(e, head, main):
                        head(0, 0, w_from, 0)
                        with e.Fori(w_from, w_to) as i:
                            for b in range(B):
                                n = (i - w_from) * B + b
                                main(n, b, i, b % 2, lambda: head(n + 1, (b + 1) % B, i + (b + 1) // B, (b + 1) % 2))

                    QK, V, S, T, O, D = bank[0], bank[1], (bank[2], bank[3]), (bank[4], bank[5]), bank[6], bank[7]

                    with nc.Block() as block:
                        @block.gpsimd
                        def _(e):
                            def head(n, b, w, k):
                                e.wait_ge(on["keys_evacuated"].sem, on["keys_evacuated"].at(n))
                                e.nop(nofuse=True)
                                e.tensor_copy(slots(ywin[0:C, k]), tokens(b, w)[0:C]).then_inc(on["windows_staged"].sem, 1)
                                e.wait_ge(on["keys_evacuated"].sem, on["keys_evacuated"].at(n + 1))
                                e.tensor_tensor(kbd[0:C, k], ksb[:, :, 0:WN].unsqueeze(2).broadcast_to([C, NW, NH, WN]),
                                                     heads[:].unsqueeze(1).unsqueeze(3).broadcast_to([C, NW, NH, WN]),
                                                     ALU.mult).then_inc(on["keys_by_head"].sem, 1)
                            loop_chunks(e, head, lambda n, b, w, k, ahead: ahead())

                        @block.tensor
                        def _(e):
                            e.nop(nofuse=True).then_inc(on["probs_transposed"].sem, 1)

                            def head(n, b, w, k):
                                e.wait_ge(on["windows_staged"].sem, on["windows_staged"].at(n + 1))
                                e.wait_ge(on["keys_evacuated"].sem, on["keys_evacuated"].at(n))
                                e.matmul(QK[:, :], wqk[:, l], ywin[0:C, k].rearrange("c s t -> c (s t)"),
                                              start=True, stop=True).then_inc(on["qk_ready"].sem, 1)
                                e.wait_ge(on["values_by_head"].sem, on["values_by_head"].at(n))
                                for s in range(NW):
                                    for half in range(2):
                                        last = e.matmul(V[64 * half:64 * half + 64, s * C:(s + 1) * C], ywin[:, k, s],
                                                        wv[:, l], start=True, stop=True)
                                last.then_inc(on["values_ready"].sem, 1)

                            def scores(n, g, k):
                                e.wait_ge(on["shifted"].sem, on["shifted"].at(4 * n + g + 1))
                                for a in range(2):
                                    s = 2 * g + a
                                    last = e.matmul(S[g % 2][64 * a:64 * a + 64, 0:NH * WN], qwin[:, k, s],
                                                    kbd[:, k, s].rearrange("c h t -> c (h t)"), start=True, stop=True)
                                last.then_inc(on["scores_ready"].sem, 1)

                            def transposes(n, g):
                                e.wait_ge(on["exponentials_ready"].sem, on["exponentials_ready"].at(4 * n + g + 1))
                                e.wait_ge(on["probs_evacuated"].sem, on["probs_evacuated"].at(4 * n + g + 1))
                                for hp in range(HP):
                                    last = e.transpose(T[g % 2][:, 128 * hp:128 * hp + 128],
                                                       P[:, g % 2, 2 * hp:2 * hp + 2].rearrange("q h t -> q (h t)"), ident[:])
                                last.then_inc(on["probs_transposed"].sem, 1)

                            def weighted(n, g, k):
                                e.wait_ge(on["probs_evacuated"].sem, on["probs_evacuated"].at(4 * n + g + 3))
                                if g == 0:
                                    e.wait_ge(on["outputs_evacuated"].sem, on["outputs_evacuated"].at(n))
                                for a in range(2):
                                    for hp in range(HP):
                                        s = 2 * g + a
                                        last = e.matmul(O[32 * hp:32 * hp + 32, s * SLOT:(s + 1) * SLOT], vbd[:, k, s, hp],
                                                        pT[:, g % 2, 128 * hp + 64 * a:128 * hp + 64 * a + 64],
                                                        start=True, stop=True)
                                if g == 3:
                                    last.then_inc(on["outputs_ready"].sem, 1)

                            def main(n, b, w, k, ahead):
                                e.wait_ge(on["keys_by_head"].sem, on["keys_by_head"].at(n + 1))
                                scores(n, 0, k)
                                ahead()
                                scores(n, 1, k)
                                transposes(n, 0)
                                scores(n, 2, k)
                                e.wait_ge(on["values_by_head"].sem, on["values_by_head"].at(n + 1))
                                weighted(n, 0, k)
                                transposes(n, 1)
                                scores(n, 3, k)
                                weighted(n, 1, k)
                                transposes(n, 2)
                                weighted(n, 2, k)
                                transposes(n, 3)
                                weighted(n, 3, k)
                                e.wait_ge(on["outputs_evacuated"].sem, on["outputs_evacuated"].at(n + 1))
                                e.wait_ge(on["denominators_read"].sem, on["denominators_read"].at(n))
                                e.matmul(D[:, :], sel[:], osb[:], start=True, stop=True).then_inc(on["denominators_ready"].sem, 1)
                            loop_chunks(e, head, main)

                        @block.scalar
                        def _(e):
                            e.nop(nofuse=True).then_inc(on["probs_evacuated"].sem, 2)

                            def head(n, b, w, k):
                                e.wait_ge(on["qk_ready"].sem, on["qk_ready"].at(n + 1))
                                e.activation(qwin[0:C, k].rearrange("c s t -> c (s t)"), QK[0:C, :], ACT.Identity,
                                                  scale=SCALE, bias=qbias[:, l:l + 1]).then_inc(on["queries_evacuated"].sem, 1)
                                e.wait_ge(on["keys_by_head"].sem, on["keys_by_head"].at(n))
                                e.activation(ksb[:].rearrange("c s t -> c (s t)"), QK[C:128, :], ACT.Identity,
                                                  bias=col(f"kb{l}")).then_inc(on["keys_evacuated"].sem, 1)

                            def exponentials(n, g):
                                e.wait_ge(on["shifted"].sem, on["shifted"].at(4 * n + g + 3))
                                e.activation(P[:, g % 2, :, 0:WN], P[:, g % 2, :, 0:WN], ACT.Exp).then_inc(on["exponentials_ready"].sem, 1)

                            def evacuate(n, g):
                                e.wait_ge(on["probs_transposed"].sem, on["probs_transposed"].at(4 * n + g + 2))
                                e.copy(pT[:, g % 2], T[g % 2][:, :]).then_inc(on["probs_evacuated"].sem, 1)

                            def main(n, b, w, k, ahead):
                                exponentials(n, 0)
                                ahead()
                                exponentials(n, 1)
                                evacuate(n, 0)
                                exponentials(n, 2)
                                evacuate(n, 1)
                                exponentials(n, 3)
                                evacuate(n, 2)
                                evacuate(n, 3)
                                e.wait_ge(on["outputs_ready"].sem, on["outputs_ready"].at(n + 1))
                                e.wait_ge(on["outputs_normalised"].sem, on["outputs_normalised"].at(n))
                                e.copy(osb[:], O[:, :]).then_inc(on["outputs_evacuated"].sem, 1)
                            loop_chunks(e, head, main)

                        @block.vector
                        def _(e):
                            e.nop(nofuse=True).then_inc(on["shifted"].sem, 2)

                            def head(n, b, w, k):
                                e.wait_ge(on["values_ready"].sem, on["values_ready"].at(n + 1))
                                e.tensor_tensor(vbd[:, k, :, :, 0:16].rearrange("t s h c -> t (s h) c"),
                                                     V[:, :].rearrange("t (x c) -> t x c", c=16),
                                                     vmask[:].unsqueeze(1).broadcast_to([128, NW * HP, 16]), ALU.mult).then_inc(on["values_by_head"].sem, 1)

                            def shift_scores(n, g):
                                e.wait_ge(on["scores_ready"].sem, on["scores_ready"].at(4 * n + g + 1))
                                sc = S[g % 2][:, 0:NH * WN].rearrange("q (h t) -> q h t", h=NH)
                                e.tensor_reduce(out=mx[:, g % 2], in_=sc, axis=AX, op=ALU.max).then_inc(on["maxima_ready"].sem, 1)
                                e.wait_ge(on["maxima_ready"].sem, on["maxima_ready"].at(4 * n + g + 1))
                                e.wait_ge(on["probs_transposed"].sem, on["probs_transposed"].at(4 * n + g))
                                e.tensor_tensor(P[:, g % 2, :, 0:WN], sc,
                                                     mx[:, g % 2].unsqueeze(2).broadcast_to([128, NH, WN]), ALU.subtract).then_inc(on["shifted"].sem, 1)

                            def main(n, b, w, k, ahead):
                                shift_scores(n, 0)
                                ahead()
                                for g in range(1, 4):
                                    shift_scores(n, g)
                                e.wait_ge(on["denominators_ready"].sem, on["denominators_ready"].at(n + 1))
                                e.reciprocal(rden[:], D[:, :]).then_inc(on["denominators_read"].sem, 1)
                                e.wait_ge(on["denominators_read"].sem, on["denominators_read"].at(n + 1))
                                e.tensor_tensor(tokens(b, w), slots(osb[:].rearrange("c (s t) -> c s t", s=NW)),
                                                     slots(rden[:].rearrange("c (s t) -> c s t", s=NW)), ALU.mult).then_inc(on["outputs_normalised"].sem, 1)
                            loop_chunks(e, head, main)
                    h, g = chunks + 1, pairs
                    ended(windows_staged=h, keys_evacuated=h, keys_by_head=h, qk_ready=h, values_ready=h, values_by_head=h,
                          queries_evacuated=h, shifted=g + 2, scores_ready=g, exponentials_ready=g, probs_evacuated=g + 2,
                          probs_transposed=g + 1, maxima_ready=g, outputs_evacuated=chunks, outputs_ready=chunks,
                          denominators_ready=chunks, denominators_read=chunks, outputs_normalised=chunks)

                windows(0, NW - 1 if shift else NW)
                if shift:
                    with nc.Block() as block:
                        @block.vector
                        def _(e):
                            bias_rows(e, True)
                            e.wait_ge(on["bias_set"].sem, on["bias_set"].at(2 * NW))
                    ended(bias_set=2 * NW)
                    windows(NW - 1, NW)
                    with nc.Block() as block:
                        @block.gpsimd
                        def _(e):
                            e.tensor_copy(yo[:, :, 0:shift, shift:HW + shift], yo[:, :, HW:HW + shift, shift:HW + shift]).then_inc(on["wrapped"].sem, 1)
                            e.wait_ge(on["wrapped"].sem, on["wrapped"].at(1))
                            e.tensor_copy(yo[:, :, 0:HW, 0:shift], yo[:, :, 0:HW, HW:HW + shift]).then_inc(on["wrapped"].sem, 1)
                            e.wait_ge(on["wrapped"].sem, on["wrapped"].at(2))
                    ended(wrapped=2)

                ysb = psb("proj_out", [128, 2, HALF])
                with nc.Block() as block:
                    @block.tensor
                    def _(e):
                        def body(n, p, w, p1, w1):
                            e.wait_ge(on["outputs_evacuated"].sem, on["outputs_evacuated"].at(n))
                            e.nop(nofuse=True)
                            for half in range(2):
                                last = e.matmul(bank[2 * p + half][0:C, 0:HALF].rearrange("c (w b h) -> c w b h", w=4, b=2), pw[:, l],
                                                yo[:, 2 * p:2 * p + 2, bass.ds(w + 4 * half, 4), 0:HW].rearrange("c b w h -> c w b h"),
                                                start=True, stop=True)
                            last.then_inc(on["outputs_ready"].sem, 1)
                            e.wait_ge(on["outputs_evacuated"].sem, on["outputs_evacuated"].at(n + 1))
                            e.wait_ge(on["residual_added"].sem, on["residual_added"].at(n))
                            for x in range(4):
                                last = e.transpose(bank[4 + p][0:TP, 128 * x:128 * (x + 1)], ysb[:, p, TP * x:TP * (x + 1)], ident[:])
                            last.then_inc(on["projected"].sem, 1)
                        loop_groups(e, body)

                    @block.scalar
                    def _(e):
                        def body(n, p, w, p1, w1):
                            e.wait_ge(on["outputs_ready"].sem, on["outputs_ready"].at(n + 1))
                            e.copy(ysb[0:C, p], bank[2 * p][0:C, 0:HALF])
                            e.copy(ysb[C:, p], bank[2 * p + 1][0:C, 0:HALF]).then_inc(on["outputs_evacuated"].sem, 1)
                        loop_groups(e, body)

                    @block.vector
                    def _(e):
                        def body(n, p, w, p1, w1):
                            e.wait_ge(on["projected"].sem, on["projected"].at(n + 1))
                            e.nop(nofuse=True)
                            halves = group(p, w).rearrange("t (h w) c -> t h w c", h=2)
                            e.tensor_tensor(halves, halves, bank[4 + p][0:TP, :].rearrange("t (w h c) -> t h w c", h=2, c=C),
                                            ALU.add).then_inc(on["residual_added"].sem, 1)
                        loop_groups(e, body)
                G = 2 * GROUPS
                ended(outputs_ready=G, outputs_evacuated=G, projected=G, residual_added=G)

            with ExitStack() as part:
                def psb(name, shape, dt=F32):
                    return part.enter_context(nc.sbuf_tensor(f"{name}_{l}", shape, dt))
                y = psb("mlp_in", [AK, GW, TP])
                hid = psb("mlp_hid", [128, 2, GW, TP])
                ysb = psb("mlp_out", [128, HALF])
                w1, w2 = psb("w1", [AK, 2 * HID]), psb("w2", [128, 2, C])
                with nc.Block() as block:
                    @block.sync
                    def _(e):
                        e.dma_start(w1[:], d["w1"][:, l]).then_inc(on["mlp_weights_loaded"].sem, 16)
                        e.dma_start(w2[:], d["w2"][:, l]).then_inc(on["mlp_weights_loaded"].sem, 16)
                        e.wait_ge(on["mlp_weights_loaded"].sem, on["mlp_weights_loaded"].at(32))

                    @block.gpsimd
                    def _(e):
                        e.memset(y[C:AK], 0.0).then_inc(on["cleared"].sem, 1)
                        e.wait_ge(on["cleared"].sem, on["cleared"].at(1))
                        norm_squares(e, 0, 0)
                        norm_gpsimd(e, 0)
                        norm_squares(e, 1, 1)
                        norm_gpsimd(e, 1)

                        def body(n, p, w, p1, w1_):
                            norm_squares(e, p, n + 2)
                            norm_gpsimd(e, n + 2)
                        loop_groups(e, body)

                    @block.vector
                    def _(e):
                        norm_vector(e, group(0, 0), 0, 0)
                        norm_vector(e, group(1, 0), 1, 1)

                        def body(n, p, w, p1, w1_):
                            e.nop(nofuse=True)
                            norm_vector(e, group(p, w + GW), p, n + 2, freed=(on["transposed"], 2 * n + 2))
                            e.wait_ge(on["mlp_ready"].sem, on["mlp_ready"].at(n + 1))
                            e.nop(nofuse=True)
                            halves = group(p, w).rearrange("t (h w) c -> t h w c", h=2)
                            e.tensor_tensor(halves, halves, bank[7][0:TP, :].rearrange("t (w h c) -> t h w c", h=2, c=C),
                                            ALU.add).then_inc(on["residual_added"].sem, 1)
                        loop_groups(e, body)

                    @block.scalar
                    def _(e):
                        def evacuate_tokens(n):
                            for half in range(2):
                                e.wait_ge(on["transposed"].sem, on["transposed"].at(2 * n + half + 1))
                                e.activation(y[0:C, 4 * half:4 * half + 4].rearrange("c w t -> c (w t)"), bank[half][0:C, 0:HALF],
                                                  ACT.Identity, scale=col(f"n2g{l}"), bias=col(f"n2b{l}")).then_inc(on["evacuated"].sem, 1)

                        def gelus(n):
                            for half in range(2):
                                for f in range(2):
                                    e.wait_ge(on["hidden_ready"].sem, on["hidden_ready"].at(4 * n + 2 * half + f + 1))
                                    e.activation(hid[:, f, 4 * half:4 * half + 4].rearrange("c w t -> c (w t)"),
                                                      bank[2 + 2 * half + f][:, 0:HALF], ACT.Gelu, bias=col(f"mb{l}{f}", 0, 128)).then_inc(on["gelu_done"].sem, 1)
                        evacuate_tokens(0)
                        gelus(0)

                        def body(n, p, w, p1, w1_):
                            evacuate_tokens(n + 1)
                            e.wait_ge(on["outputs_ready"].sem, on["outputs_ready"].at(n + 1))
                            e.activation(ysb[:], bank[6][:, 0:HALF], ACT.Identity, bias=col(f"b2{l}", 0, 128)
                                         ).then_inc(on["outputs_evacuated"].sem, 1)
                            gelus(n + 1)
                        loop_groups(e, body)

                    @block.tensor
                    def _(e):
                        def hidden(n):
                            e.wait_ge(on["gelu_done"].sem, on["gelu_done"].at(4 * n))
                            for half in range(2):
                                e.wait_ge(on["evacuated"].sem, on["evacuated"].at(2 * n + half + 1))
                                for f in range(2):
                                    e.matmul(bank[2 + 2 * half + f][:, 0:HALF], w1[:, HID * f:HID * (f + 1)],
                                                  y[:, 4 * half:4 * half + 4].rearrange("c w t -> c (w t)"),
                                                  start=True, stop=True).then_inc(on["hidden_ready"].sem, 1)
                        e.wait_ge(on["mlp_weights_loaded"].sem, on["mlp_weights_loaded"].at(32))
                        e.wait_ge(on["cleared"].sem, on["cleared"].at(1))
                        transpose_group(e, 0, 0)
                        hidden(0)

                        def body(n, p, w, p1, w1_):
                            transpose_group(e, p1, n + 1)
                            e.wait_ge(on["gelu_done"].sem, on["gelu_done"].at(4 * n + 4))
                            e.wait_ge(on["outputs_evacuated"].sem, on["outputs_evacuated"].at(n))
                            for f in range(2):
                                for half in range(2):
                                    last = e.matmul(bank[6][C * half:C * (half + 1), 0:HALF], w2[:, f],
                                                    hid[:, f, 4 * half:4 * half + 4].rearrange("c w t -> c (w t)"),
                                                    start=f == 0, stop=f == 1)
                            last.then_inc(on["outputs_ready"].sem, 1)
                            hidden(n + 1)
                            e.wait_ge(on["outputs_evacuated"].sem, on["outputs_evacuated"].at(n + 1))
                            e.wait_ge(on["residual_added"].sem, on["residual_added"].at(n))
                            for x in range(4):
                                last = e.transpose(bank[7][0:TP, 128 * x:128 * (x + 1)], ysb[:, TP * x:TP * (x + 1)], ident[:])
                            last.then_inc(on["mlp_ready"].sem, 1)
                        loop_groups(e, body)
                G = 2 * GROUPS
                norm_ended(G + 2, G + 2)
                ended(mlp_weights_loaded=32, mlp_ready=G, residual_added=G, transposed=2 * G + 2, evacuated=2 * G + 2,
                      hidden_ready=4 * G + 4, gelu_done=4 * G + 4, outputs_ready=G, outputs_evacuated=G, cleared=1)

        swin_block(0)
        swin_block(1)
        with ExitStack() as part:
            def psb(name, shape, dt=F32):
                return part.enter_context(nc.sbuf_tensor(name, shape, dt))

            hT = psb("hT", [128, B, N])
            tok = psb("tok", [C + 1, N])
            kst = psb("kst", [AK, N])
            khi, klo = psb("khi", [128, N], BF16), psb("klo", [128, N], BF16)
            vst = psb("vst", [TP, KT, C])
            qst = psb("qst", [AK, HALF])
            qnext = psb("qnext", [C + 1, HALF])
            ones = psb("ones", [TP, 1])
            psum = psb("psum", [TP, 2, HALF])
            denrow = psb("denrow", [1, HALF])
            forward = psb("forward", [TP, 2, HALF])
            qsplit = psb("qsplit", [128, HALF], BF16)
            biasT = psb("biasT", [TP, 2352])
            biasQ = psb("biasQ", [TP, 2576])
            biased = psb("biased", [TP, 2, HALF])
            pexp = psb("pexp", [TP, 4, HALF])
            tmx, rmx, nmx = psb("tmx", [TP, 4, QT]), psb("rmx", [TP, 4]), psb("nmx", [TP, 4])
            awk2, awq2 = psb("awk2", [C, 2, C]), psb("awq2", [C, 2, C])
            bias2 = psb("bias2", [128, 2])

            flip = psb("flip", [TP, TP])
            pieces = [(t, slice(i, i + n)) for t, n in ((biasT, 392), (biasQ, 368)) for i in range(0, t.shape[1], n)]

            with nc.Block() as block:
                @block.sync
                def _(e):
                    for w in range(2):
                        e.dma_start(awk2[:, w], d["awk"]).then_inc(on["tables_loaded"].sem, 16)
                        e.dma_start(awq2[:, w], d["awq"]).then_inc(on["tables_loaded"].sem, 16)
                        e.dma_start(bias2[C * w:C * (w + 1)], d["bias2"]).then_inc(on["tables_loaded"].sem, 16)
                    for to, src in ((biasT, d["ext"]), (biasQ, d["extq"])):
                        e.dma_start(to[:], bass.AP(src.tensor, 0, [[1, TP], [1, to.shape[1]]])).then_inc(on["tables_loaded"].sem, 16)
                    e.dma_start(flip[:], d["flip"]).then_inc(on["tables_loaded"].sem, 16)
                    e.wait_ge(on["tables_loaded"].sem, on["tables_loaded"].at(16 * 9))

                @block.gpsimd
                def _(e):
                    for i, (a, v) in enumerate(((kst[C:AK], 0.0), (kst[C:C + 1], 1.0), (qst[C:AK], 0.0),
                                                (ones[:], 1.0), (tok[C:C + 1], 1.0))):
                        e.memset(a, v).then_inc(on["cleared"].sem, 1)
                        e.wait_ge(on["cleared"].sem, on["cleared"].at(i + 1))
                    loop_groups(e, lambda n, p, w, p1, w1: norm_gpsimd(e, n))

                @block.vector
                def _(e):
                    for i, (t, at) in enumerate(pieces):
                        e.wait_ge(on["bias_flipped"].sem, on["bias_flipped"].at(i + 1))
                        e.tensor_scalar(t[:, at], bank[2 + i % 2][0:TP, 0:at.stop - at.start], col("last", 0, TP), None,
                                             ALU.subtract).then_inc(on["bias_set"].sem, 1)
                    norm_centre(e, group(0, 0), 0, 0)

                    def body(n, p, w, p1, w1):
                        norm_variance(e, n, weight=1 + EPS, extra=EPS ** 2)
                        e.nop(nofuse=True)
                        norm_centre(e, group(p1, w1), p1, n + 1)
                        norm_scale(e, p, n, freed=(on["transposed"], 2 * n))
                    loop_groups(e, body)
                    e.wait_ge(on["bias_set"].sem, on["bias_set"].at(len(pieces)))

                @block.tensor
                def _(e):
                    e.wait_ge(on["tables_loaded"].sem, on["tables_loaded"].at(16 * 9))
                    for i, (t, at) in enumerate(pieces):
                        e.wait_ge(on["bias_set"].sem, on["bias_set"].at(max(i - 1, 0)))
                        e.matmul(bank[2 + i % 2][0:TP, 0:at.stop - at.start], flip[:], t[:, at], start=True, stop=True).then_inc(on["bias_flipped"].sem, 1)
                    loop_groups(e, lambda n, p, w, p1, w1: transpose_group(e, p, n))

                @block.scalar
                def _(e):
                    norm_scalar(e, 0, 0)

                    def body(n, p, w, p1, w1):
                        norm_scalar(e, p1, n + 1)
                        for half in range(2):
                            e.wait_ge(on["transposed"].sem, on["transposed"].at(2 * n + half + 1))
                            e.nop(nofuse=True)
                            e.activation(hT[0:C, 2 * p:2 * p + 2, :].rearrange("c b (h w) -> c w b h", w=HW)
                                              [:, bass.ds(w + 4 * half, 4)],
                                              bank[half][0:C, 0:HALF].rearrange("c (w b h) -> c w b h", w=4, b=2),
                                              ACT.Identity, scale=col("ag"), bias=col("ab")).then_inc(on["evacuated"].sem, 1)
                    loop_groups(e, body)
            norm_ended(2 * GROUPS, 2 * GROUPS + 1)
            ended(transposed=4 * GROUPS, evacuated=4 * GROUPS, tables_loaded=16 * 9, cleared=5, bias_set=len(pieces), bias_flipped=len(pieces))

            S, M, X, O = bank[0:4], bank[4:6], bank[6], bank[7]
            AHEAD = 2, 10

            def ahead_in(step):
                first, last = AHEAD
                n = 4 * QT
                done = lambda x: min(max(x - first, 0) * n // (last + 1 - first), n)
                return [(i // QT, i % QT) for i in range(done(step), done(step + 1))]

            def loop_tiles(e, image, tile):
                with e.Fori(0, B) as b:
                    image(b)

                    def one(q, first, late, then):
                        tile(b, q, b * QT + q, (b * QT + q) * KT, first, late, then)
                    one(0, True, False, False)
                    with e.Fori(1, QFLAT - 1) as q:
                        one(q, False, False, False)
                    one(QFLAT - 1, False, False, True)
                    with e.Fori(QFLAT, QT - 1) as q:
                        one(q, False, True, True)
                    one(QT - 1, False, True, None)

            def late_tiles(b, q):
                return b * (QT - QFLAT) + q - QFLAT

            with nc.Block() as block:
                @block.sync
                def _(e):
                    with e.Fori(0, B) as b:
                        with e.Fori(0, QT) as q:
                            e.wait_ge(on["denominators_read"].sem, on["denominators_read"].at(b * QT + q + 1))
                            e.nop(nofuse=True)
                            e.dma_start(d["dens"][bass.ds((b * QT + q) * HALF, HALF)].unsqueeze(0), denrow[:]
                                        ).then_inc(on["denominators_stored"].sem, 16)
                            e.wait_ge(on["denominators_stored"].sem, on["denominators_stored"].at((b * QT + q) * 16 + 16))
                            e.nop(nofuse=True).then_inc(on["row_free"].sem, 1)

                @block.gpsimd
                def _(e):
                    e.nop(nofuse=True).then_inc(on["summed_gpsimd"].sem, 2)

                    def image(b):
                        pass

                    def tile(b, q, Q, U, first, late, then):
                        e.wait_ge(on["denominators_ready"].sem, on["denominators_ready"].at(Q))
                        for t in range(1, KT, 2):
                            e.wait_ge(on["attn_exponentials"].sem, on["attn_exponentials"].at(U + t + 5))
                            if t == 1:
                                e.nop(nofuse=True)
                                e.tensor_copy(psum[:, 1], pexp[:, 1]).then_inc(on["summed_gpsimd"].sem, 1)
                            else:
                                e.wait_ge(on["summed_gpsimd"].sem, on["summed_gpsimd"].at(KT // 2 * Q + t // 2 + 2))
                                e.tensor_tensor(psum[:, 1], psum[:, 1], pexp[:, t % 4], ALU.add).then_inc(on["summed_gpsimd"].sem, 1)
                    loop_tiles(e, image, tile)

                @block.tensor
                def _(e):
                    def query(b, q, Q):
                        e.wait_ge(on["maximum_set"].sem, on["maximum_set"].at(Q))
                        e.nop(nofuse=True)
                        e.matmul(X[:, 0:HALF], awq2[:].rearrange("c x k -> c (x k)"), hT[0:C, b, bass.ds(q * HALF, HALF)],
                                 start=True, stop=True).then_inc(on["query_ready"].sem, 1)

                    def tile_scores(U, s, t):
                        e.wait_ge(on["tile_maximum"].sem, on["tile_maximum"].at(U + 7 * s + t + 1))
                        for i, k in enumerate((khi, klo)):
                            last = e.matmul(M[(7 * s + t) % 2][0:TP, 0:HALF], qsplit[:, TP * s:TP * (s + 1)],
                                            k[:, t * HALF:(t + 1) * HALF], start=i == 0, stop=i == 1)
                        last.then_inc(on["tile_scored"].sem, 1)

                    def move_maxima(Q):
                        e.wait_ge(on["row_maximum"].sem, on["row_maximum"].at(Q + 1))
                        for s in range(4):
                            last = e.matmul(X[C:C + 1, TP * s:TP * (s + 1)], nmx[:, s:s + 1], ident[0:TP, 0:TP],
                                            start=True, stop=True)
                        last.then_inc(on["maximum_moved"].sem, 1)

                    def image(b):
                        e.wait_ge(on["attn_exponentials"].sem, on["attn_exponentials"].at(b * QT * KT + 4))
                        for t in range(QT):
                            if t >= 4:
                                e.wait_ge(on["keys_evacuated"].sem, on["keys_evacuated"].at(QT * b + t - 3))
                            e.nop(nofuse=True)
                            e.matmul(S[t % 4][:, 0:HALF], awk2[:].rearrange("c x k -> c (x k)"),
                                     hT[0:C, b, t * HALF:(t + 1) * HALF], start=True, stop=True).then_inc(on["keys_ready"].sem, 1)
                            if t < 3:
                                continue
                            g = t - 3
                            if g == 0:
                                e.wait_ge(on["tokens_staged"].sem, on["tokens_staged"].at(b + 1))
                            if g >= 2:
                                e.wait_ge(on["values_evacuated"].sem, on["values_evacuated"].at(4 * b + g - 1))
                            for x in range(7 * g, 7 * g + 7):
                                last = e.matmul(M[g % 2][0:TP, C * (x - 7 * g):C * (x - 7 * g + 1)], tok[:, x * TP:(x + 1) * TP],
                                                awv[:], start=True, stop=True)
                            last.then_inc(on["values_ready"].sem, 1)
                            if g == 0:
                                e.wait_ge(on["denominators_read"].sem, on["denominators_read"].at(b * QT))
                                query(b, 0, b * QT)
                        e.wait_ge(on["keys_evacuated"].sem, on["keys_evacuated"].at(QT * b + QT))
                        e.wait_ge(on["values_evacuated"].sem, on["values_evacuated"].at(4 * b + 4))
                        e.wait_ge(on["queries_split"].sem, on["queries_split"].at(b * QT + 1))
                        for s in range(4):
                            for t in range(QT):
                                tile_scores(b * QT * KT, s, t)
                        move_maxima(b * QT)

                    def scores(U, t):
                        e.wait_ge(on["attn_exponentials"].sem, on["attn_exponentials"].at(U + t + 1))
                        e.matmul(S[t % 4][0:TP, 0:HALF], kst[:, TP * t:TP * (t + 1)], qst[:], start=True, stop=True
                                 ).then_inc(on["attn_scored"].sem, 1)

                    def denominators(Q):
                        e.wait_ge(on["maximum_set"].sem, on["maximum_set"].at(Q + 1))
                        e.wait_ge(on["summed_vector"].sem, on["summed_vector"].at(KT // 2 * (Q + 1) + 2))
                        e.wait_ge(on["summed_gpsimd"].sem, on["summed_gpsimd"].at(KT // 2 * (Q + 1) + 2))
                        for i in range(2):
                            last = e.matmul(X[0:1, 0:HALF], ones[:], psum[:, i], start=i == 0, stop=i == 1)
                        last.then_inc(on["denominators_ready"].sem, 1)

                    def tile(b, q, Q, U, first, late, then):
                        if first:
                            e.wait_ge(on["query_set"].sem, on["query_set"].at(Q + 1))
                            scores(U, 0)
                            scores(U, 1)
                        for step in range(KT // 2):
                            ahead = ahead_in(step) if then is not None else []
                            if step == AHEAD[0] and then is not None:
                                e.wait_ge(on["queries_split"].sem, on["queries_split"].at(Q + 2))
                            for t in (2 * step + 2, 2 * step + 3):
                                if t < KT:
                                    scores(U, t)
                                    for s, k in ahead[t % 2:t % 2 + 1]:
                                        tile_scores(U + KT, s, k)
                            if step == 0 and not first:
                                denominators(Q - 1)
                            if step == KT // 2 - 1 and then is not None:
                                e.wait_ge(on["query_set"].sem, on["query_set"].at(Q + 2))
                                scores(U + KT, 0)
                                scores(U + KT, 1)
                            e.wait_ge(on["attn_exponentials"].sem, on["attn_exponentials"].at(U + 2 * step + 6))
                            if step == 0:
                                e.wait_ge(on["attn_evacuated"].sem, on["attn_evacuated"].at(Q))
                            for t in (2 * step, 2 * step + 1):
                                e.matmul(O[C * (t % 2):C * (t % 2) + C, 0:HALF], vst[:, t], pexp[:, t % 4],
                                         start=step == 0, stop=step == KT // 2 - 1).then_inc(on["attn_weighted"].sem, 1)
                            for s, k in ahead[2:]:
                                tile_scores(U + KT, s, k)
                            if then is not None:
                                if step == 0:
                                    e.wait_ge(on["denominators_read"].sem, on["denominators_read"].at(Q))
                                    query(b, q + 1, Q + 1)
                                if step == AHEAD[1] + 1:
                                    move_maxima(Q + 1)
                        if then is None:
                            denominators(Q)
                    loop_tiles(e, image, tile)

                @block.scalar
                def _(e):
                    e.nop(nofuse=True).then_inc(on["attn_exponentials"].sem, 4)

                    def query(Q):
                        e.wait_ge(on["query_ready"].sem, on["query_ready"].at(Q + 1))
                        e.activation(qsplit[:], X[:, 0:HALF], ACT.Identity, bias=bias2[:, 1:2])
                        e.activation(qnext[0:C, :], X[0:C, 0:HALF], ACT.Identity, bias=bias2[0:C, 1:2]
                                     ).then_inc(on["query_rounded"].sem, 1)

                    def denominators(Q):
                        e.wait_ge(on["denominators_ready"].sem, on["denominators_ready"].at(Q + 1))
                        e.wait_ge(on["row_free"].sem, on["row_free"].at(Q))
                        e.copy(denrow[:], X[0:1, 0:HALF]).then_inc(on["denominators_read"].sem, 1)

                    def set_maxima(Q):
                        e.wait_ge(on["maximum_moved"].sem, on["maximum_moved"].at(Q + 1))
                        e.copy(qnext[C:C + 1, :], X[C:C + 1, 0:HALF]).then_inc(on["maximum_set"].sem, 1)

                    def image(b):
                        for t in range(QT):
                            at = slice(t * HALF, (t + 1) * HALF)
                            e.wait_ge(on["keys_ready"].sem, on["keys_ready"].at(QT * b + t + 1))
                            e.activation(khi[:, at], S[t % 4][:, 0:HALF], ACT.Identity, bias=bias2[:, 0:1])
                            e.activation(kst[0:C, at], S[t % 4][0:C, 0:HALF], ACT.Identity, bias=bias2[0:C, 0:1]
                                         ).then_inc(on["keys_rounded"].sem, 1)
                            if t >= 3:
                                e.wait_ge(on["values_ready"].sem, on["values_ready"].at(4 * b + t - 2))
                                e.copy(vst[:, 7 * t - 21:7 * t - 14], M[(t - 3) % 2][0:TP, 0:7 * C].rearrange("t (x c) -> t x c", c=C)
                                       ).then_inc(on["values_evacuated"].sem, 1)
                            if t == 3:
                                query(b * QT)
                        set_maxima(b * QT)

                    def tile(b, q, Q, U, first, late, then):
                        for t in range(KT):
                            if late and t < KBIAS:
                                e.wait_ge(on["scores_biased"].sem, on["scores_biased"].at(late_tiles(b, q) * KBIAS + t + 1))
                                x = biased[:, t % 2]
                            else:
                                e.wait_ge(on["attn_scored"].sem, on["attn_scored"].at(U + t + 1))
                                x = S[t % 4][0:TP, 0:HALF]
                            free = on["summed_gpsimd" if t % 2 else "summed_vector"]
                            e.wait_ge(free.sem, free.at(KT // 2 * Q + t // 2 + 1))
                            e.activation(pexp[:, t % 4], x, ACT.Exp).then_inc(on["attn_exponentials"].sem, 1)
                            if t == 1 and not first:
                                denominators(Q - 1)
                            if then is not None and t == 3:
                                query(Q + 1)
                            if then is not None and t == KT - 3:
                                set_maxima(Q + 1)
                        if then is None:
                            denominators(Q)
                    loop_tiles(e, image, tile)

                @block.vector
                def _(e):
                    e.nop(nofuse=True).then_inc(on["tile_maximum"].sem, 2)
                    e.nop(nofuse=True).then_inc(on["summed_vector"].sem, 2)

                    def split(Q):
                        e.wait_ge(on["query_rounded"].sem, on["query_rounded"].at(Q + 1))
                        e.scalar_tensor_tensor(qsplit[C:, :], X[C:, 0:HALF], bias2[C:, 1:2], qsplit[C:, :],
                                               ALU.add, ALU.subtract).then_inc(on["queries_split"].sem, 1)

                    def maximum(b, q, U, late, s, t):
                        e.wait_ge(on["tile_scored"].sem, on["tile_scored"].at(U + 7 * s + t + 1))
                        x = M[(7 * s + t) % 2][0:TP, 0:HALF]
                        if late and t < 3:
                            e.nop(nofuse=True)
                            e.tensor_tensor(forward[:, (7 * s + t) % 2], x, biasQ[:, bass.ds(TP * (KT - 1) - HALF * q - TP * s + HALF * t, HALF)],
                                            ALU.add).then_inc(on["tile_biased"].sem, 1)
                            e.wait_ge(on["tile_biased"].sem, on["tile_biased"].at(late_tiles(b, q) * 12 + 3 * s + t + 1))
                            x = forward[:, (7 * s + t) % 2]
                        e.tensor_reduce(out=tmx[:, s, t:t + 1], in_=x, axis=AX, op=ALU.max).then_inc(on["tile_maximum"].sem, 1)

                    def row_maxima(Q):
                        e.wait_ge(on["tile_maximum"].sem, on["tile_maximum"].at(KT * (Q + 1) + 2))
                        e.tensor_reduce(out=rmx[:], in_=tmx[:], axis=AX, op=ALU.max).then_inc(on["maxima_ready"].sem, 1)
                        e.wait_ge(on["maxima_ready"].sem, on["maxima_ready"].at(Q + 1))
                        e.tensor_scalar(nmx[:], rmx[:], -1.0, None, ALU.mult).then_inc(on["row_maximum"].sem, 1)

                    def set_query(Q):
                        e.wait_ge(on["maximum_set"].sem, on["maximum_set"].at(Q + 1))
                        e.tensor_copy(qst[0:C + 1, :], qnext[:]).then_inc(on["query_set"].sem, 1)

                    def image(b):
                        e.wait_ge(on["values_ready"].sem, on["values_ready"].at(4 * b))
                        e.nop(nofuse=True)
                        e.tensor_copy(tok[0:C, :], hT[0:C, b, :]).then_inc(on["tokens_staged"].sem, 1)
                        for t in range(QT):
                            at = slice(t * HALF, (t + 1) * HALF)
                            e.wait_ge(on["keys_rounded"].sem, on["keys_rounded"].at(QT * b + t + 1))
                            e.scalar_tensor_tensor(klo[:, at], S[t % 4][:, 0:HALF], bias2[:, 0:1], khi[:, at], ALU.add, ALU.subtract
                                                   ).then_inc(on["keys_evacuated"].sem, 1)
                        split(b * QT)
                        for s in range(4):
                            for t in range(QT):
                                maximum(b, 0, b * QT * KT, False, s, t)
                        row_maxima(b * QT)
                        set_query(b * QT)

                    def tile(b, q, Q, U, first, late, then):
                        def bias(q, U, late, t):
                            if late and t < KBIAS:
                                e.wait_ge(on["attn_scored"].sem, on["attn_scored"].at(U + t + 1))
                                e.wait_ge(on["attn_exponentials"].sem, on["attn_exponentials"].at(U + t + 3))
                                e.nop(nofuse=True)
                                e.tensor_tensor(biased[:, t % 2], S[t % 4][0:TP, 0:HALF],
                                                biasT[:, bass.ds(HALF * q - TP * t - 784, HALF)], ALU.add
                                                ).then_inc(on["scores_biased"].sem, 1)
                        for step in range(KT // 2):
                            t = 2 * step
                            bias(q, U, late, t + 2)
                            e.wait_ge(on["attn_exponentials"].sem, on["attn_exponentials"].at(U + t + 5))
                            if step == 0:
                                e.wait_ge(on["denominators_ready"].sem, on["denominators_ready"].at(Q))
                                e.tensor_copy(psum[:, 0], pexp[:, 0]).then_inc(on["summed_vector"].sem, 1)
                            else:
                                e.wait_ge(on["summed_vector"].sem, on["summed_vector"].at(KT // 2 * Q + step + 2))
                                e.tensor_tensor(psum[:, 0], psum[:, 0], pexp[:, t % 4], ALU.add).then_inc(on["summed_vector"].sem, 1)
                            bias(q, U, late, t + 3)
                            if then is not None:
                                if step == AHEAD[0] - 1:
                                    split(Q + 1)
                                for s, k in ahead_in(step):
                                    maximum(b, q + 1, U + KT, then, s, k)
                                if step == AHEAD[1]:
                                    row_maxima(Q + 1)
                                if step == KT // 2 - 2:
                                    e.wait_ge(on["attn_scored"].sem, on["attn_scored"].at(U + KT))
                                    set_query(Q + 1)
                        if then is not None:
                            bias(q + 1, U + KT, then, 0)
                            bias(q + 1, U + KT, then, 1)
                        e.wait_ge(on["attn_weighted"].sem, on["attn_weighted"].at(U + KT))
                        e.nop(nofuse=True)
                        e.tensor_copy(hT[:, b, bass.ds(q * HALF, HALF)], O[:, 0:HALF]).then_inc(on["attn_evacuated"].sem, 1)
                    loop_tiles(e, image, tile)
            u, Q = B * QT * KT, B * QT
            late = B * (QT - QFLAT)
            ended(tokens_staged=B, values_ready=4 * B, values_evacuated=4 * B, keys_ready=Q, keys_evacuated=Q, keys_rounded=Q,
                  query_ready=Q, query_rounded=Q, queries_split=Q, tile_scored=u, tile_maximum=u + 2, tile_biased=12 * late,
                  maxima_ready=Q, row_maximum=Q, maximum_moved=Q, maximum_set=Q, query_set=Q, attn_scored=u,
                  attn_exponentials=u + 4, attn_weighted=u, attn_evacuated=Q, scores_biased=KBIAS * late,
                  summed_vector=u // 2 + 2, summed_gpsimd=u // 2 + 2, denominators_ready=Q, denominators_read=Q,
                  denominators_stored=16 * Q, row_free=Q)

            ysb = psb("attn_out", [128, 2, HALF])
            raw = psb("attn_raw", [TP, 2, GW, C])
            den = psb("den", [TP, PAIRS * HW])
            rden = psb("attn_rden", [TP, PAIRS * HW])
            gained = psb("attn_gained", [TP, GW, C])
            with nc.Block() as block:
                @block.sync
                def _(e):
                    for p in range(PAIRS):
                        for b in range(2):
                            e.dma_start(den[HW * b:HW * (b + 1), p * HW:(p + 1) * HW],
                                        d["dens"][(2 * p + b) * N:(2 * p + b + 1) * N].rearrange("(h w) -> h w", w=HW)
                                        ).then_inc(on["tables_loaded"].sem, 16)

                @block.tensor
                def _(e):
                    def body(n, p, w, p1, w1):
                        e.wait_ge(on["outputs_evacuated"].sem, on["outputs_evacuated"].at(n))
                        e.nop(nofuse=True)
                        for half in range(2):
                            last = e.matmul(bank[2 * p + half][0:C, 0:HALF].rearrange("c (w b h) -> c w b h", w=4, b=2), awp[:],
                                            hT[:, 2 * p:2 * p + 2, :].rearrange("c b (h w) -> c w b h", w=HW)[:, bass.ds(w + 4 * half, 4)],
                                            start=True, stop=True)
                        last.then_inc(on["outputs_ready"].sem, 1)
                        e.wait_ge(on["outputs_evacuated"].sem, on["outputs_evacuated"].at(n + 1))
                        e.wait_ge(on["outputs_normalised"].sem, on["outputs_normalised"].at(n))
                        for x in range(4):
                            last = e.transpose(bank[4 + p][0:TP, 128 * x:128 * (x + 1)], ysb[:, p, TP * x:TP * (x + 1)], ident[:])
                        last.then_inc(on["projected"].sem, 1)
                    loop_groups(e, body)

                @block.scalar
                def _(e):
                    def body(n, p, w, p1, w1):
                        e.wait_ge(on["outputs_ready"].sem, on["outputs_ready"].at(n + 1))
                        e.copy(ysb[0:C, p], bank[2 * p][0:C, 0:HALF])
                        e.copy(ysb[C:, p], bank[2 * p + 1][0:C, 0:HALF]).then_inc(on["outputs_evacuated"].sem, 1)
                        norm_scalar(e, p, n)
                    loop_groups(e, body)

                @block.vector
                def _(e):
                    e.wait_ge(on["tables_loaded"].sem, on["tables_loaded"].at(16 * B))
                    e.reciprocal(rden[:], den[:]).then_inc(on["weights_scaled"].sem, 1)
                    e.wait_ge(on["weights_scaled"].sem, on["weights_scaled"].at(1))
                    e.tensor_scalar(rden[:], rden[:], col("scale", 0, TP), None, ALU.mult).then_inc(on["weights_scaled"].sem, 1)
                    e.wait_ge(on["weights_scaled"].sem, on["weights_scaled"].at(2))

                    def take(n, p, w):
                        e.wait_ge(on["projected"].sem, on["projected"].at(n + 1))
                        e.nop(nofuse=True)
                        e.tensor_tensor(raw[:, p].rearrange("t (h w) c -> t h w c", h=2),
                                        bank[4 + p][0:TP, :].rearrange("t (w h c) -> t h w c", h=2, c=C),
                                        rden[:, bass.ds(p * HW + w, GW)].rearrange("t (h w) -> t h w", h=2).unsqueeze(3)
                                        .broadcast_to([TP, 2, 4, C]), ALU.mult).then_inc(on["outputs_normalised"].sem, 1)
                        e.wait_ge(on["outputs_normalised"].sem, on["outputs_normalised"].at(n + 1))
                        e.tensor_tensor(raw[:, p], raw[:, p], row("apb"), ALU.add).then_inc(on["projection_biased"].sem, 1)
                        e.wait_ge(on["projection_biased"].sem, on["projection_biased"].at(n + 1))
                        norm_centre(e, raw[:, p], p, n)
                    take(0, 0, 0)

                    def body(n, p, w, p1, w1):
                        norm_variance(e, n)
                        if p1 is not None:
                            take(n + 1, p1, w1)
                        norm_scale(e, p, n, freed=(on["gain_applied"], n))
                    loop_but_last(e, body)

                @block.gpsimd
                def _(e):
                    def body(n, p, w, p1, w1):
                        norm_gpsimd(e, n)
                        e.wait_ge(on["normalised"].sem, on["normalised"].at(n + 1))
                        e.tensor_tensor(gained[:], normed[:, p], row("a2g"), ALU.mult).then_inc(on["gain_applied"].sem, 1)
                        e.wait_ge(on["gain_applied"].sem, on["gain_applied"].at(n + 1))
                        e.tensor_tensor(gained[:], gained[:], row("a2b"), ALU.add).then_inc(on["output_ready"].sem, 1)
                        e.wait_ge(on["output_ready"].sem, on["output_ready"].at(n + 1))
                        e.nop(nofuse=True)
                        e.tensor_tensor(group(p, w), group(p, w), gained[:], ALU.add).then_inc(on["residual_added"].sem, 1)
                        e.wait_ge(on["residual_added"].sem, on["residual_added"].at(n + 1))
                    loop_groups(e, body)
            G = 2 * GROUPS
            norm_ended(G, G)
            ended(outputs_ready=G, outputs_evacuated=G, gain_applied=G, output_ready=G, residual_added=G, projected=G,
                  tables_loaded=16 * B, weights_scaled=2, outputs_normalised=G, projection_biased=G)
        with ExitStack() as part:
            def psb(name, shape, dt=F32):
                return part.enter_context(nc.sbuf_tensor(name, shape, dt))

            wr, ew1, ew2 = psb("wr", [AK, E]), psb("ew1", [AK, E, HID]), psb("ew2", [HID, E, C])
            eb2, number = psb("eb2", [128, E // 2]), psb("number", [TP, E])
            xn = psb("xn", [AK, GW, TP])
            hid = psb("ehid", [HID, 2, E, HALF])
            lg, top = psb("lg", [TP, GW, E]), psb("top", [TP, GW, E])
            at = psb("at", [TP, GW, E], U32)
            atf = psb("atf", [TP, GW, 2])
            lead, tanh = psb("lead", [TP, GW]), psb("tanh", [TP, GW])
            share = psb("share", [TP, 2, GW])
            one = psb("one", [TP, 2, GW, E])
            gate = psb("gate", [TP, 2, GW, E])
            ysb = psb("ysb", [128, 2, E // 2, HALF])
            yw = psb("yw", [TP, 2, E * C])
            mix = psb("mix", [TP, 2, GW, C])
            STEPS = 8
            TANH_AT = 5

            with nc.Block() as block:
                @block.sync
                def _(e):
                    for to, src in ((wr, d["wr"]), (ew1, d["ew1"]), (ew2, d["ew2"]),
                                    (eb2, d["eb2"]),
                                    (number, d["number"].unsqueeze(0).broadcast_to([TP, E]))):
                        e.dma_start(to[:], src).then_inc(on["tables_loaded"].sem, 16)
                    e.wait_ge(on["tables_loaded"].sem, on["tables_loaded"].at(16 * 5))

                @block.gpsimd
                def _(e):
                    e.memset(xn[C:AK], 0.0).then_inc(on["ones_set"].sem, 1)
                    e.wait_ge(on["ones_set"].sem, on["ones_set"].at(1))
                    e.memset(xn[C:C + 1], 1.0).then_inc(on["ones_set"].sem, 1)
                    e.wait_ge(on["ones_set"].sem, on["ones_set"].at(2))
                    norm_squares(e, 0, 0)
                    norm_gpsimd(e, 0)

                    def body(n, p, w, p1, w1):
                        norm_squares(e, p1, n + 1)
                        norm_gpsimd(e, n + 1)
                        e.wait_ge(on["mixed"].sem, on["mixed"].at(GW * (n + 1)))
                        e.nop(nofuse=True)
                        e.tensor_tensor(group(p, w), group(p, w), mix[:, p], ALU.add).then_inc(on["residual_added"].sem, 1)
                    loop_groups(e, body)

                @block.vector
                def _(e):
                    norm_vector(e, group(0, 0), 0, 0, weight=1 + EPS, extra=EPS ** 2)
                    e.wait_ge(on["tables_loaded"].sem, on["tables_loaded"].at(16 * 5))
                    e.nop(nofuse=True).then_inc(on["expert_weighted"].sem, 2)

                    def body(n, p, w, p1, w1):
                        step = STEPS * n
                        e.wait_ge(on["gate_scored"].sem, on["gate_scored"].at(n + 1))
                        e.tensor_copy(lg[:].rearrange("t w e -> t (w e)"), bank[2][0:TP, 0:GW * E]).then_inc(on["gate_step"].sem, 1)
                        e.wait_ge(on["gate_step"].sem, on["gate_step"].at(step + 1))
                        e.nop(nofuse=True)
                        for x in range(GW):
                            last = e.max(top[:, x], lg[:, x])
                        last.then_inc(on["gate_step"].sem, 1)
                        e.wait_ge(on["gate_step"].sem, on["gate_step"].at(step + 2))
                        e.tensor_tensor(lead[:], top[:, :, 0], top[:, :, 1], ALU.subtract).then_inc(on["lead_ready"].sem, 1)
                        for x in range(GW):
                            last = e.max_index(at[:, x], top[:, x], lg[:, x])
                        last.then_inc(on["gate_step"].sem, 1)
                        e.wait_ge(on["gate_step"].sem, on["gate_step"].at(step + 3))
                        e.tensor_copy(atf[:], at[:, :, 0:2]).then_inc(on["gate_step"].sem, 1)
                        e.wait_ge(on["gate_step"].sem, on["gate_step"].at(step + 4))
                        e.wait_ge(on["tanh_ready"].sem, on["tanh_ready"].at(n + 1))
                        for i in range(2):
                            last = e.tensor_scalar(share[:, i], tanh[:], 0.5 - i, 0.5, ALU.mult, ALU.add)
                        last.then_inc(on["gate_step"].sem, 1)
                        for i in range(2):
                            last = e.tensor_tensor(one[:, i], number[:].unsqueeze(1).broadcast_to([TP, GW, E]),
                                                   atf[:, :, i].unsqueeze(2).broadcast_to([TP, GW, E]), ALU.is_equal)
                        last.then_inc(on["gate_step"].sem, 1)
                        e.wait_ge(on["gate_step"].sem, on["gate_step"].at(step + 6))
                        for i in range(2):
                            last = e.tensor_tensor(one[:, i], one[:, i], share[:, i].unsqueeze(2).broadcast_to([TP, GW, E]), ALU.mult)
                        last.then_inc(on["gate_step"].sem, 1)
                        e.wait_ge(on["gate_step"].sem, on["gate_step"].at(step + 7))
                        e.tensor_tensor(gate[:, p], one[:, 0], one[:, 1], ALU.add).then_inc(on["gate_step"].sem, 1)
                        e.wait_ge(on["gate_step"].sem, on["gate_step"].at(step + 8))

                        e.nop(nofuse=True)
                        norm_vector(e, group(p1, w1), p1, n + 1, freed=(on["transposed"], 2 * n), weight=1 + EPS, extra=EPS ** 2)

                        def weight(x):
                            e.wait_ge(on["experts_done"].sem, on["experts_done"].at(GW * n + x + 1))
                            e.wait_ge(on["mixed"].sem, on["mixed"].at(GW * n + max(x - 1, 0)))
                            e.tensor_tensor(yw[:, x % 2].rearrange("t (e c) -> t e c", e=E),
                                                 bank[6 + x % 2][0:TP, :].rearrange("t (e c) -> t e c", e=E),
                                                 gate[:, p, x].unsqueeze(2).broadcast_to([TP, E, C]), ALU.mult).then_inc(on["expert_weighted"].sem, 1)
                        weight(0)
                        e.wait_ge(on["residual_added"].sem, on["residual_added"].at(n))
                        for x in range(GW):
                            if x + 1 < GW:
                                weight(x + 1)
                            e.wait_ge(on["expert_weighted"].sem, on["expert_weighted"].at(GW * n + x + 3))
                            e.tensor_reduce(out=mix[:, p, x], in_=yw[:, x % 2].rearrange("t (e c) -> t c e", e=E), axis=AX,
                                                 op=ALU.add).then_inc(on["mixed"].sem, 1)
                    loop_groups(e, body)

                @block.scalar
                def _(e):
                    e.nop(nofuse=True).then_inc(on["expert_gelu"].sem, 2)

                    def evacuate_tokens(n):
                        for half in range(2):
                            e.wait_ge(on["transposed"].sem, on["transposed"].at(2 * n + half + 1))
                            e.activation(xn[0:C, 4 * half:4 * half + 4].rearrange("c w t -> c (w t)"), bank[half][0:C, 0:HALF],
                                              ACT.Identity, scale=col("fg"), bias=col("fb")).then_inc(on["evacuated"].sem, 1)

                    def evacuate_outputs(n, k):
                        e.wait_ge(on["outputs_ready"].sem, on["outputs_ready"].at(E * n + k + 1))
                        e.activation(ysb[:, k // 4, k % 4], bank[5][:, 0:HALF], ACT.Identity, bias=eb2[:, k % 4:k % 4 + 1]
                                     ).then_inc(on["outputs_evacuated"].sem, 1)

                    evacuate_tokens(0)

                    def body(n, p, w, p1, w1):
                        for i in range(2 * E):
                            e.wait_ge(on["expert_hidden"].sem, on["expert_hidden"].at(2 * E * n + i + 1))
                            e.activation(hid[:, i // E, i % E], bank[3 + i % 2][:, 0:HALF], ACT.Gelu,
                                              bias=col(f"eb{i % E}", 0, 128)).then_inc(on["expert_gelu"].sem, 1)
                            if i >= 3 and i % 2:
                                evacuate_outputs(n, (i - 3) // 2)
                            if i == TANH_AT:
                                e.wait_ge(on["lead_ready"].sem, on["lead_ready"].at(n + 1))
                                e.activation(tanh[:], lead[:], ACT.Tanh, scale=0.5).then_inc(on["tanh_ready"].sem, 1)
                        evacuate_tokens(n + 1)
                        evacuate_outputs(n, E - 1)
                    loop_groups(e, body)

                @block.tensor
                def _(e):
                    e.wait_ge(on["tables_loaded"].sem, on["tables_loaded"].at(16 * 5))
                    e.wait_ge(on["ones_set"].sem, on["ones_set"].at(2))

                    def hidden(n, i):
                        half, x = divmod(i, E)
                        e.wait_ge(on["expert_gelu"].sem, on["expert_gelu"].at(2 * E * n + i + 1))
                        e.matmul(bank[3 + i % 2][:, 0:HALF], ew1[:, x], xn[:, 4 * half:4 * half + 4].rearrange("c w t -> c (w t)"),
                                 start=True, stop=True).then_inc(on["expert_hidden"].sem, 1)

                    def outputs(n, k):
                        half, j = divmod(k, E // 2)
                        e.wait_ge(on["expert_gelu"].sem, on["expert_gelu"].at(2 * E * n + 2 * k + 4))
                        e.wait_ge(on["outputs_evacuated"].sem, on["outputs_evacuated"].at(E * n + k))
                        for i in range(2):
                            last = e.matmul(bank[5][C * i:C * (i + 1), 0:HALF], ew2[:, 2 * j + i], hid[:, half, 2 * j + i],
                                            start=True, stop=True)
                        last.then_inc(on["outputs_ready"].sem, 1)

                    def by_token(n, x):
                        e.wait_ge(on["outputs_evacuated"].sem, on["outputs_evacuated"].at(E * n + (4 if x < 4 else 8)))
                        e.wait_ge(on["expert_weighted"].sem, on["expert_weighted"].at(GW * n + x + 1))
                        for j in range(E // 2):
                            last = e.transpose(bank[6 + x % 2][0:TP, 128 * j:128 * (j + 1)],
                                               ysb[:, x // 4, j, TP * (x % 4):TP * (x % 4 + 1)], ident[:])
                        last.then_inc(on["experts_done"].sem, 1)

                    transpose_group(e, 0, 0)

                    def body(n, p, w, p1, w1):
                        e.wait_ge(on["evacuated"].sem, on["evacuated"].at(2 * n + 2))
                        e.wait_ge(on["lead_ready"].sem, on["lead_ready"].at(n))
                        for x in range(GW):
                            last = e.matmul(bank[2][0:TP, E * x:E * (x + 1)], xn[:, x], wr[:], start=True, stop=True)
                        last.then_inc(on["gate_scored"].sem, 1)
                        for i in range(2 * E):
                            hidden(n, i)
                            if i >= 3 and i % 2:
                                outputs(n, (i - 3) // 2)
                            if i >= 12:
                                by_token(n, i - 12)
                        transpose_group(e, p1, n + 1)
                        outputs(n, E - 1)
                        for x in range(4, GW):
                            by_token(n, x)
                    loop_groups(e, body)
            G = 2 * GROUPS
            norm_ended(G + 1, G + 1)
            ended(tables_loaded=16 * 5, ones_set=2, transposed=2 * G + 2, evacuated=2 * G + 2)

        with nc.Block() as block:
            @block.sync
            def _(e):
                for p in range(PAIRS):
                    for b in range(2):
                        e.dma_start(out[2 * p + b].rearrange("(h w) c -> h w c", w=HW),
                                         xr[HW * b:HW * (b + 1), p * HW:(p + 1) * HW, :]).then_inc(on["stored"].sem, 16)
                e.wait_ge(on["stored"].sem, on["stored"].at(16 * B))


def layouts(i):
    import numpy as np
    t = {k: np.asarray(v) for k, v in i.items()}
    T = lambda k: t["L0_tok_" + k]
    A = lambda k: t["L0_attn_" + k]
    FF = lambda k: t["L0_ffn_" + k]
    f = np.float32
    vec = {"ag": A("ln1_g"), "ab": A("ln1_b"),
           "fg": FF("gamma"), "fb": FF("beta"),
           "scale": np.broadcast_to(A("scale").reshape(1), (128,)),
           "last": np.broadcast_to(A("bias_table")[-1:], (128,))}
    for l in range(BLOCKS):
        vec |= {f"n1g{l}": T("n1g")[l], f"n1b{l}": T("n1b")[l], f"n2g{l}": T("n2g")[l], f"n2b{l}": T("n2b")[l],
                f"qb{l}": T("qkv_b")[l, 0:C], f"kb{l}": T("qkv_b")[l, C:2 * C]}
        vec[f"b2{l}"] = np.concatenate([T("b2")[l]] * 2, 0)
        for q in range(2):
            vec[f"mb{l}{q}"] = T("b1")[l, 128 * q:128 * (q + 1)]
    for q in range(E):
        vec[f"eb{q}"] = FF("b1")[q]
    cols = np.zeros((128, len(COLS)), f)
    for n, k in enumerate(COLS):
        cols[:len(vec[k]), n] = vec[k]
    rows = np.stack([T("pe_b"), T("pe_ng"), T("pe_nb"), A("proj_b"), A("ln2_g"), A("ln2_b")])
    pew = np.zeros((GW, 16, GW, C), f)
    for w in range(GW):
        pew[w, :, w, :] = T("pe_w").reshape(C, 16).T
    wv = np.concatenate([T("qkv_w")[:, 2 * C:].transpose(2, 0, 1), T("qkv_b")[:, 2 * C:][None]], 0)
    pw = np.zeros((HP, 32, BLOCKS, C), f)
    pw[:, 0:16] = T("proj_w").transpose(2, 0, 1).reshape(HP, 16, BLOCKS, C)
    pw[0, 16] = T("proj_b")
    c, r = np.divmod(np.arange(WN), WS)
    rel = (r[:, None] - r[None, :] + WS - 1) * (2 * WS - 1) + c[:, None] - c[None, :] + WS - 1
    edge = lambda x: (x >= WS - SHIFT).astype(int)
    masks = np.stack([np.where(g[:, None] != g[None, :], f(-100), f(0))
                      for g in (edge(r), edge(c), 2 * edge(r) + edge(c))], 1)
    sel = np.zeros((128, 128), f)
    for q in range(128):
        hp, j = divmod(q, 32)
        sel[32 * hp + (17 if 8 <= j < 16 or j == 17 else 16), q] = 1
    heads = np.zeros((C, NH), f)
    vmask = np.zeros((128, 16), f)
    for h in range(NH):
        heads[HD * h:HD * (h + 1), h] = 1
    vmask[0:64, 0:8] = 1
    vmask[64:128, 8:16] = 1
    table = A("bias_table")
    ext = table[TAB - 1 - np.clip(np.arange(2352 + TP) - 1440, 0, TAB - 1)]
    extq = table[np.clip(np.arange(2576 + TP), 0, TAB - 1)]
    x = {"cols": cols, "rows": rows, "ident": np.eye(128, dtype=f), "pew": pew.reshape(128, GW * C),
         "wqk": T("qkv_w")[:, 0:2 * C].transpose(2, 0, 1), "wv": wv, "pw": pw.reshape(128, BLOCKS, C),
         "w1": np.concatenate([T("w1").transpose(2, 0, 1), np.zeros((AK - C, BLOCKS, 2 * HID), f)], 0), "w2": T("w2").transpose(2, 0, 1).reshape(2, 128, BLOCKS, C).transpose(1, 2, 0, 3),
         "awq": A("qkv_w")[:, 0:C], "awk": A("qkv_w")[:, C:2 * C],
         "awv": np.concatenate([A("qkv_w")[:, 2 * C:], A("qkv_b")[2 * C:][None]], 0), "awp": np.concatenate([A("proj_w")] * 2, 0),
         "rpb": T("rpb")[:, rel].transpose(1, 0, 3, 2), "masks": masks, "sel": sel, "heads": heads, "vmask": vmask,
         "wr": np.concatenate([FF("Wr"), FF("br")[None], np.zeros((AK - C - 1, E), f)], 0),
         "ew1": np.concatenate([FF("W1").transpose(1, 0, 2), np.zeros((AK - C, E, HID), f)], 0),
         "ew2": FF("W2").transpose(1, 0, 2), "eb2": FF("b2").reshape(E // 2, 128).T,
         "ext": ext, "flip": np.eye(TP, dtype=f)[::-1], "bias2": np.stack([A("qkv_b")[C:2 * C], A("qkv_b")[0:C]], 1), "extq": extq, "number": np.arange(E, dtype=f)}
    return x


def kernel(**inputs):
    import numpy as np
    import concourse.bacc as bacc
    from concourse.bass_utils import run_bass_kernel_spmd as run

    nc = bacc.Bacc("TRN2", target_bir_lowering=False, num_devices=1)
    arrays = {f"in_{k}": np.ascontiguousarray(v) for k, v in layouts(inputs).items()}
    arrays["in_x"] = np.ascontiguousarray(inputs["x"])
    dram = {k: nc.dram_tensor(k, v.shape, mybir.dt.from_np(v.dtype), kind="ExternalInput").ap() for k, v in arrays.items()}
    out = nc.dram_tensor("out", (B, N, C), F32, kind="ExternalOutput").ap()
    build(nc, dram["in_x"], out, {k[3:]: v for k, v in dram.items()})
    return run(nc, [arrays], core_ids=[0]).results[0]["out"]
```

```python
import concourse.bass as bass
from concourse import mybir
from contextlib import ExitStack

F32 = mybir.dt.float32
BF16 = mybir.dt.bfloat16
U32 = mybir.dt.uint32
ALU = mybir.AluOpType
ACT = mybir.ActivationFunctionType
AX = mybir.AxisListType.X

B, HW, C = 4, 56, 64
PAIRS = B // 2
TP = 2 * HW
GW = 8
GROUPS = HW // GW
HALF = GW // 2 * TP
WS, NH, HD = 7, 8, 8
WN = WS * WS
NW = HW // WS
SHIFT = WS // 2
SCALE = HD ** -0.5
SLOT = 64
YW, YH = 66, 59
HP = NH // 2
N = HW * HW
KT = N // TP
QT = N // HALF
QFLAT = 4
KBIAS = 10
TAB = 1023
AK = 96
E, HID = 8, 128
EPS = 1e-5
BLOCKS = 2

COLS = (["n1g0", "n1b0", "n1g1", "n1b1", "n2g0", "n2b0", "n2g1", "n2b1", "qb0", "kb0", "qb1", "kb1",
         "ag", "ab", "fg", "fb", "scale", "last", "b20", "b21"]
        + [f"mb{l}{f}" for l in range(2) for f in range(2)] + [f"eb{e}" for e in range(E)])
ROWS = ["peb", "peg", "pen", "apb", "a2g", "a2b"]

LOADS = {
    "denominators_stored": "a query tile's denominators are in DRAM",
    "image_loaded": "pixels and the embedding's weights",
    "constants_loaded": "constants",
    "tables_loaded": "a stage's tables",
    "mlp_weights_loaded": "the MLP's weights",
    "stored": "the result is in DRAM",
}
SIGNALS = {
    "summed_vector": "VectorE: an even key tile's exponentials are added up",
    "summed_gpsimd": "GpSimd: an odd key tile's exponentials are added up",
    "row_free": "SyncE: the row of denominators is in DRAM",
    "sums_joined": "GpSimd: both engines' sums are added up",
    "query_set": "VectorE: the next query tile is in the products' buffer",
    "attn_evacuated": "ScalarE: a query tile's outputs and denominators are in SBUF",
    "attn_exponentials": "ScalarE: a key tile's exponentials are in SBUF",
    "attn_scored": "TensorE: a key tile's scores less the maxima",
    "attn_weighted": "TensorE: a key tile's values are added to the outputs",
    "bias_flipped": "TensorE: a piece of the Toeplitz bias is turned round",
    "bias_set": "VectorE: bias rows or pieces are in place",
    "centred": "VectorE: a group less its means",
    "cleared": "GpSimd: padding and fixed rows are set",
    "conv_biased": "VectorE: a group's patch embedding is in the residual stream, before its norm",
    "convolved": "TensorE: a group's patch embedding",
    "denominators_read": "VectorE: reciprocals of the denominators",
    "denominators_ready": "TensorE: the denominators on their heads' partitions",
    "embedded": "GpSimd: a group's normalised embedding is in the residual stream",
    "evacuated": "ScalarE: a channel-major half group with its gain and bias",
    "expert_gelu": "ScalarE: an expert's hidden activations",
    "expert_hidden": "TensorE: an expert's hidden layer",
    "expert_weighted": "VectorE: a column's expert outputs times their gates",
    "experts_done": "TensorE: a column's expert outputs",
    "exponentials_ready": "ScalarE: a pair of windows' exponentials",
    "gain_applied": "GpSimd or VectorE: a group times its gain",
    "gate_scored": "TensorE: a group's router logits",
    "gate_step": "VectorE: a step of the gating",
    "gelu_done": "ScalarE: half of the hidden activations of a half group",
    "hidden_ready": "TensorE: half of the hidden layer of a half group",
    "keys_by_head": "GpSimd: a chunk's keys, block-diagonal by head",
    "keys_evacuated": "the keys have left PSUM",
    "keys_ready": "TensorE: a tile of keys",
    "keys_rounded": "ScalarE: a key tile's high part, and the tile itself",
    "lead_ready": "VectorE: the first logit less the second",
    "maxima_ready": "VectorE: maxima of rows of scores",
    "maximum_moved": "TensorE: the maxima as a row",
    "maximum_set": "ScalarE: that row is below the queries",
    "mean_ready": "VectorE: a group's means",
    "mixed": "VectorE: a column's sum over experts",
    "mlp_ready": "TensorE: a group's MLP output",
    "normalised": "VectorE: a group's normalised tokens",
    "ones_set": "GpSimd: rows and columns of ones",
    "output_ready": "GpSimd: a group of the attention's output with gain and bias",
    "outputs_evacuated": "ScalarE: a chunk's outputs are in SBUF",
    "outputs_normalised": "VectorE: outputs over their denominators",
    "outputs_ready": "TensorE: a chunk's outputs",
    "outputs_staged": "GpSimd: a group's outputs are in the projection's buffer",
    "patchT_ready": "VectorE: transposed patches are in SBUF",
    "patches_ready": "VectorE: a group's pixels by patch",
    "patches_transposed": "TensorE: a group's patches, transposed",
    "probs_evacuated": "ScalarE: transposed exponentials are in SBUF",
    "exponentials_summed": "VectorE: their sums for a pair of windows",
    "sums_inverted": "VectorE: the sums' reciprocals",
    "probs_normalised": "VectorE: a pair of windows' softmax",
    "probs_transposed": "TensorE: the softmax, transposed",
    "projected": "TensorE: a group's projection",
    "projection_biased": "VectorE: a group's projection with its bias",
    "qbias_ready": "VectorE: the scaled query biases",
    "qk_ready": "TensorE: a chunk's queries and keys",
    "queries_evacuated": "ScalarE: a chunk's queries are in SBUF",
    "queries_split": "VectorE: a query tile's low part",
    "query_ready": "TensorE: a query tile",
    "query_rounded": "ScalarE: a query tile's high part, and the tile itself",
    "residual_added": "a group of the residual stream is up to date",
    "row_maximum": "VectorE: minus the maxima of a query tile",
    "rstd_ready": "GpSimd: a group's reciprocal standard deviations",
    "scores_biased": "VectorE: a key tile's scores with varying bias",
    "scores_ready": "TensorE: a pair of windows' scores",
    "shifted": "VectorE: a pair of windows' scores less their maxima",
    "squared": "ScalarE or GpSimd: squares of a centred group",
    "squares_summed": "VectorE: their sums",
    "summed": "VectorE: a group's sums",
    "tanh_ready": "ScalarE: tanh of half the lead",
    "tile_biased": "VectorE: a score tile with varying bias, for the maximum",
    "tile_maximum": "VectorE: a score tile's row maxima",
    "tile_scored": "TensorE: a score tile for the maximum",
    "tokens_staged": "VectorE: an image's tokens are in the fixed buffer",
    "transposed": "TensorE: a half group, transposed",
    "values_by_head": "ScalarE: a chunk's values, block-diagonal by head",
    "values_evacuated": "ScalarE: seven tiles of values are in SBUF",
    "values_ready": "TensorE: values",
    "variance_ready": "VectorE: a group's variances with epsilon",
    "weights_scaled": "VectorE: reciprocals times the attention's scale",
    "windows_staged": "GpSimd: a chunk's windows are in the fixed buffer",
    "wrapped": "GpSimd: copies at the image's seam",
}



def build(nc, img, out, d):
    d["dens"] = nc.dram_tensor("dens", (B * N,), F32).ap()
    ctx = ExitStack()
    with ctx:
        def sb(name, shape, dt=F32):
            return ctx.enter_context(nc.sbuf_tensor(name, shape, dt))

        class Signal:
            def __init__(self, name):
                self.sem, self.past = ctx.enter_context(nc.semaphore(name)), int(name in SIGNALS)

            def at(self, n):
                return n + self.past

        on = {name: Signal(name) for name in (*LOADS, *SIGNALS)}

        def ended(**counts):
            for name, n in counts.items():
                on[name].past += n

        with nc.Block() as block:
            @block.sync
            def _(e):
                for name in SIGNALS:
                    e.nop(nofuse=True).then_inc(on[name].sem, 1)

        xr = sb("xr", [TP, PAIRS * HW + GW, C])
        ident = sb("ident", [128, 128])
        cols = sb("cols_sb", [128, len(COLS)])
        rows = sb("rows_sb", [TP, len(ROWS), C])
        neghalf = sb("neghalf", [TP, GW])
        cent = sb("cent", [TP, 2, GW, C])
        normed = sb("normed", [TP, 2, GW, C])
        sq = sb("sq", [TP, GW, C])
        stat = sb("stat", [TP, 5, GW])
        bank = [ctx.enter_context(nc.psum_tensor(f"bank{i}", [128, 512], F32)) for i in range(8)]

        def col(name, p0=0, p1=C):
            return cols[p0:p1, COLS.index(name):COLS.index(name) + 1]

        def row(name, n=GW):
            return rows[:, ROWS.index(name), :].unsqueeze(1).broadcast_to([TP, n, C])

        def group(p, w):
            return xr[:, bass.ds(p * HW + w, GW), :]

        def per_token(ap):
            return ap.unsqueeze(2).broadcast_to([TP, GW, C])

        def norm_centre(e, x, k, n):
            e.tensor_reduce(out=stat[:, 0, :], in_=x, axis=AX, op=ALU.add).then_inc(on["summed"].sem, 1)
            e.wait_ge(on["summed"].sem, on["summed"].at(n + 1))
            e.tensor_scalar(stat[:, 1, :], stat[:, 0, :], 1.0 / C, None, ALU.mult).then_inc(on["mean_ready"].sem, 1)
            e.wait_ge(on["mean_ready"].sem, on["mean_ready"].at(n + 1))
            e.tensor_tensor(cent[:, k], x, per_token(stat[:, 1, :]), ALU.subtract).then_inc(on["centred"].sem, 1)

        def norm_variance(e, n, weight=1.0, extra=EPS):
            e.wait_ge(on["squared"].sem, on["squared"].at(n + 1))
            e.tensor_reduce(out=stat[:, 2, :], in_=sq[:], axis=AX, op=ALU.add).then_inc(on["squares_summed"].sem, 1)
            e.wait_ge(on["squares_summed"].sem, on["squares_summed"].at(n + 1))
            e.tensor_scalar(stat[:, 3, :], stat[:, 2, :], weight / C, extra, ALU.mult, ALU.add).then_inc(on["variance_ready"].sem, 1)

        def norm_scale(e, k, n, freed=None):
            e.wait_ge(on["rstd_ready"].sem, on["rstd_ready"].at(n + 1))
            if freed:
                e.wait_ge(freed[0].sem, freed[0].at(freed[1]))
            e.tensor_tensor(normed[:, k], cent[:, k], per_token(stat[:, 4, :]), ALU.mult).then_inc(on["normalised"].sem, 1)

        def norm_squares(e, k, n):
            e.wait_ge(on["centred"].sem, on["centred"].at(n + 1))
            e.tensor_tensor(sq[:], cent[:, k], cent[:, k], ALU.mult).then_inc(on["squared"].sem, 1)

        def norm_vector(e, x, k, n, freed=None, weight=1.0, extra=EPS, squares=False):
            norm_centre(e, x, k, n)
            if squares:
                norm_squares(e, k, n)
            norm_variance(e, n, weight, extra)
            norm_scale(e, k, n, freed)

        def norm_scalar(e, k, n):
            e.wait_ge(on["centred"].sem, on["centred"].at(n + 1))
            e.activation(sq[:], cent[:, k], ACT.Square).then_inc(on["squared"].sem, 1)

        def norm_gpsimd(e, n):
            e.wait_ge(on["variance_ready"].sem, on["variance_ready"].at(n + 1))
            e.tensor_tensor(stat[:, 4, :], stat[:, 3, :], neghalf[:], ALU.pow).then_inc(on["rstd_ready"].sem, 1)

        def norm_ended(n, centred):
            ended(summed=centred, mean_ready=centred, centred=centred, squared=centred, squares_summed=n, variance_ready=n,
                  rstd_ready=n, normalised=n)

        def transpose_group(e, k, n):
            e.wait_ge(on["normalised"].sem, on["normalised"].at(n + 1))
            e.wait_ge(on["evacuated"].sem, on["evacuated"].at(2 * n))
            e.nop(nofuse=True)
            for half in range(2):
                for w in range(4):
                    last = e.transpose(bank[half][0:C, w * TP:(w + 1) * TP], normed[:, k, half * 4 + w, :],
                                       ident[0:TP, 0:TP])
                last.then_inc(on["transposed"].sem, 1)

        def loop_groups(e, body):
            with e.Fori(0, GROUPS) as j:
                body(2 * j, 0, GW * j, 1, GW * j)
                body(2 * j + 1, 1, GW * j, 0, GW * j + GW)

        def loop_but_last(e, body):
            with e.Fori(0, GROUPS - 1) as j:
                body(2 * j, 0, GW * j, 1, GW * j)
                body(2 * j + 1, 1, GW * j, 0, GW * j + GW)
            j = GROUPS - 1
            body(2 * j, 0, GW * j, 1, GW * j)
            body(2 * j + 1, 1, GW * j, None, None)

        def is_last_column(w):
            return isinstance(w, int)

        wqk, wv, pw = sb("wqk", [C, BLOCKS, 128]), sb("wv", [C + 1, BLOCKS, C]), sb("pw", [128, BLOCKS, C])
        awq, awk, awv, awp = sb("awq", [C, C]), sb("awk", [C, C]), sb("awv", [C + 1, C]), sb("awp", [128, C])
        qbias = sb("qbias", [C, BLOCKS])
        loads = [(ident[:], d["ident"]), (cols[:], d["cols"]),
                 (rows[:], d["rows"].unsqueeze(0).broadcast_to([TP, len(ROWS), C])),
                 (wqk[:], d["wqk"]), (wv[:], d["wv"]), (pw[:], d["pw"]),
                 (awq[:], d["awq"]), (awk[:], d["awk"]), (awv[:], d["awv"]), (awp[:], d["awp"])]
        with ExitStack() as part:
            px = part.enter_context(nc.sbuf_tensor("px", [TP, PAIRS, 4, 4 * (HW + GW)], F32))
            patches = part.enter_context(nc.sbuf_tensor("patches", [TP, GW, 16], F32))
            patchT = part.enter_context(nc.sbuf_tensor("patchT", [128, 2, TP], F32))
            gained = part.enter_context(nc.sbuf_tensor("gained", [TP, GW, C], F32))
            pew = part.enter_context(nc.sbuf_tensor("pew", [128, GW * C], F32))
            with nc.Block() as block:
                @block.sync
                def _(e):
                    for p in range(PAIRS):
                        for b in range(2):
                            e.dma_start(px[HW * b:HW * (b + 1), p, :, 0:4 * HW],
                                             img[2 * p + b, 0].rearrange("(h i) w -> h i w", i=4)).then_inc(on["image_loaded"].sem, 16)
                    e.dma_start(pew[:], d["pew"]).then_inc(on["image_loaded"].sem, 16)
                    for to, src in loads:
                        e.dma_start(to, src).then_inc(on["constants_loaded"].sem, 16)

                @block.gpsimd
                def _(e):
                    e.memset(neghalf[:], -0.5).then_inc(on["cleared"].sem, 1)
                    e.memset(px[:, :, :, 4 * HW:], 0.0).then_inc(on["cleared"].sem, 1)
                    e.memset(xr[:, PAIRS * HW:, :], 0.0).then_inc(on["cleared"].sem, 1)
                    e.wait_ge(on["cleared"].sem, on["cleared"].at(3))

                    def body(n, p, w, p1, w1):
                        norm_gpsimd(e, n)
                        e.wait_ge(on["normalised"].sem, on["normalised"].at(n + 1))
                        e.tensor_tensor(gained[:], normed[:, p], row("peg"), ALU.mult).then_inc(on["gain_applied"].sem, 1)
                        e.wait_ge(on["gain_applied"].sem, on["gain_applied"].at(n + 1))
                        e.tensor_tensor(group(p, w), gained[:], row("pen"), ALU.add).then_inc(on["embedded"].sem, 1)
                        e.wait_ge(on["embedded"].sem, on["embedded"].at(n + 1))
                    loop_groups(e, body)

                @block.vector
                def _(e):
                    e.wait_ge(on["image_loaded"].sem, on["image_loaded"].at(16 * 5))
                    e.wait_ge(on["constants_loaded"].sem, on["constants_loaded"].at(16 * len(loads)))
                    e.wait_ge(on["cleared"].sem, on["cleared"].at(3))
                    for l in range(BLOCKS):
                        e.tensor_scalar(qbias[:, l:l + 1], col(f"qb{l}"), SCALE, None, ALU.mult).then_inc(on["qbias_ready"].sem, 1)

                    def take_patches(n, p, w):
                        e.wait_ge(on["patches_transposed"].sem, on["patches_transposed"].at(n))
                        e.tensor_copy(patches[:].rearrange("q w (i j) -> q w i j", i=4),
                                           px[:, p, :, bass.ds(4 * w, 4 * GW)].rearrange("q i (w j) -> q w i j", j=4)).then_inc(on["patches_ready"].sem, 1)
                        e.wait_ge(on["patches_transposed"].sem, on["patches_transposed"].at(n + 1))
                        e.tensor_copy(patchT[:, p], bank[2 + p][:, 0:TP]).then_inc(on["patchT_ready"].sem, 1)

                    def take(n, p, w):
                        e.wait_ge(on["convolved"].sem, on["convolved"].at(n + 1))
                        e.tensor_tensor(group(p, w), bank[4 + p][0:TP, :].rearrange("q (w c) -> q w c", c=C),
                                             row("peb"), ALU.add).then_inc(on["conv_biased"].sem, 1)
                        e.wait_ge(on["conv_biased"].sem, on["conv_biased"].at(n + 1))
                        e.nop(nofuse=True)
                        norm_centre(e, group(p, w), p, n)

                    take_patches(0, 0, 0)
                    take_patches(1, 1, 0)
                    take(0, 0, 0)

                    def body(n, p, w, p1, w1):
                        norm_variance(e, n)
                        if not is_last_column(w):
                            take_patches(n + 2, p, w + GW)
                        if p1 is not None:
                            take(n + 1, p1, w1)
                        norm_scale(e, p, n, freed=(on["gain_applied"], n))
                    loop_but_last(e, body)

                @block.scalar
                def _(e):
                    loop_groups(e, lambda n, p, w, p1, w1: norm_scalar(e, p, n))

                @block.tensor
                def _(e):
                    def convolve(n, p):
                        e.wait_ge(on["patches_ready"].sem, on["patches_ready"].at(n + 1))
                        e.wait_ge(on["patchT_ready"].sem, on["patchT_ready"].at(n))
                        e.transpose(bank[2 + p][:, 0:TP], patches[:].rearrange("q w i -> q (w i)"),
                                         ident[0:TP, 0:TP]).then_inc(on["patches_transposed"].sem, 1)
                        e.wait_ge(on["patchT_ready"].sem, on["patchT_ready"].at(n + 1))
                        e.matmul(bank[4 + p][0:TP, :], patchT[:, p], pew[:], start=True, stop=True).then_inc(on["convolved"].sem, 1)

                    convolve(0, 0)
                    convolve(1, 1)

                    def body(n, p, w, p1, w1):
                        if not is_last_column(w):
                            e.wait_ge(on["conv_biased"].sem, on["conv_biased"].at(n + 1))
                            convolve(n + 2, p)
                    loop_but_last(e, body)
            G = PAIRS * GROUPS
            norm_ended(G, G)
            ended(image_loaded=16 * 5, constants_loaded=16 * len(loads), cleared=3, qbias_ready=2, gain_applied=G,
                  embedded=G, patches_transposed=G, patches_ready=G, patchT_ready=G, conv_biased=G, convolved=G)

        def swin_block(l):
            shift = SHIFT * l
            with ExitStack() as part:
                def psb(name, shape, dt=F32):
                    return part.enter_context(nc.sbuf_tensor(f"{name}_{l}", shape, dt))

                yo = psb("yo", [128, B, YW, YH])
                ywin = psb("ywin", [C + 1, 2, NW, SLOT])
                qwin = psb("qwin", [C + WN, 2, NW, SLOT])
                ksb = psb("ksb", [C, NW, SLOT])
                kbd = psb("kbd", [C + WN, 2, NW, NH, WN])
                vbd = psb("vbd", [128, 2, NW, HP, 32])
                P = psb("P", [128, 4, NH, SLOT])
                pT = psb("pT", [128, 2, 512])
                mx = psb("mx", [128, 2, NH])
                total = psb("total", [128, 2, 2, NH])
                heads = psb("heads", [C, NH])
                rpb = psb("rpb", [C + WN, NH, WN])
                masks = psb("masks", [C + WN, 3, WN])

                with nc.Block() as block:
                    @block.sync
                    def _(e):
                        for to, src in ((heads[:], d["heads"]),
                                        (rpb[C:C + WN], d["rpb"][:, l]), (masks[C:C + WN], d["masks"])):
                            e.dma_start(to, src).then_inc(on["tables_loaded"].sem, 16)
                        for k in range(2):
                            for s in range(NW):
                                e.dma_start(qwin[C:C + WN, k, s, 0:WN], d["ident"][0:WN, 0:WN]).then_inc(on["tables_loaded"].sem, 16)
                        e.wait_ge(on["tables_loaded"].sem, on["tables_loaded"].at(16 * (3 + 2 * NW)))

                    @block.gpsimd
                    def _(e):
                        for i, a in enumerate((ywin[0:C], qwin[:, :, :, WN:], P[:], vbd[:], yo[0:C, :, HW:, :],
                                               yo[0:C, :, 0:HW, HW:])):
                            e.memset(a, 0.0).then_inc(on["cleared"].sem, 1)
                            e.wait_ge(on["cleared"].sem, on["cleared"].at(i + 1))
                        for i, a in enumerate((ywin[C:C + 1], vbd[0:C, :, :, :, 16:17])):
                            e.memset(a, 1.0).then_inc(on["ones_set"].sem, 1)
                            e.wait_ge(on["ones_set"].sem, on["ones_set"].at(i + 1))
                        loop_groups(e, lambda n, p, w, p1, w1: norm_gpsimd(e, n))

                    @block.vector
                    def _(e):
                        norm_centre(e, group(0, 0), 0, 0)

                        def body(n, p, w, p1, w1):
                            norm_variance(e, n)
                            e.nop(nofuse=True)
                            norm_centre(e, group(p1, w1), p1, n + 1)
                            norm_scale(e, p, n, freed=(on["transposed"], 2 * n))
                        loop_groups(e, body)

                    @block.tensor
                    def _(e):
                        loop_groups(e, lambda n, p, w, p1, w1: transpose_group(e, p, n))

                    @block.scalar
                    def _(e):
                        e.wait_ge(on["cleared"].sem, on["cleared"].at(6))
                        norm_scalar(e, 0, 0)

                        def body(n, p, w, p1, w1):
                            norm_scalar(e, p1, n + 1)
                            for half in range(2):
                                e.wait_ge(on["transposed"].sem, on["transposed"].at(2 * n + half + 1))
                                e.nop(nofuse=True)
                                e.activation(yo[0:C, 2 * p:2 * p + 2, bass.ds(w + 4 * half, 4), 0:HW]
                                                  .rearrange("c b w h -> c w b h"),
                                                  bank[half][0:C, 0:HALF].rearrange("c (w b h) -> c w b h", w=4, b=2),
                                                  ACT.Identity, scale=col(f"n1g{l}"), bias=col(f"n1b{l}")).then_inc(on["evacuated"].sem, 1)
                        loop_groups(e, body)
                norm_ended(2 * GROUPS, 2 * GROUPS + 1)
                ended(transposed=4 * GROUPS, evacuated=4 * GROUPS, tables_loaded=16 * (3 + 2 * NW), cleared=6, ones_set=2)

                def bias_rows(e, w_edge):
                    for k in range(2):
                        for s in range(NW):
                            to = kbd[C:C + WN, k, s]
                            m = (2 if w_edge else 0) if s == NW - 1 else 1 if w_edge else None
                            if shift and m is not None:
                                ins = e.tensor_tensor(to, rpb[C:C + WN],
                                                      masks[C:C + WN, m].unsqueeze(1).broadcast_to([WN, NH, WN]), ALU.add)
                            else:
                                ins = e.tensor_copy(to, rpb[C:C + WN])
                            ins.then_inc(on["bias_set"].sem, 1)

                with nc.Block() as block:
                    @block.vector
                    def _(e):
                        bias_rows(e, False)
                        e.wait_ge(on["bias_set"].sem, on["bias_set"].at(2 * NW))
                    if shift:
                        @block.gpsimd
                        def _(e):
                            e.tensor_copy(yo[0:C, :, 0:HW, HW:HW + shift], yo[0:C, :, 0:HW, 0:shift]).then_inc(on["wrapped"].sem, 1)
                            e.wait_ge(on["wrapped"].sem, on["wrapped"].at(1))
                            e.tensor_copy(yo[0:C, :, HW:HW + shift, 0:HW + shift], yo[0:C, :, 0:shift, 0:HW + shift]).then_inc(on["wrapped"].sem, 1)
                            e.wait_ge(on["wrapped"].sem, on["wrapped"].at(2))
                ended(bias_set=2 * NW, wrapped=2 if shift else 0)

                def windows(w_from, w_to):
                    chunks, pairs = (w_to - w_from) * B, (w_to - w_from) * B * 4

                    def tokens(b, w):
                        return yo[:, b, bass.ds(WS * w + shift, WS), shift:shift + HW].rearrange("c w (s r) -> c s w r", r=WS)

                    def slots(ap):
                        return ap[:, :, 0:WN].rearrange("c s (w r) -> c s w r", w=WS)

                    def loop_chunks(e, head, main):
                        head(0, 0, w_from, 0)
                        head(1, 1, w_from, 1)
                        main(None)
                        with e.Fori(w_from, w_to) as i:
                            for b in range(B):
                                n = (i - w_from) * B + b
                                main((n, b, i, b % 2), (n + 2, (b + 2) % B, i + (b + 2) // B, b % 2))

                    QK, V, S, T, O = bank[0], bank[1], (bank[2], bank[3]), (bank[4], bank[5]), bank[6]

                    with nc.Block() as block:
                        @block.gpsimd
                        def _(e):
                            def head(n, b, w, k):
                                if not (isinstance(n, int) and n < 2):
                                    e.wait_ge(on["values_ready"].sem, on["values_ready"].at(n - 1))
                                e.nop(nofuse=True)
                                e.tensor_copy(slots(ywin[0:C, k]), tokens(b, w)[0:C]).then_inc(on["windows_staged"].sem, 1)
                                e.wait_ge(on["keys_evacuated"].sem, on["keys_evacuated"].at(n + 1))
                                e.tensor_tensor(kbd[0:C, k], ksb[:, :, 0:WN].unsqueeze(2).broadcast_to([C, NW, NH, WN]),
                                                     heads[:].unsqueeze(1).unsqueeze(3).broadcast_to([C, NW, NH, WN]),
                                                     ALU.mult).then_inc(on["keys_by_head"].sem, 1)

                            def main(now, then=None):
                                if now:
                                    head(*then)
                            loop_chunks(e, head, main)

                        @block.tensor
                        def _(e):
                            e.nop(nofuse=True).then_inc(on["probs_transposed"].sem, 4)

                            def head_keys(n, b, w, k):
                                e.wait_ge(on["windows_staged"].sem, on["windows_staged"].at(n + 1))
                                e.wait_ge(on["keys_evacuated"].sem, on["keys_evacuated"].at(n))
                                e.matmul(QK[:, :], wqk[:, l], ywin[0:C, k].rearrange("c s t -> c (s t)"),
                                              start=True, stop=True).then_inc(on["qk_ready"].sem, 1)

                            def head_values(n, b, w, k):
                                e.wait_ge(on["values_by_head"].sem, on["values_by_head"].at(n))
                                for s in range(NW):
                                    for half in range(2):
                                        last = e.matmul(V[64 * half:64 * half + 64, s * C:(s + 1) * C], ywin[:, k, s],
                                                        wv[:, l], start=True, stop=True)
                                last.then_inc(on["values_ready"].sem, 1)

                            def head(*chunk):
                                head_keys(*chunk)
                                head_values(*chunk)

                            def scores(n, g, k):
                                e.wait_ge(on["keys_by_head"].sem, on["keys_by_head"].at(n + 1))
                                e.wait_ge(on["shifted"].sem, on["shifted"].at(4 * n + g + 1))
                                for a in range(2):
                                    s = 2 * g + a
                                    last = e.matmul(S[g % 2][64 * a:64 * a + 64, 0:NH * WN], qwin[:, k, s],
                                                    kbd[:, k, s].rearrange("c h t -> c (h t)"), start=True, stop=True)
                                last.then_inc(on["scores_ready"].sem, 1)

                            def transposes(n, g):
                                e.wait_ge(on["probs_normalised"].sem, on["probs_normalised"].at(4 * n + g + 1))
                                e.wait_ge(on["probs_evacuated"].sem, on["probs_evacuated"].at(4 * n + g + 1))
                                for hp in range(HP):
                                    last = e.transpose(T[g % 2][:, 128 * hp:128 * hp + 128],
                                                       P[:, g, 2 * hp:2 * hp + 2].rearrange("q h t -> q (h t)"), ident[:])
                                last.then_inc(on["probs_transposed"].sem, 1)

                            def weighted(n, g, k):
                                e.wait_ge(on["probs_evacuated"].sem, on["probs_evacuated"].at(4 * n + g + 3))
                                if g == 0:
                                    e.wait_ge(on["values_by_head"].sem, on["values_by_head"].at(n + 1))
                                    e.wait_ge(on["outputs_evacuated"].sem, on["outputs_evacuated"].at(n))
                                for a in range(2):
                                    for hp in range(HP):
                                        s = 2 * g + a
                                        last = e.matmul(O[32 * hp:32 * hp + 32, s * SLOT:(s + 1) * SLOT], vbd[:, k, s, hp],
                                                        pT[:, g % 2, 128 * hp + 64 * a:128 * hp + 64 * a + 64],
                                                        start=True, stop=True)
                                if g == 3:
                                    last.then_inc(on["outputs_ready"].sem, 1)

                            def main(now, then=None):
                                if not now:
                                    scores(0, 0, 0)
                                    scores(0, 1, 0)
                                    scores(0, 2, 0)
                                    return
                                n, b, w, k = now
                                transposes(n, 0)
                                scores(n, 3, k)
                                weighted(n, 0, k)
                                transposes(n, 1)
                                head_keys(*then)
                                scores(n + 1, 0, 1 - k)
                                weighted(n, 1, k)
                                transposes(n, 2)
                                scores(n + 1, 1, 1 - k)
                                weighted(n, 2, k)
                                transposes(n, 3)
                                scores(n + 1, 2, 1 - k)
                                head_values(*then)
                                weighted(n, 3, k)
                            loop_chunks(e, head, main)

                        @block.scalar
                        def _(e):
                            e.nop(nofuse=True).then_inc(on["probs_evacuated"].sem, 2)

                            def head_keys(n, b, w, k):
                                e.wait_ge(on["qk_ready"].sem, on["qk_ready"].at(n + 1))
                                e.activation(qwin[0:C, k].rearrange("c s t -> c (s t)"), QK[0:C, :], ACT.Identity,
                                                  scale=SCALE, bias=qbias[:, l:l + 1]).then_inc(on["queries_evacuated"].sem, 1)
                                e.wait_ge(on["keys_by_head"].sem, on["keys_by_head"].at(n))
                                e.activation(ksb[:].rearrange("c s t -> c (s t)"), QK[C:128, :], ACT.Identity,
                                                  bias=col(f"kb{l}")).then_inc(on["keys_evacuated"].sem, 1)

                            def head_values(n, b, w, k):
                                e.wait_ge(on["values_ready"].sem, on["values_ready"].at(n + 1))
                                for half in range(2):
                                    at = slice(HD * half, HD * (half + 1))
                                    last = e.copy(vbd[64 * half:64 * half + 64, k, :, :, at].rearrange("t s h c -> t (s h) c"),
                                                  V[64 * half:64 * half + 64, :].rearrange("t (x c) -> t x c", c=16)[:, :, at])
                                last.then_inc(on["values_by_head"].sem, 1)

                            def head(*chunk):
                                head_keys(*chunk)
                                head_values(*chunk)

                            def exponentials(n, g):
                                e.wait_ge(on["shifted"].sem, on["shifted"].at(4 * n + g + 3))
                                e.activation(P[:, g, :, 0:WN], P[:, g, :, 0:WN], ACT.Exp).then_inc(on["exponentials_ready"].sem, 1)

                            def evacuate(n, g):
                                e.wait_ge(on["probs_transposed"].sem, on["probs_transposed"].at(4 * n + g + 5))
                                e.copy(pT[:, g % 2], T[g % 2][:, :]).then_inc(on["probs_evacuated"].sem, 1)

                            def main(now, then=None):
                                if not now:
                                    exponentials(0, 0)
                                    exponentials(0, 1)
                                    return
                                n, b, w, k = now
                                exponentials(n, 2)
                                evacuate(n, 0)
                                exponentials(n, 3)
                                evacuate(n, 1)
                                head_keys(*then)
                                exponentials(n + 1, 0)
                                evacuate(n, 2)
                                exponentials(n + 1, 1)
                                evacuate(n, 3)
                                e.wait_ge(on["outputs_ready"].sem, on["outputs_ready"].at(n + 1))
                                e.nop(nofuse=True)
                                e.copy(tokens(b, w), slots(O[:].rearrange("c (s t) -> c s t", s=NW))).then_inc(on["outputs_evacuated"].sem, 1)
                                head_values(*then)
                            loop_chunks(e, head, main)

                        @block.vector
                        def _(e):
                            e.nop(nofuse=True).then_inc(on["shifted"].sem, 2)

                            def head(*chunk):
                                pass

                            def shift_scores(n, g):
                                e.wait_ge(on["scores_ready"].sem, on["scores_ready"].at(4 * n + g + 1))
                                sc = S[g % 2][:, 0:NH * WN].rearrange("q (h t) -> q h t", h=NH)
                                e.tensor_reduce(out=mx[:, g % 2], in_=sc, axis=AX, op=ALU.max).then_inc(on["maxima_ready"].sem, 1)
                                e.wait_ge(on["maxima_ready"].sem, on["maxima_ready"].at(4 * n + g + 1))
                                e.wait_ge(on["probs_transposed"].sem, on["probs_transposed"].at(4 * n + g + 1))
                                e.tensor_tensor(P[:, g, :, 0:WN], sc,
                                                     mx[:, g % 2].unsqueeze(2).broadcast_to([128, NH, WN]), ALU.subtract).then_inc(on["shifted"].sem, 1)

                            def normalise(n, g):
                                v = 4 * n + g
                                e.wait_ge(on["exponentials_ready"].sem, on["exponentials_ready"].at(v + 1))
                                e.tensor_reduce(out=total[:, g % 2, 0], in_=P[:, g, :, 0:WN], axis=AX, op=ALU.add).then_inc(on["exponentials_summed"].sem, 1)
                                e.wait_ge(on["exponentials_summed"].sem, on["exponentials_summed"].at(v + 1))
                                e.reciprocal(total[:, g % 2, 1], total[:, g % 2, 0]).then_inc(on["sums_inverted"].sem, 1)
                                e.wait_ge(on["sums_inverted"].sem, on["sums_inverted"].at(v + 1))
                                e.tensor_tensor(P[:, g, :, 0:WN], P[:, g, :, 0:WN],
                                                total[:, g % 2, 1].unsqueeze(2).broadcast_to([128, NH, WN]), ALU.mult).then_inc(on["probs_normalised"].sem, 1)

                            def main(now, then=None):
                                if not now:
                                    shift_scores(0, 0)
                                    shift_scores(0, 1)
                                    normalise(0, 0)
                                    return
                                n, b, w, k = now
                                shift_scores(n, 2)
                                normalise(n, 1)
                                shift_scores(n, 3)
                                normalise(n, 2)
                                shift_scores(n + 1, 0)
                                normalise(n, 3)
                                shift_scores(n + 1, 1)
                                normalise(n + 1, 0)
                            loop_chunks(e, head, main)
                    h, g = chunks + 2, pairs
                    ended(windows_staged=h, keys_evacuated=h, keys_by_head=h, qk_ready=h, values_ready=h, values_by_head=h,
                          queries_evacuated=h, shifted=g + 4, scores_ready=g + 3, exponentials_ready=g + 2, probs_evacuated=g + 2,
                          probs_transposed=g + 4, maxima_ready=g + 2, outputs_evacuated=chunks, outputs_ready=chunks,
                          exponentials_summed=g + 1, sums_inverted=g + 1, probs_normalised=g + 1)

                windows(0, NW - 1 if shift else NW)
                if shift:
                    with nc.Block() as block:
                        @block.vector
                        def _(e):
                            bias_rows(e, True)
                            e.wait_ge(on["bias_set"].sem, on["bias_set"].at(2 * NW))
                    ended(bias_set=2 * NW)
                    windows(NW - 1, NW)
                    with nc.Block() as block:
                        @block.gpsimd
                        def _(e):
                            e.tensor_copy(yo[:, :, 0:shift, shift:HW + shift], yo[:, :, HW:HW + shift, shift:HW + shift]).then_inc(on["wrapped"].sem, 1)
                            e.wait_ge(on["wrapped"].sem, on["wrapped"].at(1))
                            e.tensor_copy(yo[:, :, 0:HW, 0:shift], yo[:, :, 0:HW, HW:HW + shift]).then_inc(on["wrapped"].sem, 1)
                            e.wait_ge(on["wrapped"].sem, on["wrapped"].at(2))
                    ended(wrapped=2)

                ysb = psb("proj_out", [128, 2, HALF])
                with nc.Block() as block:
                    @block.tensor
                    def _(e):
                        def body(n, p, w, p1, w1):
                            e.wait_ge(on["outputs_evacuated"].sem, on["outputs_evacuated"].at(n))
                            e.nop(nofuse=True)
                            for half in range(2):
                                last = e.matmul(bank[2 * p + half][0:C, 0:HALF].rearrange("c (w b h) -> c w b h", w=4, b=2), pw[:, l],
                                                yo[:, 2 * p:2 * p + 2, bass.ds(w + 4 * half, 4), 0:HW].rearrange("c b w h -> c w b h"),
                                                start=True, stop=True)
                            last.then_inc(on["outputs_ready"].sem, 1)
                            e.wait_ge(on["outputs_evacuated"].sem, on["outputs_evacuated"].at(n + 1))
                            e.wait_ge(on["residual_added"].sem, on["residual_added"].at(n))
                            for x in range(4):
                                last = e.transpose(bank[4 + p][0:TP, 128 * x:128 * (x + 1)], ysb[:, p, TP * x:TP * (x + 1)], ident[:])
                            last.then_inc(on["projected"].sem, 1)
                        loop_groups(e, body)

                    @block.scalar
                    def _(e):
                        def body(n, p, w, p1, w1):
                            e.wait_ge(on["outputs_ready"].sem, on["outputs_ready"].at(n + 1))
                            e.copy(ysb[0:C, p], bank[2 * p][0:C, 0:HALF])
                            e.copy(ysb[C:, p], bank[2 * p + 1][0:C, 0:HALF]).then_inc(on["outputs_evacuated"].sem, 1)
                        loop_groups(e, body)

                    @block.vector
                    def _(e):
                        def body(n, p, w, p1, w1):
                            e.wait_ge(on["projected"].sem, on["projected"].at(n + 1))
                            e.nop(nofuse=True)
                            halves = group(p, w).rearrange("t (h w) c -> t h w c", h=2)
                            e.tensor_tensor(halves, halves, bank[4 + p][0:TP, :].rearrange("t (w h c) -> t h w c", h=2, c=C),
                                            ALU.add).then_inc(on["residual_added"].sem, 1)
                        loop_groups(e, body)
                G = 2 * GROUPS
                ended(outputs_ready=G, outputs_evacuated=G, projected=G, residual_added=G)

            with ExitStack() as part:
                def psb(name, shape, dt=F32):
                    return part.enter_context(nc.sbuf_tensor(f"{name}_{l}", shape, dt))
                y = psb("mlp_in", [AK, GW, TP])
                hid = psb("mlp_hid", [128, 2, GW, TP])
                ysb = psb("mlp_out", [128, HALF])
                w1, w2 = psb("w1", [AK, 2 * HID]), psb("w2", [128, 2, C])
                with nc.Block() as block:
                    @block.sync
                    def _(e):
                        e.dma_start(w1[:], d["w1"][:, l]).then_inc(on["mlp_weights_loaded"].sem, 16)
                        e.dma_start(w2[:], d["w2"][:, l]).then_inc(on["mlp_weights_loaded"].sem, 16)
                        e.wait_ge(on["mlp_weights_loaded"].sem, on["mlp_weights_loaded"].at(32))

                    @block.gpsimd
                    def _(e):
                        e.memset(y[C:AK], 0.0).then_inc(on["cleared"].sem, 1)
                        e.wait_ge(on["cleared"].sem, on["cleared"].at(1))
                        norm_gpsimd(e, 0)
                        norm_gpsimd(e, 1)
                        loop_groups(e, lambda n, p, w, p1, w1_: norm_gpsimd(e, n + 2))

                    @block.vector
                    def _(e):
                        norm_vector(e, group(0, 0), 0, 0, squares=True)
                        norm_vector(e, group(1, 0), 1, 1, squares=True)

                        def body(n, p, w, p1, w1_):
                            e.nop(nofuse=True)
                            norm_vector(e, group(p, w + GW), p, n + 2, freed=(on["transposed"], 2 * n + 2), squares=True)
                            e.wait_ge(on["mlp_ready"].sem, on["mlp_ready"].at(n + 1))
                            e.nop(nofuse=True)
                            halves = group(p, w).rearrange("t (h w) c -> t h w c", h=2)
                            e.tensor_tensor(halves, halves, bank[7][0:TP, :].rearrange("t (w h c) -> t h w c", h=2, c=C),
                                            ALU.add).then_inc(on["residual_added"].sem, 1)
                        loop_groups(e, body)

                    @block.scalar
                    def _(e):
                        def evacuate_tokens(n):
                            for half in range(2):
                                e.wait_ge(on["transposed"].sem, on["transposed"].at(2 * n + half + 1))
                                e.activation(y[0:C, 4 * half:4 * half + 4].rearrange("c w t -> c (w t)"), bank[half][0:C, 0:HALF],
                                                  ACT.Identity, scale=col(f"n2g{l}"), bias=col(f"n2b{l}")).then_inc(on["evacuated"].sem, 1)

                        def gelus(n):
                            for half in range(2):
                                for f in range(2):
                                    e.wait_ge(on["hidden_ready"].sem, on["hidden_ready"].at(4 * n + 2 * half + f + 1))
                                    e.activation(hid[:, f, 4 * half:4 * half + 4].rearrange("c w t -> c (w t)"),
                                                      bank[2 + 2 * half + f][:, 0:HALF], ACT.Gelu, bias=col(f"mb{l}{f}", 0, 128)).then_inc(on["gelu_done"].sem, 1)
                        evacuate_tokens(0)
                        gelus(0)

                        def body(n, p, w, p1, w1_):
                            evacuate_tokens(n + 1)
                            e.wait_ge(on["outputs_ready"].sem, on["outputs_ready"].at(n + 1))
                            e.activation(ysb[:], bank[6][:, 0:HALF], ACT.Identity, bias=col(f"b2{l}", 0, 128)
                                         ).then_inc(on["outputs_evacuated"].sem, 1)
                            gelus(n + 1)
                        loop_groups(e, body)

                    @block.tensor
                    def _(e):
                        def hidden(n):
                            e.wait_ge(on["gelu_done"].sem, on["gelu_done"].at(4 * n))
                            for half in range(2):
                                e.wait_ge(on["evacuated"].sem, on["evacuated"].at(2 * n + half + 1))
                                for f in range(2):
                                    e.matmul(bank[2 + 2 * half + f][:, 0:HALF], w1[:, HID * f:HID * (f + 1)],
                                                  y[:, 4 * half:4 * half + 4].rearrange("c w t -> c (w t)"),
                                                  start=True, stop=True).then_inc(on["hidden_ready"].sem, 1)
                        e.wait_ge(on["mlp_weights_loaded"].sem, on["mlp_weights_loaded"].at(32))
                        e.wait_ge(on["cleared"].sem, on["cleared"].at(1))
                        transpose_group(e, 0, 0)
                        hidden(0)

                        def body(n, p, w, p1, w1_):
                            transpose_group(e, p1, n + 1)
                            e.wait_ge(on["gelu_done"].sem, on["gelu_done"].at(4 * n + 4))
                            e.wait_ge(on["outputs_evacuated"].sem, on["outputs_evacuated"].at(n))
                            for f in range(2):
                                for half in range(2):
                                    last = e.matmul(bank[6][C * half:C * (half + 1), 0:HALF], w2[:, f],
                                                    hid[:, f, 4 * half:4 * half + 4].rearrange("c w t -> c (w t)"),
                                                    start=f == 0, stop=f == 1)
                            last.then_inc(on["outputs_ready"].sem, 1)
                            hidden(n + 1)
                            e.wait_ge(on["outputs_evacuated"].sem, on["outputs_evacuated"].at(n + 1))
                            e.wait_ge(on["residual_added"].sem, on["residual_added"].at(n))
                            for x in range(4):
                                last = e.transpose(bank[7][0:TP, 128 * x:128 * (x + 1)], ysb[:, TP * x:TP * (x + 1)], ident[:])
                            last.then_inc(on["mlp_ready"].sem, 1)
                        loop_groups(e, body)
                G = 2 * GROUPS
                norm_ended(G + 2, G + 2)
                ended(mlp_weights_loaded=32, mlp_ready=G, residual_added=G, transposed=2 * G + 2, evacuated=2 * G + 2,
                      hidden_ready=4 * G + 4, gelu_done=4 * G + 4, outputs_ready=G, outputs_evacuated=G, cleared=1)

        swin_block(0)
        swin_block(1)
        with ExitStack() as part:
            def psb(name, shape, dt=F32):
                return part.enter_context(nc.sbuf_tensor(name, shape, dt))

            hT = psb("hT", [128, B, N])
            tok = psb("tok", [C + 1, N])
            kst = psb("kst", [AK, N])
            khi, klo = psb("khi", [128, N], BF16), psb("klo", [128, N], BF16)
            vst = psb("vst", [TP, KT, C])
            qst = psb("qst", [AK, HALF])
            qnext = psb("qnext", [C + 1, HALF])
            ones = psb("ones", [TP, 1])
            psum = psb("psum", [TP, 2, HALF])
            denrow = psb("denrow", [1, HALF])
            forward = psb("forward", [TP, 2, HALF])
            qsplit = psb("qsplit", [128, HALF], BF16)
            biasT = psb("biasT", [TP, 2352])
            biasQ = psb("biasQ", [TP, 2576])
            biased = psb("biased", [TP, 2, HALF])
            pexp = psb("pexp", [TP, 4, HALF])
            tmx, rmx, nmx = psb("tmx", [TP, 4, QT]), psb("rmx", [TP, 4]), psb("nmx", [TP, 4])
            awk2, awq2 = psb("awk2", [C, 2, C]), psb("awq2", [C, 2, C])
            bias2 = psb("bias2", [128, 2])

            flip = psb("flip", [TP, TP])
            pieces = [(t, slice(i, i + n)) for t, n in ((biasT, 392), (biasQ, 368)) for i in range(0, t.shape[1], n)]

            with nc.Block() as block:
                @block.sync
                def _(e):
                    for w in range(2):
                        e.dma_start(awk2[:, w], d["awk"]).then_inc(on["tables_loaded"].sem, 16)
                        e.dma_start(awq2[:, w], d["awq"]).then_inc(on["tables_loaded"].sem, 16)
                        e.dma_start(bias2[C * w:C * (w + 1)], d["bias2"]).then_inc(on["tables_loaded"].sem, 16)
                    for to, src in ((biasT, d["ext"]), (biasQ, d["extq"])):
                        e.dma_start(to[:], bass.AP(src.tensor, 0, [[1, TP], [1, to.shape[1]]])).then_inc(on["tables_loaded"].sem, 16)
                    e.dma_start(flip[:], d["flip"]).then_inc(on["tables_loaded"].sem, 16)
                    e.wait_ge(on["tables_loaded"].sem, on["tables_loaded"].at(16 * 9))

                @block.gpsimd
                def _(e):
                    for i, (a, v) in enumerate(((kst[C:AK], 0.0), (kst[C:C + 1], 1.0), (qst[C:AK], 0.0),
                                                (ones[:], 1.0), (tok[C:C + 1], 1.0))):
                        e.memset(a, v).then_inc(on["cleared"].sem, 1)
                        e.wait_ge(on["cleared"].sem, on["cleared"].at(i + 1))
                    loop_groups(e, lambda n, p, w, p1, w1: norm_gpsimd(e, n))

                @block.vector
                def _(e):
                    norm_centre(e, group(0, 0), 0, 0)

                    def body(n, p, w, p1, w1):
                        norm_variance(e, n, weight=1 + EPS, extra=EPS ** 2)
                        e.nop(nofuse=True)
                        norm_centre(e, group(p1, w1), p1, n + 1)
                        norm_scale(e, p, n, freed=(on["transposed"], 2 * n))
                    loop_groups(e, body)
                    for i, (t, at) in enumerate(pieces):
                        e.wait_ge(on["bias_flipped"].sem, on["bias_flipped"].at(i + 1))
                        e.tensor_scalar(t[:, at], bank[2 + i % 2][0:TP, 0:at.stop - at.start], col("last", 0, TP), None,
                                             ALU.subtract).then_inc(on["bias_set"].sem, 1)
                    e.wait_ge(on["bias_set"].sem, on["bias_set"].at(len(pieces)))

                @block.tensor
                def _(e):
                    loop_groups(e, lambda n, p, w, p1, w1: transpose_group(e, p, n))
                    e.wait_ge(on["tables_loaded"].sem, on["tables_loaded"].at(16 * 9))
                    for i, (t, at) in enumerate(pieces):
                        e.wait_ge(on["bias_set"].sem, on["bias_set"].at(max(i - 1, 0)))
                        e.matmul(bank[2 + i % 2][0:TP, 0:at.stop - at.start], flip[:], t[:, at], start=True, stop=True).then_inc(on["bias_flipped"].sem, 1)

                @block.scalar
                def _(e):
                    norm_scalar(e, 0, 0)

                    def body(n, p, w, p1, w1):
                        norm_scalar(e, p1, n + 1)
                        for half in range(2):
                            e.wait_ge(on["transposed"].sem, on["transposed"].at(2 * n + half + 1))
                            e.nop(nofuse=True)
                            e.activation(hT[0:C, 2 * p:2 * p + 2, :].rearrange("c b (h w) -> c w b h", w=HW)
                                              [:, bass.ds(w + 4 * half, 4)],
                                              bank[half][0:C, 0:HALF].rearrange("c (w b h) -> c w b h", w=4, b=2),
                                              ACT.Identity, scale=col("ag"), bias=col("ab")).then_inc(on["evacuated"].sem, 1)
                    loop_groups(e, body)
            norm_ended(2 * GROUPS, 2 * GROUPS + 1)
            ended(transposed=4 * GROUPS, evacuated=4 * GROUPS, tables_loaded=16 * 9, cleared=5, bias_set=len(pieces), bias_flipped=len(pieces))

            S, M, X, O = bank[0:4], bank[4:6], bank[6], bank[7]
            AHEAD = 2, 10

            def ahead_in(step):
                first, last = AHEAD
                n = 4 * QT
                done = lambda x: min(max(x - first, 0) * n // (last + 1 - first), n)
                return [(i // QT, i % QT) for i in range(done(step), done(step + 1))]

            def loop_tiles(e, image, tile):
                with e.Fori(0, B) as b:
                    image(b)

                    def one(q, first, late, then):
                        tile(b, q, b * QT + q, (b * QT + q) * KT, first, late, then)
                    one(0, True, False, False)
                    with e.Fori(1, QFLAT - 1) as q:
                        one(q, False, False, False)
                    one(QFLAT - 1, False, False, True)
                    with e.Fori(QFLAT, QT - 1) as q:
                        one(q, False, True, True)
                    one(QT - 1, False, True, None)

            def late_tiles(b, q):
                return b * (QT - QFLAT) + q - QFLAT

            with nc.Block() as block:
                @block.sync
                def _(e):
                    with e.Fori(0, B) as b:
                        with e.Fori(0, QT) as q:
                            e.wait_ge(on["denominators_read"].sem, on["denominators_read"].at(b * QT + q + 1))
                            e.nop(nofuse=True)
                            e.dma_start(d["dens"][bass.ds((b * QT + q) * HALF, HALF)].unsqueeze(0), denrow[:]
                                        ).then_inc(on["denominators_stored"].sem, 16)
                            e.wait_ge(on["denominators_stored"].sem, on["denominators_stored"].at((b * QT + q) * 16 + 16))
                            e.nop(nofuse=True).then_inc(on["row_free"].sem, 1)

                @block.gpsimd
                def _(e):
                    e.nop(nofuse=True).then_inc(on["summed_gpsimd"].sem, 2)

                    def image(b):
                        pass

                    def tile(b, q, Q, U, first, late, then):
                        e.wait_ge(on["denominators_ready"].sem, on["denominators_ready"].at(Q))
                        for t in range(1, KT, 2):
                            e.wait_ge(on["attn_exponentials"].sem, on["attn_exponentials"].at(U + t + 5))
                            if t == 1:
                                e.nop(nofuse=True)
                                e.tensor_copy(psum[:, 1], pexp[:, 1]).then_inc(on["summed_gpsimd"].sem, 1)
                            else:
                                e.wait_ge(on["summed_gpsimd"].sem, on["summed_gpsimd"].at(KT // 2 * Q + t // 2 + 2))
                                e.tensor_tensor(psum[:, 1], psum[:, 1], pexp[:, t % 4], ALU.add).then_inc(on["summed_gpsimd"].sem, 1)
                        e.wait_ge(on["summed_gpsimd"].sem, on["summed_gpsimd"].at(KT // 2 * (Q + 1) + 2))
                        e.wait_ge(on["summed_vector"].sem, on["summed_vector"].at(KT // 2 * (Q + 1) + 2))
                        e.nop(nofuse=True)
                        e.tensor_tensor(psum[:, 1], psum[:, 1], psum[:, 0], ALU.add).then_inc(on["sums_joined"].sem, 1)
                    loop_tiles(e, image, tile)

                @block.tensor
                def _(e):
                    def query(b, q, Q):
                        e.wait_ge(on["maximum_set"].sem, on["maximum_set"].at(Q))
                        e.nop(nofuse=True)
                        e.matmul(X[:, 0:HALF], awq2[:].rearrange("c x k -> c (x k)"), hT[0:C, b, bass.ds(q * HALF, HALF)],
                                 start=True, stop=True).then_inc(on["query_ready"].sem, 1)

                    def tile_scores(U, s, t):
                        e.wait_ge(on["tile_maximum"].sem, on["tile_maximum"].at(U + 7 * s + t + 1))
                        for i, k in enumerate((khi, klo)):
                            last = e.matmul(M[(7 * s + t) % 2][0:TP, 0:HALF], qsplit[:, TP * s:TP * (s + 1)],
                                            k[:, t * HALF:(t + 1) * HALF], start=i == 0, stop=i == 1)
                        last.then_inc(on["tile_scored"].sem, 1)

                    def move_maxima(Q):
                        e.wait_ge(on["row_maximum"].sem, on["row_maximum"].at(Q + 1))
                        for s in range(4):
                            last = e.matmul(X[C:C + 1, TP * s:TP * (s + 1)], nmx[:, s:s + 1], ident[0:TP, 0:TP],
                                            start=True, stop=True)
                        last.then_inc(on["maximum_moved"].sem, 1)

                    def image(b):
                        e.wait_ge(on["attn_exponentials"].sem, on["attn_exponentials"].at(b * QT * KT + 4))
                        for t in range(QT):
                            if t >= 4:
                                e.wait_ge(on["keys_evacuated"].sem, on["keys_evacuated"].at(QT * b + t - 3))
                            e.nop(nofuse=True)
                            e.matmul(S[t % 4][:, 0:HALF], awk2[:].rearrange("c x k -> c (x k)"),
                                     hT[0:C, b, t * HALF:(t + 1) * HALF], start=True, stop=True).then_inc(on["keys_ready"].sem, 1)
                            if t < 3:
                                continue
                            g = t - 3
                            if g == 0:
                                e.wait_ge(on["tokens_staged"].sem, on["tokens_staged"].at(b + 1))
                                e.wait_ge(on["denominators_read"].sem, on["denominators_read"].at(b * QT))
                            if g >= 2:
                                e.wait_ge(on["values_evacuated"].sem, on["values_evacuated"].at(4 * b + g - 1))
                            for x in range(7 * g, 7 * g + 7):
                                last = e.matmul(M[g % 2][0:TP, C * (x - 7 * g):C * (x - 7 * g + 1)], tok[:, x * TP:(x + 1) * TP],
                                                awv[:], start=True, stop=True)
                            last.then_inc(on["values_ready"].sem, 1)
                            if g == 0:
                                query(b, 0, b * QT)
                        e.wait_ge(on["keys_evacuated"].sem, on["keys_evacuated"].at(QT * b + QT))
                        e.wait_ge(on["values_evacuated"].sem, on["values_evacuated"].at(4 * b + 4))
                        e.wait_ge(on["queries_split"].sem, on["queries_split"].at(b * QT + 1))
                        for s in range(4):
                            for t in range(QT):
                                tile_scores(b * QT * KT, s, t)
                        move_maxima(b * QT)

                    def scores(U, t):
                        e.wait_ge(on["attn_exponentials"].sem, on["attn_exponentials"].at(U + t + 1))
                        e.matmul(S[t % 4][0:TP, 0:HALF], kst[:, TP * t:TP * (t + 1)], qst[:], start=True, stop=True
                                 ).then_inc(on["attn_scored"].sem, 1)

                    def denominators(Q):
                        e.wait_ge(on["sums_joined"].sem, on["sums_joined"].at(Q + 1))
                        e.matmul(M[0][0:1, 0:HALF], ones[:], psum[:, 1], start=True, stop=True).then_inc(on["denominators_ready"].sem, 1)

                    def tile(b, q, Q, U, first, late, then):
                        if first:
                            e.wait_ge(on["query_set"].sem, on["query_set"].at(Q + 1))
                            scores(U, 0)
                            scores(U, 1)
                        for step in range(KT // 2):
                            ahead = ahead_in(step) if then is not None else []
                            if step == AHEAD[0] and then is not None:
                                e.wait_ge(on["queries_split"].sem, on["queries_split"].at(Q + 2))
                                e.wait_ge(on["denominators_read"].sem, on["denominators_read"].at(Q))
                            for t in (2 * step + 2, 2 * step + 3):
                                if t < KT:
                                    scores(U, t)
                                    for s, k in ahead[t % 2:t % 2 + 1]:
                                        tile_scores(U + KT, s, k)
                            if step == 1 and not first:
                                denominators(Q - 1)
                            if step == KT // 2 - 1 and then is not None:
                                e.wait_ge(on["query_set"].sem, on["query_set"].at(Q + 2))
                                scores(U + KT, 0)
                                scores(U + KT, 1)
                            e.wait_ge(on["attn_exponentials"].sem, on["attn_exponentials"].at(U + 2 * step + 6))
                            if step == 0:
                                e.wait_ge(on["attn_evacuated"].sem, on["attn_evacuated"].at(Q))
                            for t in (2 * step, 2 * step + 1):
                                e.matmul(O[C * (t % 2):C * (t % 2) + C, 0:HALF], vst[:, t], pexp[:, t % 4],
                                         start=step == 0, stop=step == KT // 2 - 1).then_inc(on["attn_weighted"].sem, 1)
                            for s, k in ahead[2:]:
                                tile_scores(U + KT, s, k)
                            if then is not None:
                                if step == 0:
                                    query(b, q + 1, Q + 1)
                                if step == AHEAD[1] + 1:
                                    move_maxima(Q + 1)
                        if then is None:
                            denominators(Q)
                    loop_tiles(e, image, tile)

                @block.scalar
                def _(e):
                    e.nop(nofuse=True).then_inc(on["attn_exponentials"].sem, 4)

                    def query(Q):
                        e.wait_ge(on["query_ready"].sem, on["query_ready"].at(Q + 1))
                        e.activation(qsplit[:], X[:, 0:HALF], ACT.Identity, bias=bias2[:, 1:2])
                        e.activation(qnext[0:C, :], X[0:C, 0:HALF], ACT.Identity, bias=bias2[0:C, 1:2]
                                     ).then_inc(on["query_rounded"].sem, 1)

                    def denominators(Q):
                        e.wait_ge(on["denominators_ready"].sem, on["denominators_ready"].at(Q + 1))
                        e.wait_ge(on["row_free"].sem, on["row_free"].at(Q))
                        e.copy(denrow[:], M[0][0:1, 0:HALF]).then_inc(on["denominators_read"].sem, 1)

                    def set_maxima(Q):
                        e.wait_ge(on["maximum_moved"].sem, on["maximum_moved"].at(Q + 1))
                        e.copy(qnext[C:C + 1, :], X[C:C + 1, 0:HALF]).then_inc(on["maximum_set"].sem, 1)

                    def image(b):
                        for t in range(QT):
                            at = slice(t * HALF, (t + 1) * HALF)
                            e.wait_ge(on["keys_ready"].sem, on["keys_ready"].at(QT * b + t + 1))
                            e.activation(khi[:, at], S[t % 4][:, 0:HALF], ACT.Identity, bias=bias2[:, 0:1])
                            e.activation(kst[0:C, at], S[t % 4][0:C, 0:HALF], ACT.Identity, bias=bias2[0:C, 0:1]
                                         ).then_inc(on["keys_rounded"].sem, 1)
                            if t >= 3:
                                e.wait_ge(on["values_ready"].sem, on["values_ready"].at(4 * b + t - 2))
                                e.copy(vst[:, 7 * t - 21:7 * t - 14], M[(t - 3) % 2][0:TP, 0:7 * C].rearrange("t (x c) -> t x c", c=C)
                                       ).then_inc(on["values_evacuated"].sem, 1)
                            if t == 3:
                                query(b * QT)
                        set_maxima(b * QT)

                    def tile(b, q, Q, U, first, late, then):
                        for t in range(KT):
                            if late and t < KBIAS:
                                e.wait_ge(on["scores_biased"].sem, on["scores_biased"].at(late_tiles(b, q) * KBIAS + t + 1))
                                x = biased[:, t % 2]
                            else:
                                e.wait_ge(on["attn_scored"].sem, on["attn_scored"].at(U + t + 1))
                                x = S[t % 4][0:TP, 0:HALF]
                            free = on["summed_gpsimd" if t % 2 else "summed_vector"]
                            e.wait_ge(free.sem, free.at(KT // 2 * Q + t // 2 + 1))
                            e.activation(pexp[:, t % 4], x, ACT.Exp).then_inc(on["attn_exponentials"].sem, 1)
                            if then is not None and t == 2:
                                query(Q + 1)
                            if t == 3 and not first:
                                denominators(Q - 1)
                            if then is not None and t == KT - 3:
                                set_maxima(Q + 1)
                        if then is None:
                            denominators(Q)
                    loop_tiles(e, image, tile)

                @block.vector
                def _(e):
                    e.nop(nofuse=True).then_inc(on["tile_maximum"].sem, 2)
                    e.nop(nofuse=True).then_inc(on["summed_vector"].sem, 2)

                    def split(Q):
                        e.wait_ge(on["query_rounded"].sem, on["query_rounded"].at(Q + 1))
                        e.scalar_tensor_tensor(qsplit[C:, :], X[C:, 0:HALF], bias2[C:, 1:2], qsplit[C:, :],
                                               ALU.add, ALU.subtract).then_inc(on["queries_split"].sem, 1)

                    def maximum(b, q, U, late, s, t):
                        e.wait_ge(on["tile_scored"].sem, on["tile_scored"].at(U + 7 * s + t + 1))
                        x = M[(7 * s + t) % 2][0:TP, 0:HALF]
                        if late and t < 3:
                            e.nop(nofuse=True)
                            e.tensor_tensor(forward[:, (7 * s + t) % 2], x, biasQ[:, bass.ds(TP * (KT - 1) - HALF * q - TP * s + HALF * t, HALF)],
                                            ALU.add).then_inc(on["tile_biased"].sem, 1)
                            e.wait_ge(on["tile_biased"].sem, on["tile_biased"].at(late_tiles(b, q) * 12 + 3 * s + t + 1))
                            x = forward[:, (7 * s + t) % 2]
                        e.tensor_reduce(out=tmx[:, s, t:t + 1], in_=x, axis=AX, op=ALU.max).then_inc(on["tile_maximum"].sem, 1)

                    def row_maxima(Q):
                        e.wait_ge(on["tile_maximum"].sem, on["tile_maximum"].at(KT * (Q + 1) + 2))
                        e.tensor_reduce(out=rmx[:], in_=tmx[:], axis=AX, op=ALU.max).then_inc(on["maxima_ready"].sem, 1)
                        e.wait_ge(on["maxima_ready"].sem, on["maxima_ready"].at(Q + 1))
                        e.tensor_scalar(nmx[:], rmx[:], -1.0, None, ALU.mult).then_inc(on["row_maximum"].sem, 1)

                    def set_query(Q):
                        e.wait_ge(on["maximum_set"].sem, on["maximum_set"].at(Q + 1))
                        e.tensor_copy(qst[0:C + 1, :], qnext[:]).then_inc(on["query_set"].sem, 1)

                    def image(b):
                        e.wait_ge(on["values_ready"].sem, on["values_ready"].at(4 * b))
                        e.nop(nofuse=True)
                        e.tensor_copy(tok[0:C, :], hT[0:C, b, :]).then_inc(on["tokens_staged"].sem, 1)
                        for t in range(QT):
                            at = slice(t * HALF, (t + 1) * HALF)
                            e.wait_ge(on["keys_rounded"].sem, on["keys_rounded"].at(QT * b + t + 1))
                            e.scalar_tensor_tensor(klo[:, at], S[t % 4][:, 0:HALF], bias2[:, 0:1], khi[:, at], ALU.add, ALU.subtract
                                                   ).then_inc(on["keys_evacuated"].sem, 1)
                        split(b * QT)
                        for s in range(4):
                            for t in range(QT):
                                maximum(b, 0, b * QT * KT, False, s, t)
                        row_maxima(b * QT)
                        set_query(b * QT)

                    def tile(b, q, Q, U, first, late, then):
                        def bias(q, U, late, t):
                            if late and t < KBIAS:
                                e.wait_ge(on["attn_scored"].sem, on["attn_scored"].at(U + t + 1))
                                e.wait_ge(on["attn_exponentials"].sem, on["attn_exponentials"].at(U + t + 3))
                                e.nop(nofuse=True)
                                e.tensor_tensor(biased[:, t % 2], S[t % 4][0:TP, 0:HALF],
                                                biasT[:, bass.ds(HALF * q - TP * t - 784, HALF)], ALU.add
                                                ).then_inc(on["scores_biased"].sem, 1)
                        for step in range(KT // 2):
                            t = 2 * step
                            bias(q, U, late, t + 2)
                            e.wait_ge(on["attn_exponentials"].sem, on["attn_exponentials"].at(U + t + 5))
                            if step == 0:
                                e.wait_ge(on["sums_joined"].sem, on["sums_joined"].at(Q))
                                e.tensor_copy(psum[:, 0], pexp[:, 0]).then_inc(on["summed_vector"].sem, 1)
                            else:
                                e.wait_ge(on["summed_vector"].sem, on["summed_vector"].at(KT // 2 * Q + step + 2))
                                e.tensor_tensor(psum[:, 0], psum[:, 0], pexp[:, t % 4], ALU.add).then_inc(on["summed_vector"].sem, 1)
                            bias(q, U, late, t + 3)
                            if then is not None:
                                if step == AHEAD[0] - 1:
                                    split(Q + 1)
                                for s, k in ahead_in(step):
                                    maximum(b, q + 1, U + KT, then, s, k)
                                if step == AHEAD[1]:
                                    row_maxima(Q + 1)
                                if step == KT // 2 - 2:
                                    e.wait_ge(on["attn_scored"].sem, on["attn_scored"].at(U + KT))
                                    set_query(Q + 1)
                        if then is not None:
                            bias(q + 1, U + KT, then, 0)
                            bias(q + 1, U + KT, then, 1)
                        e.wait_ge(on["attn_weighted"].sem, on["attn_weighted"].at(U + KT))
                        e.nop(nofuse=True)
                        e.tensor_copy(hT[:, b, bass.ds(q * HALF, HALF)], O[:, 0:HALF]).then_inc(on["attn_evacuated"].sem, 1)
                    loop_tiles(e, image, tile)
            u, Q = B * QT * KT, B * QT
            late = B * (QT - QFLAT)
            ended(tokens_staged=B, values_ready=4 * B, values_evacuated=4 * B, keys_ready=Q, keys_evacuated=Q, keys_rounded=Q,
                  query_ready=Q, query_rounded=Q, queries_split=Q, tile_scored=u, tile_maximum=u + 2, tile_biased=12 * late,
                  maxima_ready=Q, row_maximum=Q, maximum_moved=Q, maximum_set=Q, query_set=Q, attn_scored=u,
                  attn_exponentials=u + 4, attn_weighted=u, attn_evacuated=Q, scores_biased=KBIAS * late,
                  summed_vector=u // 2 + 2, summed_gpsimd=u // 2 + 2, denominators_ready=Q, denominators_read=Q, sums_joined=Q,
                  denominators_stored=16 * Q, row_free=Q)

            ysb = psb("attn_out", [128, 2, HALF])
            raw = psb("attn_raw", [TP, 2, GW, C])
            den = psb("den", [TP, PAIRS * HW])
            rden = psb("attn_rden", [TP, PAIRS * HW])
            gained = psb("attn_gained", [TP, 2, GW, C])
            with nc.Block() as block:
                @block.sync
                def _(e):
                    for p in range(PAIRS):
                        for b in range(2):
                            e.dma_start(den[HW * b:HW * (b + 1), p * HW:(p + 1) * HW],
                                        d["dens"][(2 * p + b) * N:(2 * p + b + 1) * N].rearrange("(h w) -> h w", w=HW)
                                        ).then_inc(on["tables_loaded"].sem, 16)

                @block.tensor
                def _(e):
                    def body(n, p, w, p1, w1):
                        e.wait_ge(on["outputs_evacuated"].sem, on["outputs_evacuated"].at(n))
                        e.nop(nofuse=True)
                        for half in range(2):
                            last = e.matmul(bank[2 * p + half][0:C, 0:HALF].rearrange("c (w b h) -> c w b h", w=4, b=2), awp[:],
                                            hT[:, 2 * p:2 * p + 2, :].rearrange("c b (h w) -> c w b h", w=HW)[:, bass.ds(w + 4 * half, 4)],
                                            start=True, stop=True)
                        last.then_inc(on["outputs_ready"].sem, 1)
                        e.wait_ge(on["outputs_evacuated"].sem, on["outputs_evacuated"].at(n + 1))
                        e.wait_ge(on["outputs_normalised"].sem, on["outputs_normalised"].at(n))
                        for x in range(4):
                            last = e.transpose(bank[4 + p][0:TP, 128 * x:128 * (x + 1)], ysb[:, p, TP * x:TP * (x + 1)], ident[:])
                        last.then_inc(on["projected"].sem, 1)
                    loop_groups(e, body)

                @block.scalar
                def _(e):
                    def body(n, p, w, p1, w1):
                        e.wait_ge(on["outputs_ready"].sem, on["outputs_ready"].at(n + 1))
                        e.copy(ysb[0:C, p], bank[2 * p][0:C, 0:HALF])
                        e.copy(ysb[C:, p], bank[2 * p + 1][0:C, 0:HALF]).then_inc(on["outputs_evacuated"].sem, 1)
                        norm_scalar(e, p, n)
                    loop_groups(e, body)

                @block.vector
                def _(e):
                    e.wait_ge(on["tables_loaded"].sem, on["tables_loaded"].at(16 * B))
                    e.reciprocal(rden[:], den[:]).then_inc(on["weights_scaled"].sem, 1)
                    e.wait_ge(on["weights_scaled"].sem, on["weights_scaled"].at(1))
                    e.tensor_scalar(rden[:], rden[:], col("scale", 0, TP), None, ALU.mult).then_inc(on["weights_scaled"].sem, 1)
                    e.wait_ge(on["weights_scaled"].sem, on["weights_scaled"].at(2))

                    def take(n, p, w):
                        e.wait_ge(on["projected"].sem, on["projected"].at(n + 1))
                        e.nop(nofuse=True)
                        e.tensor_tensor(raw[:, p].rearrange("t (h w) c -> t h w c", h=2),
                                        bank[4 + p][0:TP, :].rearrange("t (w h c) -> t h w c", h=2, c=C),
                                        rden[:, bass.ds(p * HW + w, GW)].rearrange("t (h w) -> t h w", h=2).unsqueeze(3)
                                        .broadcast_to([TP, 2, 4, C]), ALU.mult).then_inc(on["outputs_normalised"].sem, 1)
                        e.wait_ge(on["outputs_normalised"].sem, on["outputs_normalised"].at(n + 1))
                        e.tensor_tensor(raw[:, p], raw[:, p], row("apb"), ALU.add).then_inc(on["projection_biased"].sem, 1)
                        e.wait_ge(on["projection_biased"].sem, on["projection_biased"].at(n + 1))
                        norm_centre(e, raw[:, p], p, n)
                    take(0, 0, 0)

                    def body(n, p, w, p1, w1):
                        norm_variance(e, n)
                        if p1 is not None:
                            take(n + 1, p1, w1)
                        norm_scale(e, p, n)
                        e.wait_ge(on["normalised"].sem, on["normalised"].at(n + 1))
                        e.wait_ge(on["residual_added"].sem, on["residual_added"].at(n))
                        e.tensor_tensor(gained[:, p], normed[:, p], row("a2g"), ALU.mult).then_inc(on["gain_applied"].sem, 1)
                    loop_but_last(e, body)

                @block.gpsimd
                def _(e):
                    e.nop(nofuse=True).then_inc(on["residual_added"].sem, 1)
                    norm_gpsimd(e, 0)

                    def body(n, p, w, p1, w1):
                        if p1 is not None:
                            norm_gpsimd(e, n + 1)
                        e.wait_ge(on["gain_applied"].sem, on["gain_applied"].at(n + 1))
                        e.tensor_tensor(gained[:, p], gained[:, p], row("a2b"), ALU.add).then_inc(on["output_ready"].sem, 1)
                        e.wait_ge(on["output_ready"].sem, on["output_ready"].at(n + 1))
                        e.nop(nofuse=True)
                        e.tensor_tensor(group(p, w), group(p, w), gained[:, p], ALU.add).then_inc(on["residual_added"].sem, 1)
                    loop_but_last(e, body)
            G = 2 * GROUPS
            norm_ended(G, G)
            ended(outputs_ready=G, outputs_evacuated=G, gain_applied=G, output_ready=G, residual_added=G + 1, projected=G,
                  tables_loaded=16 * B, weights_scaled=2, outputs_normalised=G, projection_biased=G)
        with ExitStack() as part:
            def psb(name, shape, dt=F32):
                return part.enter_context(nc.sbuf_tensor(name, shape, dt))

            wr, ew1, ew2 = psb("wr", [AK, E]), psb("ew1", [AK, E, HID]), psb("ew2", [HID, E, C])
            eb2, number = psb("eb2", [128, E // 2]), psb("number", [TP, E])
            xn = psb("xn", [AK, 2, GW, TP])
            hid = psb("ehid", [HID, 2, E, HALF])
            lg, top = psb("lg", [TP, GW, E]), psb("top", [TP, GW, E])
            at = psb("at", [TP, GW, E], U32)
            atf = psb("atf", [TP, GW, 2])
            lead, tanh = psb("lead", [TP, GW]), psb("tanh", [TP, GW])
            share = psb("share", [TP, 2, GW])
            one = psb("one", [TP, 2, GW, E])
            gate = psb("gate", [TP, 2, GW, E])
            ysb = psb("ysb", [128, 2, E // 2, HALF])
            yw = psb("yw", [TP, 2, E * C])
            mix = psb("mix", [TP, 2, GW, C])
            STEPS = 8
            HEAD = 4
            NEXT_AT = 13
            TANH_AT = 5

            with nc.Block() as block:
                @block.sync
                def _(e):
                    for to, src in ((wr, d["wr"]), (ew1, d["ew1"]), (ew2, d["ew2"]),
                                    (eb2, d["eb2"]),
                                    (number, d["number"].unsqueeze(0).broadcast_to([TP, E]))):
                        e.dma_start(to[:], src).then_inc(on["tables_loaded"].sem, 16)
                    e.wait_ge(on["tables_loaded"].sem, on["tables_loaded"].at(16 * 5))

                @block.gpsimd
                def _(e):
                    e.memset(xn[C:AK], 0.0).then_inc(on["ones_set"].sem, 1)
                    e.wait_ge(on["ones_set"].sem, on["ones_set"].at(1))
                    e.memset(xn[C:C + 1], 1.0).then_inc(on["ones_set"].sem, 1)
                    e.wait_ge(on["ones_set"].sem, on["ones_set"].at(2))
                    norm_squares(e, 0, 0)
                    norm_gpsimd(e, 0)

                    def body(n, p, w, p1, w1):
                        norm_squares(e, p1, n + 1)
                        norm_gpsimd(e, n + 1)
                        e.wait_ge(on["mixed"].sem, on["mixed"].at(GW * (n + 1)))
                        e.nop(nofuse=True)
                        e.tensor_tensor(group(p, w), group(p, w), mix[:, p], ALU.add).then_inc(on["residual_added"].sem, 1)
                    loop_groups(e, body)

                @block.vector
                def _(e):
                    norm_vector(e, group(0, 0), 0, 0, weight=1 + EPS, extra=EPS ** 2)
                    e.wait_ge(on["tables_loaded"].sem, on["tables_loaded"].at(16 * 5))
                    e.nop(nofuse=True).then_inc(on["expert_weighted"].sem, 2)

                    def body(n, p, w, p1, w1):
                        step = STEPS * n
                        e.wait_ge(on["gate_scored"].sem, on["gate_scored"].at(n + 1))
                        e.tensor_copy(lg[:].rearrange("t w e -> t (w e)"), bank[2][0:TP, 0:GW * E]).then_inc(on["gate_step"].sem, 1)
                        e.wait_ge(on["gate_step"].sem, on["gate_step"].at(step + 1))
                        e.nop(nofuse=True)
                        for x in range(GW):
                            last = e.max(top[:, x], lg[:, x])
                        last.then_inc(on["gate_step"].sem, 1)
                        e.wait_ge(on["gate_step"].sem, on["gate_step"].at(step + 2))
                        e.tensor_tensor(lead[:], top[:, :, 0], top[:, :, 1], ALU.subtract).then_inc(on["lead_ready"].sem, 1)
                        for x in range(GW):
                            last = e.max_index(at[:, x], top[:, x], lg[:, x])
                        last.then_inc(on["gate_step"].sem, 1)
                        e.wait_ge(on["gate_step"].sem, on["gate_step"].at(step + 3))
                        e.tensor_copy(atf[:], at[:, :, 0:2]).then_inc(on["gate_step"].sem, 1)
                        e.wait_ge(on["gate_step"].sem, on["gate_step"].at(step + 4))
                        e.wait_ge(on["tanh_ready"].sem, on["tanh_ready"].at(n + 1))
                        for i in range(2):
                            last = e.tensor_scalar(share[:, i], tanh[:], 0.5 - i, 0.5, ALU.mult, ALU.add)
                        last.then_inc(on["gate_step"].sem, 1)
                        for i in range(2):
                            last = e.tensor_tensor(one[:, i], number[:].unsqueeze(1).broadcast_to([TP, GW, E]),
                                                   atf[:, :, i].unsqueeze(2).broadcast_to([TP, GW, E]), ALU.is_equal)
                        last.then_inc(on["gate_step"].sem, 1)
                        e.wait_ge(on["gate_step"].sem, on["gate_step"].at(step + 6))
                        for i in range(2):
                            last = e.tensor_tensor(one[:, i], one[:, i], share[:, i].unsqueeze(2).broadcast_to([TP, GW, E]), ALU.mult)
                        last.then_inc(on["gate_step"].sem, 1)
                        e.wait_ge(on["gate_step"].sem, on["gate_step"].at(step + 7))
                        e.tensor_tensor(gate[:, p], one[:, 0], one[:, 1], ALU.add).then_inc(on["gate_step"].sem, 1)
                        e.wait_ge(on["gate_step"].sem, on["gate_step"].at(step + 8))

                        e.nop(nofuse=True)
                        norm_vector(e, group(p1, w1), p1, n + 1, freed=(on["transposed"], 2 * n), weight=1 + EPS, extra=EPS ** 2)

                        def weight(x):
                            e.wait_ge(on["experts_done"].sem, on["experts_done"].at(GW * n + x + 1))
                            e.wait_ge(on["mixed"].sem, on["mixed"].at(GW * n + max(x - 1, 0)))
                            e.tensor_tensor(yw[:, x % 2].rearrange("t (e c) -> t e c", e=E),
                                                 bank[6 + x % 2][0:TP, :].rearrange("t (e c) -> t e c", e=E),
                                                 gate[:, p, x].unsqueeze(2).broadcast_to([TP, E, C]), ALU.mult).then_inc(on["expert_weighted"].sem, 1)
                        weight(0)
                        e.wait_ge(on["residual_added"].sem, on["residual_added"].at(n))
                        for x in range(GW):
                            if x + 1 < GW:
                                weight(x + 1)
                            e.wait_ge(on["expert_weighted"].sem, on["expert_weighted"].at(GW * n + x + 3))
                            e.tensor_reduce(out=mix[:, p, x], in_=yw[:, x % 2].rearrange("t (e c) -> t c e", e=E), axis=AX,
                                                 op=ALU.add).then_inc(on["mixed"].sem, 1)
                    loop_groups(e, body)

                @block.scalar
                def _(e):
                    e.nop(nofuse=True).then_inc(on["expert_gelu"].sem, 2)

                    def evacuate_tokens(n, p):
                        for half in range(2):
                            e.wait_ge(on["transposed"].sem, on["transposed"].at(2 * n + half + 1))
                            e.activation(xn[0:C, p, 4 * half:4 * half + 4].rearrange("c w t -> c (w t)"), bank[half][0:C, 0:HALF],
                                              ACT.Identity, scale=col("fg"), bias=col("fb")).then_inc(on["evacuated"].sem, 1)

                    def evacuate_outputs(n, k):
                        e.wait_ge(on["outputs_ready"].sem, on["outputs_ready"].at(E * n + k + 1))
                        e.activation(ysb[:, k // 4, k % 4], bank[5][:, 0:HALF], ACT.Identity, bias=eb2[:, k % 4:k % 4 + 1]
                                     ).then_inc(on["outputs_evacuated"].sem, 1)

                    def gelu(n, i):
                        e.wait_ge(on["expert_hidden"].sem, on["expert_hidden"].at(2 * E * n + i + 1))
                        e.activation(hid[:, i // E, i % E], bank[3 + i % 2][:, 0:HALF], ACT.Gelu,
                                          bias=col(f"eb{i % E}", 0, 128)).then_inc(on["expert_gelu"].sem, 1)

                    evacuate_tokens(0, 0)
                    for i in range(HEAD):
                        gelu(0, i)

                    def body(n, p, w, p1, w1):
                        for i in range(HEAD, 2 * E):
                            gelu(n, i)
                            if i == HEAD:
                                evacuate_outputs(n, 0)
                            if i % 2:
                                evacuate_outputs(n, (i - 3) // 2)
                            if i == TANH_AT:
                                e.wait_ge(on["lead_ready"].sem, on["lead_ready"].at(n + 1))
                                e.activation(tanh[:], lead[:], ACT.Tanh, scale=0.5).then_inc(on["tanh_ready"].sem, 1)
                            if i == NEXT_AT + 1:
                                evacuate_tokens(n + 1, p1)
                        evacuate_outputs(n, E - 1)
                        for i in range(HEAD):
                            gelu(n + 1, i)
                    loop_groups(e, body)

                @block.tensor
                def _(e):
                    e.wait_ge(on["tables_loaded"].sem, on["tables_loaded"].at(16 * 5))
                    e.wait_ge(on["ones_set"].sem, on["ones_set"].at(2))

                    def hidden(n, p, i):
                        half, x = divmod(i, E)
                        e.wait_ge(on["expert_gelu"].sem, on["expert_gelu"].at(2 * E * n + i + 1))
                        e.matmul(bank[3 + i % 2][:, 0:HALF], ew1[:, x], xn[:, p, 4 * half:4 * half + 4].rearrange("c w t -> c (w t)"),
                                 start=True, stop=True).then_inc(on["expert_hidden"].sem, 1)

                    def outputs(n, k):
                        half, j = divmod(k, E // 2)
                        e.wait_ge(on["expert_gelu"].sem, on["expert_gelu"].at(2 * E * n + 2 * k + 4))
                        e.wait_ge(on["outputs_evacuated"].sem, on["outputs_evacuated"].at(E * n + k))
                        for i in range(2):
                            last = e.matmul(bank[5][C * i:C * (i + 1), 0:HALF], ew2[:, 2 * j + i], hid[:, half, 2 * j + i],
                                            start=True, stop=True)
                        last.then_inc(on["outputs_ready"].sem, 1)

                    def by_token(n, x):
                        e.wait_ge(on["outputs_evacuated"].sem, on["outputs_evacuated"].at(E * n + (4 if x < 4 else 8)))
                        e.wait_ge(on["expert_weighted"].sem, on["expert_weighted"].at(GW * n + x + 1))
                        for j in range(E // 2):
                            last = e.transpose(bank[6 + x % 2][0:TP, 128 * j:128 * (j + 1)],
                                               ysb[:, x // 4, j, TP * (x % 4):TP * (x % 4 + 1)], ident[:])
                        last.then_inc(on["experts_done"].sem, 1)

                    def logits(n, p):
                        e.wait_ge(on["lead_ready"].sem, on["lead_ready"].at(n))
                        for x in range(GW):
                            last = e.matmul(bank[2][0:TP, E * x:E * (x + 1)], xn[:, p, x], wr[:], start=True, stop=True)
                        last.then_inc(on["gate_scored"].sem, 1)

                    transpose_group(e, 0, 0)
                    e.wait_ge(on["evacuated"].sem, on["evacuated"].at(2))
                    logits(0, 0)
                    for i in range(HEAD):
                        hidden(0, 0, i)

                    def body(n, p, w, p1, w1):
                        for i in range(HEAD, 2 * E):
                            hidden(n, p, i)
                            if i == HEAD:
                                outputs(n, 0)
                            if i % 2:
                                outputs(n, (i - 3) // 2)
                            if i >= 12:
                                by_token(n, i - 12)
                            if i == NEXT_AT:
                                transpose_group(e, p1, n + 1)
                        e.wait_ge(on["evacuated"].sem, on["evacuated"].at(2 * n + 4))
                        hidden(n + 1, p1, 0)
                        outputs(n, E - 1)
                        hidden(n + 1, p1, 1)
                        by_token(n, 4)
                        hidden(n + 1, p1, 2)
                        by_token(n, 5)
                        logits(n + 1, p1)
                        by_token(n, 6)
                        hidden(n + 1, p1, 3)
                        by_token(n, 7)
                    loop_groups(e, body)
            G = 2 * GROUPS
            norm_ended(G + 1, G + 1)
            ended(tables_loaded=16 * 5, ones_set=2, transposed=2 * G + 2, evacuated=2 * G + 2)

        with nc.Block() as block:
            @block.sync
            def _(e):
                for p in range(PAIRS):
                    for b in range(2):
                        e.dma_start(out[2 * p + b].rearrange("(h w) c -> h w c", w=HW),
                                         xr[HW * b:HW * (b + 1), p * HW:(p + 1) * HW, :]).then_inc(on["stored"].sem, 16)
                e.wait_ge(on["stored"].sem, on["stored"].at(16 * B))


def layouts(i):
    import numpy as np
    t = {k: np.asarray(v) for k, v in i.items()}
    T = lambda k: t["L0_tok_" + k]
    A = lambda k: t["L0_attn_" + k]
    FF = lambda k: t["L0_ffn_" + k]
    f = np.float32
    vec = {"ag": A("ln1_g"), "ab": A("ln1_b"),
           "fg": FF("gamma"), "fb": FF("beta"),
           "scale": np.broadcast_to(A("scale").reshape(1), (128,)),
           "last": np.broadcast_to(A("bias_table")[-1:], (128,))}
    for l in range(BLOCKS):
        vec |= {f"n1g{l}": T("n1g")[l], f"n1b{l}": T("n1b")[l], f"n2g{l}": T("n2g")[l], f"n2b{l}": T("n2b")[l],
                f"qb{l}": T("qkv_b")[l, 0:C], f"kb{l}": T("qkv_b")[l, C:2 * C]}
        vec[f"b2{l}"] = np.concatenate([T("b2")[l]] * 2, 0)
        for q in range(2):
            vec[f"mb{l}{q}"] = T("b1")[l, 128 * q:128 * (q + 1)]
    for q in range(E):
        vec[f"eb{q}"] = FF("b1")[q]
    cols = np.zeros((128, len(COLS)), f)
    for n, k in enumerate(COLS):
        cols[:len(vec[k]), n] = vec[k]
    rows = np.stack([T("pe_b"), T("pe_ng"), T("pe_nb"), A("proj_b"), A("ln2_g"), A("ln2_b")])
    pew = np.zeros((GW, 16, GW, C), f)
    for w in range(GW):
        pew[w, :, w, :] = T("pe_w").reshape(C, 16).T
    wv = np.concatenate([T("qkv_w")[:, 2 * C:].transpose(2, 0, 1), T("qkv_b")[:, 2 * C:][None]], 0)
    pw = np.zeros((HP, 32, BLOCKS, C), f)
    pw[:, 0:16] = T("proj_w").transpose(2, 0, 1).reshape(HP, 16, BLOCKS, C)
    pw[0, 16] = T("proj_b")
    c, r = np.divmod(np.arange(WN), WS)
    rel = (r[:, None] - r[None, :] + WS - 1) * (2 * WS - 1) + c[:, None] - c[None, :] + WS - 1
    edge = lambda x: (x >= WS - SHIFT).astype(int)
    masks = np.stack([np.where(g[:, None] != g[None, :], f(-100), f(0))
                      for g in (edge(r), edge(c), 2 * edge(r) + edge(c))], 1)
    heads = np.zeros((C, NH), f)
    for h in range(NH):
        heads[HD * h:HD * (h + 1), h] = 1
    table = A("bias_table")
    ext = table[TAB - 1 - np.clip(np.arange(2352 + TP) - 1440, 0, TAB - 1)]
    extq = table[np.clip(np.arange(2576 + TP), 0, TAB - 1)]
    x = {"cols": cols, "rows": rows, "ident": np.eye(128, dtype=f), "pew": pew.reshape(128, GW * C),
         "wqk": T("qkv_w")[:, 0:2 * C].transpose(2, 0, 1), "wv": wv, "pw": pw.reshape(128, BLOCKS, C),
         "w1": np.concatenate([T("w1").transpose(2, 0, 1), np.zeros((AK - C, BLOCKS, 2 * HID), f)], 0), "w2": T("w2").transpose(2, 0, 1).reshape(2, 128, BLOCKS, C).transpose(1, 2, 0, 3),
         "awq": A("qkv_w")[:, 0:C], "awk": A("qkv_w")[:, C:2 * C],
         "awv": np.concatenate([A("qkv_w")[:, 2 * C:], A("qkv_b")[2 * C:][None]], 0), "awp": np.concatenate([A("proj_w")] * 2, 0),
         "rpb": T("rpb")[:, rel].transpose(1, 0, 3, 2), "masks": masks, "heads": heads,
         "wr": np.concatenate([FF("Wr"), FF("br")[None], np.zeros((AK - C - 1, E), f)], 0),
         "ew1": np.concatenate([FF("W1").transpose(1, 0, 2), np.zeros((AK - C, E, HID), f)], 0),
         "ew2": FF("W2").transpose(1, 0, 2), "eb2": FF("b2").reshape(E // 2, 128).T,
         "ext": ext, "flip": np.eye(TP, dtype=f)[::-1], "bias2": np.stack([A("qkv_b")[C:2 * C], A("qkv_b")[0:C]], 1), "extq": extq, "number": np.arange(E, dtype=f)}
    return x


def kernel(**inputs):
    import numpy as np
    import concourse.bacc as bacc
    from concourse.bass_utils import run_bass_kernel_spmd as run

    nc = bacc.Bacc("TRN2", target_bir_lowering=False, num_devices=1)
    arrays = {f"in_{k}": np.ascontiguousarray(v) for k, v in layouts(inputs).items()}
    arrays["in_x"] = np.ascontiguousarray(inputs["x"])
    dram = {k: nc.dram_tensor(k, v.shape, mybir.dt.from_np(v.dtype), kind="ExternalInput").ap() for k, v in arrays.items()}
    out = nc.dram_tensor("out", (B, N, C), F32, kind="ExternalOutput").ap()
    build(nc, dram["in_x"], out, {k[3:]: v for k, v in dram.items()})
    return run(nc, [arrays], core_ids=[0]).results[0]["out"]
```
